# Optimizing a Trainium2 kernel written in Bass

```python
import numpy as np
import jax
import jax.numpy as jnp

def _softmax(x, axis=-1):
    return jax.nn.softmax(x, axis=axis)

def _gelu(x):
    return jax.nn.gelu(x, approximate=True)

def _silu(x):
    return jax.nn.silu(x)

def _sigmoid(x):
    return jax.nn.sigmoid(x)

def _layernorm(x, axis=-1, eps=1e-05):
    m = jnp.mean(x, axis=axis, keepdims=True)
    v = jnp.var(x, axis=axis, keepdims=True)
    return (x - m) / jnp.sqrt(v + eps)

def _scatter_add(tgt, idx, src, axis=0):
    return tgt.at[idx].add(src)

def _segment_sum(src, seg, n):
    return jax.ops.segment_sum(src, seg, n)
kernel_name = 'mk_gnn_preln_d4_gnn_r64_9f0d3f'

def setup_inputs(seed: int=0):
    np.random.seed(seed)
    _w = jnp.asarray

    def _rec_inputs():
        import jax
        import jax.numpy as jnp
        _gk = jax.random.key(seed)
        x = -0.0003713 + 1 * jax.random.normal(jax.random.fold_in(_gk, 1), (50000, 128), jnp.float32)
        src = jax.random.randint(jax.random.fold_in(_gk, 2), (25000,), 0, 50000, jnp.int32)
        dst = jnp.minimum((50000 * jax.random.uniform(jax.random.fold_in(_gk, 3), (25000,)) ** 2.0).astype(jnp.int32), 49999)
        _o = jnp.argsort(dst, stable=True)
        src = src[_o]
        dst = dst[_o]
        edge_attr_16 = 0.000312547 + 1.00004 * jax.random.normal(jax.random.fold_in(_gk, 12), (25000, 16), jnp.float32)
        return (x, src, dst, edge_attr_16)
    x, src, dst, edge_attr_16 = _rec_inputs()

    def _L0_gnn_setup():
        import jax, jax.numpy as jnp
        import numpy as np
        import math
        N = 100000
        E = 15625
        D = 128
        ED = 16
        L = 5
        MID = 3
        ALPHA = 0.2
        THETA = 0.2
        NEG_SLOPE_ATT = 0.2

        def _gat_layer(x, src, dst, ea, W, We, a_src, a_dst, a_edge, b, n):
            h = x @ W
            e = ea @ We
            s = (h @ a_src)[src] + (h @ a_dst)[dst] + e @ a_edge
            s = jax.nn.leaky_relu(s, NEG_SLOPE_ATT)
            smax = jax.ops.segment_max(s, dst, num_segments=n)
            ex = jnp.exp(s - jax.lax.stop_gradient(smax)[dst])
            denom = jax.ops.segment_sum(ex, dst, num_segments=n)
            alpha = ex / denom[dst]
            out = jax.ops.segment_sum(h[src] * alpha[:, None], dst, num_segments=n)
            return out + b

        def _forward(x, edge_index, edge_attr, Ws, Wes, a_srcs, a_dsts, a_edges, biases, mid_ws):
            n = x.shape[0]
            src0, dst0 = (edge_index[0], edge_index[1])
            deg = jax.ops.segment_sum(jnp.ones_like(dst0, dtype=x.dtype), dst0, num_segments=n)
            loop_attr = jax.ops.segment_sum(edge_attr, dst0, num_segments=n) / jnp.clip(deg, 1.0)[:, None]
            loops = jnp.arange(n, dtype=src0.dtype)
            src = jnp.concatenate([src0, loops])
            dst = jnp.concatenate([dst0, loops])
            ea = jnp.concatenate([edge_attr, loop_attr], axis=0)
            x0 = _gat_layer(x, src, dst, ea, Ws[0], Wes[0], a_srcs[0], a_dsts[0], a_edges[0], biases[0], n)
            h = x0
            for i in range(MID):
                c = _gat_layer(h, src, dst, ea, Ws[i + 1], Wes[i + 1], a_srcs[i + 1], a_dsts[i + 1], a_edges[i + 1], biases[i + 1], n)
                beta = math.log(THETA / (i + 1) + 1.0)
                h = (1.0 - ALPHA) * c + ALPHA * x0
                h = (1.0 - beta) * h + beta * (h @ mid_ws[i])
                h = jax.nn.leaky_relu(h, 0.01)
            return _gat_layer(h, src, dst, ea, Ws[L - 1], Wes[L - 1], a_srcs[L - 1], a_dsts[L - 1], a_edges[L - 1], biases[L - 1], n)
        key = jax.random.key(seed)
        ks = jax.random.split(key, 10)
        s = 1.0 / np.sqrt(D)
        se = 1.0 / np.sqrt(ED)
        return {'x': jax.random.normal(ks[0], (N, D), jnp.float32), 'edge_index': jax.random.randint(ks[1], (2, E), 0, N, dtype=jnp.int64), 'edge_attr': jax.random.normal(ks[2], (E, ED), jnp.float32), 'Ws': jax.random.normal(ks[3], (L, D, D), jnp.float32) * s, 'Wes': jax.random.normal(ks[4], (L, ED, D), jnp.float32) * se, 'a_srcs': jax.random.normal(ks[5], (L, D), jnp.float32) * s, 'a_dsts': jax.random.normal(ks[6], (L, D), jnp.float32) * s, 'a_edges': jax.random.normal(ks[7], (L, D), jnp.float32) * s, 'biases': jnp.zeros((L, D), jnp.float32), 'mid_ws': jax.random.normal(ks[8], (MID, D, D), jnp.float32) * s}
    _L0_gnn_all = _L0_gnn_setup()
    _L0_gnn_in = {k: v for k, v in _L0_gnn_all.items() if k in ('Ws', 'Wes', 'a_srcs', 'a_dsts', 'a_edges', 'biases', 'mid_ws')}
    del _L0_gnn_all

    def _L1_gnn_setup():
        import jax, jax.numpy as jnp
        import numpy as np
        N, E, F_IN, H, C = (50000, 12500, 128, 4, 32)
        NEG_SLOPE = 0.2
        key = jax.random.key(seed)
        k1, k2, k3, k4, k5, k6, k7 = jax.random.split(key, 7)
        nodes = jax.random.normal(k1, (N, F_IN), dtype=jnp.float32)
        senders = jax.random.randint(k2, (E,), 0, N, dtype=jnp.int32)
        receivers = jax.random.randint(k3, (E,), 0, N, dtype=jnp.int32)
        W = jax.random.normal(k4, (F_IN, H * C), dtype=jnp.float32) / np.sqrt(F_IN)
        b_lin = jnp.zeros((H * C,), dtype=jnp.float32)
        alpha = jax.random.normal(k5, (1, H, 2 * C), dtype=jnp.float32)
        bias = jnp.zeros((H * C,), dtype=jnp.float32)
        return {'nodes': nodes, 'senders': senders, 'receivers': receivers, 'W': W, 'b_lin': b_lin, 'alpha': alpha, 'bias': bias}
    _L1_gnn_all = _L1_gnn_setup()
    _L1_gnn_in = {k: v for k, v in _L1_gnn_all.items() if k in ('W', 'b_lin', 'alpha', 'bias')}
    del _L1_gnn_all

    def _L2_gnn_setup():
        import jax, jax.numpy as jnp
        import numpy as np
        N_NODES = 50000
        N_EDGES = 12500
        D = 128
        key = jax.random.key(seed)
        k1, k2, k3, k4, k5, k6 = jax.random.split(key, 6)
        node_feats = jax.random.normal(k1, (N_NODES, D), dtype=jnp.float32)
        edge_index = jax.random.randint(k2, (2, N_EDGES), 0, N_NODES, dtype=jnp.int64)
        nbr_w = jax.random.normal(k3, (D, D), dtype=jnp.float32)
        self_w = jax.random.normal(k4, (D, D), dtype=jnp.float32)
        b = jax.random.normal(k5, (D,), dtype=jnp.float32)
        return {'node_feats': node_feats, 'edge_index': edge_index, 'nbr_w': nbr_w, 'self_w': self_w, 'b': b}
    _L2_gnn_all = _L2_gnn_setup()
    _L2_gnn_in = {k: v for k, v in _L2_gnn_all.items() if k in ('nbr_w', 'self_w', 'b')}
    del _L2_gnn_all

    def _L3_gnn_setup():
        import jax, jax.numpy as jnp
        import numpy as np
        N_NODES = 50000
        N_EDGES = 12500
        D_IN, D_HID, D_OUT = (128, 256, 128)
        key = jax.random.key(seed)
        ks = jax.random.split(key, 12)
        inp = {'x': jax.random.normal(ks[0], (N_NODES, D_IN), dtype=jnp.float32), 'edge_src': jax.random.randint(ks[1], (N_EDGES,), 0, N_NODES, dtype=jnp.int32), 'edge_dst': jax.random.randint(ks[2], (N_EDGES,), 0, N_NODES, dtype=jnp.int32)}

        def lin(k, fi, fo):
            return jax.random.normal(k, (fi, fo), dtype=jnp.float32) * (1.0 / np.sqrt(fi))
        inp['Ws0'] = lin(ks[3], D_IN, D_HID)
        inp['Wn0'] = lin(ks[4], D_IN, D_HID)
        inp['b0'] = jnp.zeros((D_HID,), jnp.float32)
        inp['Ws1'] = lin(ks[5], D_HID, D_HID)
        inp['Wn1'] = lin(ks[6], D_HID, D_HID)
        inp['b1'] = jnp.zeros((D_HID,), jnp.float32)
        inp['Ws2'] = lin(ks[7], D_HID, D_OUT)
        inp['Wn2'] = lin(ks[8], D_HID, D_OUT)
        inp['b2'] = jnp.zeros((D_OUT,), jnp.float32)
        return inp
    _L3_gnn_all = _L3_gnn_setup()
    _L3_gnn_in = {k: v for k, v in _L3_gnn_all.items() if k in ('Ws0', 'Wn0', 'b0', 'Ws1', 'Wn1', 'b1', 'Ws2', 'Wn2', 'b2')}
    del _L3_gnn_all
    return {'x': x, 'src': src, 'dst': dst, 'edge_attr_16': edge_attr_16, 'L0_gnn_Ws': _L0_gnn_in['Ws'], 'L0_gnn_Wes': _L0_gnn_in['Wes'], 'L0_gnn_a_srcs': _L0_gnn_in['a_srcs'], 'L0_gnn_a_dsts': _L0_gnn_in['a_dsts'], 'L0_gnn_a_edges': _L0_gnn_in['a_edges'], 'L0_gnn_biases': _L0_gnn_in['biases'], 'L0_gnn_mid_ws': _L0_gnn_in['mid_ws'], 'L1_gnn_W': _L1_gnn_in['W'], 'L1_gnn_b_lin': _L1_gnn_in['b_lin'], 'L1_gnn_alpha': _L1_gnn_in['alpha'], 'L1_gnn_bias': _L1_gnn_in['bias'], 'L2_gnn_nbr_w': _L2_gnn_in['nbr_w'], 'L2_gnn_self_w': _L2_gnn_in['self_w'], 'L2_gnn_b': _L2_gnn_in['b'], 'L3_gnn_Ws0': _L3_gnn_in['Ws0'], 'L3_gnn_Wn0': _L3_gnn_in['Wn0'], 'L3_gnn_b0': _L3_gnn_in['b0'], 'L3_gnn_Ws1': _L3_gnn_in['Ws1'], 'L3_gnn_Wn1': _L3_gnn_in['Wn1'], 'L3_gnn_b1': _L3_gnn_in['b1'], 'L3_gnn_Ws2': _L3_gnn_in['Ws2'], 'L3_gnn_Wn2': _L3_gnn_in['Wn2'], 'L3_gnn_b2': _L3_gnn_in['b2']}

def reference(x, src, dst, edge_attr_16, L0_gnn_Ws, L0_gnn_Wes, L0_gnn_a_srcs, L0_gnn_a_dsts, L0_gnn_a_edges, L0_gnn_biases, L0_gnn_mid_ws, L1_gnn_W, L1_gnn_b_lin, L1_gnn_alpha, L1_gnn_bias, L2_gnn_nbr_w, L2_gnn_self_w, L2_gnn_b, L3_gnn_Ws0, L3_gnn_Wn0, L3_gnn_b0, L3_gnn_Ws1, L3_gnn_Wn1, L3_gnn_b1, L3_gnn_Ws2, L3_gnn_Wn2, L3_gnn_b2):
    import jax
    import jax.numpy as jnp

    def _L0_gnn_ref(x, edge_index, edge_attr, Ws, Wes, a_srcs, a_dsts, a_edges, biases, mid_ws):
        import jax, jax.numpy as jnp
        import numpy as np
        import math
        N = 100000
        E = 15625
        D = 128
        ED = 16
        L = 5
        MID = 3
        ALPHA = 0.2
        THETA = 0.2
        NEG_SLOPE_ATT = 0.2

        def _gat_layer(x, src, dst, ea, W, We, a_src, a_dst, a_edge, b, n):
            h = x @ W
            e = ea @ We
            s = (h @ a_src)[src] + (h @ a_dst)[dst] + e @ a_edge
            s = jax.nn.leaky_relu(s, NEG_SLOPE_ATT)
            smax = jax.ops.segment_max(s, dst, num_segments=n)
            ex = jnp.exp(s - jax.lax.stop_gradient(smax)[dst])
            denom = jax.ops.segment_sum(ex, dst, num_segments=n)
            alpha = ex / denom[dst]
            out = jax.ops.segment_sum(h[src] * alpha[:, None], dst, num_segments=n)
            return out + b

        def _forward(x, edge_index, edge_attr, Ws, Wes, a_srcs, a_dsts, a_edges, biases, mid_ws):
            n = x.shape[0]
            src0, dst0 = (edge_index[0], edge_index[1])
            deg = jax.ops.segment_sum(jnp.ones_like(dst0, dtype=x.dtype), dst0, num_segments=n)
            loop_attr = jax.ops.segment_sum(edge_attr, dst0, num_segments=n) / jnp.clip(deg, 1.0)[:, None]
            loops = jnp.arange(n, dtype=src0.dtype)
            src = jnp.concatenate([src0, loops])
            dst = jnp.concatenate([dst0, loops])
            ea = jnp.concatenate([edge_attr, loop_attr], axis=0)
            x0 = _gat_layer(x, src, dst, ea, Ws[0], Wes[0], a_srcs[0], a_dsts[0], a_edges[0], biases[0], n)
            h = x0
            for i in range(MID):
                c = _gat_layer(h, src, dst, ea, Ws[i + 1], Wes[i + 1], a_srcs[i + 1], a_dsts[i + 1], a_edges[i + 1], biases[i + 1], n)
                beta = math.log(THETA / (i + 1) + 1.0)
                h = (1.0 - ALPHA) * c + ALPHA * x0
                h = (1.0 - beta) * h + beta * (h @ mid_ws[i])
                h = jax.nn.leaky_relu(h, 0.01)
            return _gat_layer(h, src, dst, ea, Ws[L - 1], Wes[L - 1], a_srcs[L - 1], a_dsts[L - 1], a_edges[L - 1], biases[L - 1], n)
        return _forward(x, edge_index, edge_attr, Ws, Wes, a_srcs, a_dsts, a_edges, biases, mid_ws)

    def _L1_gnn_ref(nodes, senders, receivers, W, b_lin, alpha, bias):
        import jax, jax.numpy as jnp
        import numpy as np
        N, E, F_IN, H, C = (50000, 12500, 128, 4, 32)
        NEG_SLOPE = 0.2
        n = nodes.shape[0]
        x = nodes @ W + b_lin
        loop = jnp.arange(n, dtype=senders.dtype)
        snd = jnp.concatenate([senders, loop])
        rcv = jnp.concatenate([receivers, loop])
        sent = x[snd]
        recvd = x[rcv]
        feat = jnp.concatenate([sent, recvd], axis=1).reshape(-1, H, 2 * C)
        logits = jnp.sum(feat * alpha, axis=-1)
        logits = jax.nn.leaky_relu(logits, negative_slope=NEG_SLOPE)
        seg_max = jax.ops.segment_max(logits, rcv, num_segments=n)
        e = jnp.exp(logits - seg_max[rcv])
        denom = jax.ops.segment_sum(e, rcv, num_segments=n)
        att = e / denom[rcv]
        msgs = att[:, :, None] * sent.reshape(-1, H, C)
        out = jax.ops.segment_sum(msgs, rcv, num_segments=n)
        out = out.reshape(-1, H * C)
        out = out + bias
        return out

    def _L2_gnn_ref(node_feats, edge_index, nbr_w, self_w, b):
        import jax, jax.numpy as jnp
        import numpy as np
        N_NODES = 50000
        N_EDGES = 12500
        D = 128
        src = edge_index[0]
        dst = edge_index[1]
        nbr_features = node_feats[dst]
        nbr_sum = jax.ops.segment_sum(nbr_features, src, num_segments=node_feats.shape[0])
        nbr_msg = jnp.tanh(nbr_sum @ nbr_w + b)
        self_msg = node_feats @ self_w
        return self_msg + nbr_msg

    def _L3_gnn_ref(x, edge_src, edge_dst, Ws0, Wn0, b0, Ws1, Wn1, b1, Ws2, Wn2, b2):
        import jax, jax.numpy as jnp
        import numpy as np
        N_NODES = 50000
        N_EDGES = 12500
        D_IN, D_HID, D_OUT = (128, 256, 128)
        n = x.shape[0]
        deg = jax.ops.segment_sum(jnp.ones(edge_dst.shape, x.dtype), edge_dst, num_segments=n)
        inv_deg = jnp.where(deg > 0, 1.0 / jnp.maximum(deg, 1.0), 0.0)[:, None]

        def sage_conv(h, Ws, Wn, b):
            agg = jax.ops.segment_sum(h[edge_src], edge_dst, num_segments=n)
            h_neigh = agg * inv_deg
            return h @ Ws + h_neigh @ Wn + b
        h = jax.nn.relu(sage_conv(x, Ws0, Wn0, b0))
        h = jax.nn.relu(sage_conv(h, Ws1, Wn1, b1))
        h = jax.nn.relu(sage_conv(h, Ws2, Wn2, b2))
        return h
    edge_index = jnp.stack([src, dst])
    h = jnp.maximum(_layernorm(x, axis=-1), 0.0)
    x = x + _L0_gnn_ref(h, edge_index, edge_attr_16, L0_gnn_Ws, L0_gnn_Wes, L0_gnn_a_srcs, L0_gnn_a_dsts, L0_gnn_a_edges, L0_gnn_biases, L0_gnn_mid_ws)
    h = jnp.maximum(_layernorm(x, axis=-1), 0.0)
    x = x + _L1_gnn_ref(h, src, dst, L1_gnn_W, L1_gnn_b_lin, L1_gnn_alpha, L1_gnn_bias)
    h = jnp.maximum(_layernorm(x, axis=-1), 0.0)
    x = x + _L2_gnn_ref(h, edge_index, L2_gnn_nbr_w, L2_gnn_self_w, L2_gnn_b)
    h = jnp.maximum(_layernorm(x, axis=-1), 0.0)
    x = x + _L3_gnn_ref(h, src, dst, L3_gnn_Ws0, L3_gnn_Wn0, L3_gnn_b0, L3_gnn_Ws1, L3_gnn_Wn1, L3_gnn_b1, L3_gnn_Ws2, L3_gnn_Wn2, L3_gnn_b2)
    return x

_drawn_inputs = setup_inputs


def setup_inputs(seed=0):
    import zlib

    import numpy as np

    out = dict(_drawn_inputs(seed))
    spreads = {'L0_gnn_biases': (0.0, 0.1),
     'L1_gnn_b_lin': (0.0, 0.1),
     'L1_gnn_bias': (0.0, 0.1),
     'L3_gnn_b0': (0.0, 0.8),
     'L3_gnn_b1': (0.0, 0.8),
     'L3_gnn_b2': (0.0, 0.8)}
    factors = {'edge_attr_16': 20.95,
     'L0_gnn_Wes': 60.585,
     'L0_gnn_a_srcs': 87.9,
     'L0_gnn_a_dsts': 200.0,
     'L0_gnn_a_edges': 21.777,
     'L0_gnn_mid_ws': 2.786,
     'L3_gnn_Wn0': 3.44,
     'L3_gnn_Wn1': 3.302,
     'L3_gnn_Wn2': 2.953}
    for name, (base, spread) in spreads.items():
        noise = np.random.default_rng([zlib.crc32(name.encode()), seed]).standard_normal(out[name].shape)
        drawn = base * np.exp(spread * noise) if base else spread * noise
        out[name] = jnp.asarray(drawn.astype(out[name].dtype))
    for name, factor in factors.items():
        out[name] = (out[name] * factor).astype(out[name].dtype)
    return out
```

```python
import math
from contextlib import ExitStack

import concourse.bass as bass
from concourse import mybir

F32 = mybir.dt.float32
I32 = mybir.dt.int32
U8 = mybir.dt.uint8
ACT = mybir.ActivationFunctionType
ALU = mybir.AluOpType
AX = mybir.AxisListType.X

P = 128
D = 128
MAC = 512
K4 = MAC // P
BIG = 1.0e30
SKIP = 1.0e6
EPS = 1e-5
ALPHA, THETA = 0.2, 0.2


class Signals:

    SOFT = ("slot", "put", "x_in", "ns_zero", "soft")
    kept = []

    def __init__(self, nc, tag):
        self.nc, self.tag, self.stack, self.named, self.taken = nc, tag, ExitStack(), {}, 0

    def __call__(self, name):
        if name not in self.named:
            if name.startswith(self.SOFT):
                self.named[name] = self.kept[self.taken]
                self.taken += 1
            else:
                self.named[name] = self.stack.enter_context(self.nc.semaphore(f"{self.tag}_{name}"))
        return self.named[name]

    def end(self):
        if self.taken:
            first = min(s.num for s in self.kept)
            self.nc.gpsimd.dma_reset(range(first, first + len(self.kept)))
        for s in self.named.values():
            self.nc.gpsimd.sem_clear(s)
        self.nc.all_engine_barrier()
        self.stack.close()


def node_rows(t, g, n):
    if isinstance(g, int):
        r = min(g * MAC, n - MAC)
        return t[r:r + MAC, :].rearrange("(p k) f -> p k f", k=K4)
    v = t[0:n // MAC * MAC, :].rearrange("(g p k) f -> g p k f", p=P, k=K4)
    return v[bass.ds(g, 1)].rearrange("a p k f -> p (a k) f")


def edge_rows(t, m):
    v = t.rearrange("(m k p) f -> m p k f", p=P, k=K4)
    return v[m] if isinstance(m, int) else v[bass.ds(m, 1)].rearrange("a p k f -> p (a k) f")


def chunk(t, m, w):
    return t[:, m * w:(m + 1) * w] if isinstance(m, int) else t[:, bass.ds(m * w, w)]


class Dims:
    def __init__(self, n, e):
        self.N, self.E = n, e
        self.NM = -(-n // MAC)
        self.NM += self.NM % 2
        self.NP = self.NM * MAC
        self.EM = -(-e // MAC)
        self.ET, self.EP, self.QP = 4 * self.EM, MAC * self.EM, 2 * self.EM
        self.U = 7 if self.EM % 7 == 0 else 1
        assert n >= (self.NM - 1) * MAC and self.QP <= P


def pairs(nc_eng, count, body):
    if count // 2 > 0:
        with nc_eng.Fori(0, count // 2) as i:
            body(i * 2, (0, 1))
    if count % 2:
        body(count - 1, (0,))


def prepare_edges(nc, c, src, dst, ea):
    d, S = c.d, Signals(nc, "edges")
    QP, ET, E, NP = d.QP, d.ET, d.E, d.NP
    qf, rem = E // 256, E % 256
    n1 = (E - 1) // 256
    with ExitStack() as st:
        def sb(name, shape, dt=F32):
            return st.enter_context(nc.sbuf_tensor(f"{S.tag}_{name}", shape, dt))
        di, si = sb("di", [P, 256], I32), sb("si", [P, 256], I32)
        nfi, pli = sb("nfi", [P, 1], I32), sb("pli", [P, 1], I32)
        nf, pl = sb("nf", [P, 1]), sb("pl", [P, 1])
        dR, sR = sb("dR", [P, 256]), sb("sR", [P, 256])
        t1, t2, t3, t4, nl = (sb(x, [P, 256]) for x in ("t1", "t2", "t3", "t4", "nl"))
        wf = sb("wf", [P, 4])
        wb = sb("wb", [P, 4])
        posi = sb("posi", [P, NP // P], I32)
        ps = st.enter_context(nc.psum_tensor("pe_ps", [P, 8, 128], F32))
        block = st.enter_context(nc.Block())

        @block.gpsimd
        def _(pool):
            pool.memset(di[:], -1).then_inc(S("cleared"), 1)
            pool.memset(si[:], -1).then_inc(S("cleared"), 1)
            pool.memset(nfi[:], -2).then_inc(S("cleared"), 1)
            pool.memset(pli[:], -3).then_inc(S("cleared"), 1)
            pool.memset(c.ident[:], 0.0).then_inc(S("zeroed"), 1)
            pool.memset(c.upper[:], 0.0).then_inc(S("zeroed"), 1)
            pool.wait_ge(S("zeroed"), 2)
            pool.affine_select(out=c.ident[:], in_=c.ident[:], compare_op=ALU.not_equal, fill=1.0, base=0,
                               pattern=[[-1, P]], channel_multiplier=1).then_inc(S("ident"), 1)
            pool.affine_select(out=c.upper[:], in_=c.upper[:], compare_op=ALU.is_ge, fill=1.0, base=0,
                               pattern=[[-1, P]], channel_multiplier=1).then_inc(S("upper"), 1)
            pool.iota(posi[:], pattern=[[1, NP // P]], base=0, channel_multiplier=NP // P).then_inc(S("pos"), 1)
            pool.iota(c.slotI[:], pattern=[[P, ET]], base=d.N, channel_multiplier=1).then_inc(S("slots"), 1)

        @block.sync
        def _(sp):
            sp.wait_ge(S("cleared"), 4)
            for n, (t, a) in enumerate(((di, dst), (si, src))):
                sp.dma_start(t[0:qf, :], a[0:qf * 256].rearrange("(q j) -> q j", j=256)).then_inc(S("idx_full"), 16)
                if rem:
                    sp.dma_start(t[qf:qf + 1, 0:rem], a[qf * 256:E].rearrange("(q j) -> q j", q=1)).then_inc(S("idx_rem"), 16)
            sp.dma_start(nfi[0:n1, :], dst[256:256 * n1 + 1:256].rearrange("(q j) -> q j", j=1), allow_slow_non_contiguous=True).then_inc(S("nf_in"), 16)
            n2 = E // 256
            sp.dma_start(pli[1:min(n2, QP - 1) + 1, :],
                         dst[255:255 + 256 * (min(n2, QP - 1) - 1) + 1:256].rearrange("(q j) -> q j", j=1),
                         allow_slow_non_contiguous=True).then_inc(S("pl_in"), 16)
            sp.wait_ge(S("pos"), 1)
            sp.dma_start(c.POS.rearrange("(p c) a -> p (c a)", p=P), posi[:]).then_inc(S("pos_out"), 16)
            sp.wait_ge(S("rows"), 1)
            sp.dma_start(c.dstRow.rearrange("(q j) -> q j", j=256), dR[0:QP, :]).then_inc(S("row_out"), 16)
            sp.dma_start(c.srcRow.rearrange("(q j) -> q j", j=256), sR[0:QP, :]).then_inc(S("row_out"), 16)
            sp.wait_ge(S("pos_out"), 16)
            sp.wait_ge(S("row_out"), 32)

        @block.vector
        def _(v):
            v.wait_ge(S("idx_full"), 32)
            if rem:
                v.wait_ge(S("idx_rem"), 32)
            v.wait_ge(S("nf_in"), 16)
            v.wait_ge(S("pl_in"), 16)
            v.tensor_copy(sR[:], si[:]).then_inc(S("c0"), 1)
            v.tensor_copy(nf[:], nfi[:]).then_inc(S("c1"), 1)
            v.tensor_copy(pl[:], pli[:]).then_inc(S("c2"), 1)
            v.tensor_copy(dR[:], di[:]).then_inc(S("rows"), 1)
            v.wait_ge(S("rows"), 1)
            v.memset(c.contF[:, :, 0:1], 0.0)
            v.memset(c.contB[:, :, 255:256], 0.0)
            for h in range(4):
                v.tensor_tensor(c.contF[:, h, 1:256], dR[:, 1:256], dR[:, 0:255], ALU.is_equal)
                last = v.tensor_tensor(c.contB[:, h, 0:255], dR[:, 0:255], dR[:, 1:256], ALU.is_equal)
            last.then_inc(S("cont"), 1)
            v.tensor_scalar(c.runF[:], dR[:], pl[:], None, ALU.is_equal).then_inc(S("runF"), 1)
            v.tensor_scalar(c.runB[:], dR[:], nf[:], None, ALU.is_equal).then_inc(S("runB"), 1)
            v.wait_ge(S("cont"), 1)
            v.tensor_scalar(c.negF[:], c.contF[:], 1.0, BIG, ALU.subtract, ALU.mult).then_inc(S("m1"), 1)
            v.tensor_scalar(c.last[:, 0:255], c.contB[:, 0, 0:255], -1.0, 1.0, ALU.mult, ALU.add)
            v.tensor_scalar(c.last[:, 255:256], dR[:, 255:256], nf[:], None, ALU.not_equal).then_inc(S("last"), 1)
            v.wait_ge(S("runF"), 1)
            v.wait_ge(S("runB"), 1)
            v.tensor_scalar(c.negRunF[:], c.runF[:], 1.0, BIG, ALU.subtract, ALU.mult).then_inc(S("m2"), 1)
            for h in range(4):
                v.tensor_copy(wf[:, h:h + 1], c.runF[:, 255:256])
                last = v.tensor_copy(wb[:, h:h + 1], c.runB[:, 0:1])
            last.then_inc(S("whole"), 1)
            v.wait_ge(S("last"), 1)
            v.tensor_scalar(c.negLast[:], c.last[:], 1.0, BIG, ALU.subtract, ALU.mult).then_inc(S("m3"), 1)
            v.tensor_scalar(nl[:], c.last[:], -SKIP, SKIP, ALU.mult, ALU.add).then_inc(S("nl"), 1)
            v.tensor_scalar(t1[:], dR[:], 0.0, SKIP, ALU.is_lt, ALU.mult).then_inc(S("t1"), 1)
            v.wait_ge(S("nl"), 1)
            v.tensor_tensor(t2[:], nl[:], dR[:], ALU.add).then_inc(S("t2"), 1)
            v.wait_ge(S("t1"), 1)
            v.wait_ge(S("t2"), 1)
            v.tensor_tensor(t3[:], t1[:], t2[:], ALU.add).then_inc(S("canon_rows"), 1)
            v.wait_ge(S("c0"), 1)
            v.wait_ge(S("columns"), 1)
            for j in range(2):
                v.tensor_copy(c.dstF[:, j::2], ps[:, j, 0:QP])
                v.tensor_copy(c.srcF[:, j::2], ps[:, 2 + j, 0:QP])
                last = v.tensor_copy(c.canonI[:, j::2], ps[:, 4 + j, 0:QP])
            last.then_inc(S("cols"), 1)
            v.wait_ge(S("cols"), 1)
            v.tensor_scalar(c.idxD[:], c.dstF[:], 0.0, None, ALU.max).then_inc(S("m4"), 1)
            v.tensor_scalar(c.idxS[:], c.srcF[:], 0.0, None, ALU.max).then_inc(S("m5"), 1)
            v.wait_ge(S("chains"), 1)
            v.tensor_copy(c.wholeF[:], ps[0:4, 6, 0:QP]).then_inc(S("wF"), 1)
            v.tensor_copy(c.wholeB[:], ps[0:4, 7, 0:QP]).then_inc(S("m6"), 1)
            v.wait_ge(S("wF"), 1)
            v.tensor_scalar(c.negWholeF[:], c.wholeF[:], 1.0, BIG, ALU.subtract, ALU.mult).then_inc(S("m7"), 1)

        @block.tensor
        def _(pe):
            pe.wait_ge(S("ident"), 1)
            pe.wait_ge(S("rows"), 1)
            pe.wait_ge(S("c0"), 1)
            pe.wait_ge(S("canon_rows"), 1)
            for n, r in enumerate((dR, sR, t3)):
                for j in range(2):
                    last = pe.transpose(ps[:, 2 * n + j, 0:QP], r[0:QP, j * P:(j + 1) * P], c.ident[0:QP, 0:QP])
            last.then_inc(S("columns"), 1)
            pe.wait_ge(S("whole"), 1)
            pe.wait_ge(S("cols"), 1)
            pe.transpose(ps[0:4, 6, 0:QP], wf[0:QP, :], c.ident[0:QP, 0:QP])
            pe.transpose(ps[0:4, 7, 0:QP], wb[0:QP, :], c.ident[0:QP, 0:QP]).then_inc(S("chains"), 1)
    S.end()


def prepare_tiles(nc, c):
    d, S = c.d, Signals(nc, "tiles")
    with ExitStack() as st:
        def sb(name, shape, dt=F32):
            return st.enter_context(nc.sbuf_tensor(f"{S.tag}_{name}", shape, dt))
        db = [sb(f"db{i}", [P, MAC]) for i in range(2)]
        sbc = [sb(f"sbc{i}", [P, MAC]) for i in range(2)]
        sf = [sb(f"sf{i}", [P, 2 * MAC], U8) for i in range(2)]
        tail = [sb(f"tail{i}", [P, 1]) for i in range(2)]
        junk, dup = [sb(f"junk{i}", [P, K4, P]) for i in range(2)], [sb(f"dup{i}", [P, K4]) for i in range(2)]
        spareI, spareF = sb("spareI", [P, 1], I32), sb("spareF", [P, 1])
        dupF, a1, a2 = sb("dupF", [P, d.ET]), sb("a1", [P, d.ET]), sb("a2", [P, d.ET])
        block = st.enter_context(nc.Block())

        def bcast(row, m):
            v = row.rearrange("(a e) -> a e", a=1)
            return chunk(v, m, MAC).broadcast_to([P, MAC])

        @block.sync
        def _(sp):
            def load(m, pars):
                for b in pars:
                    g = m + b
                    sp.wait_ge(S("bfree"), g + 1)
                    sp.sem_inc(S("sp_pass"), 1)
                    sp.dma_start(db[b][:], bcast(c.dstRow, g)).then_inc(S(f"d_in{b}"), 16)
                    sp.dma_start(sbc[b][:], bcast(c.srcRow, g)).then_inc(S(f"s_in{b}"), 16)
            pairs(sp, d.EM, load)

        @block.scalar
        def _(act):
            def store(m, pars):
                for b in pars:
                    g = m + b
                    act.wait_ge(S("sf_done"), g + 1)
                    act.dma_start(chunk(c.SF, g, 2 * MAC), sf[b][:]).then_inc(S(f"sf_out{b}"), 16)
                    act.wait_ge(S(f"sf_out{b}"), (g - b) * 8 + 16)
                    act.sem_inc(S("sf_free"), 1)
            pairs(act, d.EM, store)

        @block.vector
        def _(v):
            v.memset(tail[1][:], -3.0).then_inc(S("tail"), 1)
            v.sem_inc(S("bfree"), 2)
            v.sem_inc(S("sf_free"), 2)

            def tiles(m, pars):
                for b in pars:
                    g = m + b
                    v.wait_ge(S(f"d_in{b}"), (g - b) * 8 + 16)
                    v.wait_ge(S(f"s_in{b}"), (g - b) * 8 + 16)
                    v.wait_ge(S("sf_free"), g + 1)
                    v.wait_ge(S("tail"), g + 1)
                    for k in range(K4):
                        col = slice(k * P, (k + 1) * P)
                        v.tensor_scalar(sf[b][:, col], db[b][:, col], c.dstF[:, bass.ds(g * 4 + k, 1)], None, ALU.is_equal)
                        before = db[b][:, k * P - 1:k * P] if k else tail[1 - b][:]
                        last = v.tensor_scalar(sf[b][:, MAC + k * P:MAC + (k + 1) * P], db[b][:, col], before, None, ALU.is_equal)
                    last.then_inc(S("sf_done"), 1)
                    v.tensor_copy(tail[b][:], db[b][:, MAC - 1:MAC]).then_inc(S("tail"), 1)
                    for k in range(K4):
                        last = v.scalar_tensor_tensor(out=junk[b][:, k, :], in0=sbc[b][:, k * P:(k + 1) * P],
                                                      scalar=c.srcF[:, bass.ds(g * 4 + k, 1)], in1=c.upper[:],
                                                      op0=ALU.is_equal, op1=ALU.mult, accum_out=dup[b][:, k:k + 1])
                    last.then_inc(S("dup"), 1)
                    v.wait_ge(S("dup"), g + 1)
                    v.tensor_copy(chunk(dupF, g, K4), dup[b][:]).then_inc(S("bfree"), 1)
            pairs(v, d.EM, tiles)
            v.wait_ge(S("bfree"), d.EM + 2)
            v.tensor_scalar(a1[:], dupF[:], 0.5, None, ALU.is_gt).then_inc(S("a1"), 1)
            v.tensor_scalar(a2[:], c.srcF[:], 0.0, None, ALU.is_lt).then_inc(S("a2"), 1)
            v.wait_ge(S("spare"), 1)
            v.tensor_copy(spareF[:], spareI[:]).then_inc(S("spareF"), 1)
            v.wait_ge(S("a2"), 1)
            v.tensor_tensor(a1[:], a1[:], a2[:], ALU.max).then_inc(S("a3"), 1)
            v.wait_ge(S("spareF"), 1)
            v.wait_ge(S("a3"), 1)
            v.tensor_scalar(a2[:], c.srcF[:], -1.0, spareF[:], ALU.mult, ALU.add).then_inc(S("a4"), 1)
            v.wait_ge(S("a4"), 1)
            v.tensor_tensor(a2[:], a2[:], a1[:], ALU.mult).then_inc(S("a5"), 1)
            v.wait_ge(S("a5"), 1)
            v.tensor_tensor(c.accI[:], a2[:], c.srcF[:], ALU.add).then_inc(S("a6"), 1)

        @block.gpsimd
        def _(pool):
            pool.iota(spareI[:], pattern=[[1, 1]], base=d.NP, channel_multiplier=1).then_inc(S("spare"), 1)
    S.end()


def prepare_weights(nc, c, w):
    d, S = c.d, Signals(nc, "weights")
    QP, EL_ROWS = d.QP, 256
    qf, rem = d.E // 256, d.E % 256
    with ExitStack() as st:
        def sb(name, shape, dt=F32):
            return st.enter_context(nc.sbuf_tensor(f"{S.tag}_{name}", shape, dt))
        asd = sb("asd", [P, 5, 2, D])
        al1 = sb("al1", [P, 2, 2, 64])
        aed, we = sb("aed", [16, 5, D]), sb("we", [16, 5, D])
        prod = sb("prod", [P, 5, D])
        prod2 = sb("prod2", [P, 4, 64])
        prodb = sb("prodb", [P, 4, 64])
        vcol = sb("vcol", [16, 5])
        vbc = sb("vbc", [16, 5, P])
        vrow = sb("vrow", [P, 5, 16])
        eat = sb("eat", [P, 256, 16])
        pe_prod = sb("ea_prod", [P, 256, 16])
        bcol = sb("bcol", [P, 3])
        mid = sb("mid", [P, 3, D])
        ps = st.enter_context(nc.psum_tensor("w_ps", [P, 512], F32))
        psv = st.enter_context(nc.psum_tensor("v_ps", [P, 5, 16], F32))
        block = st.enter_context(nc.Block())

        def rowvec(a):
            return a.rearrange("(a n) -> a n", a=1).broadcast_to([P, a.shape[0]])

        def colvec(a):
            return a.rearrange("(p a) -> p a", a=1)

        loads = []
        for l in range(5):
            loads += [(c.W0[:, l, 0:D], w["L0_gnn_Ws"][l]),
                      (asd[:, l, 0, :], rowvec(w["L0_gnn_a_srcs"][l])), (asd[:, l, 1, :], rowvec(w["L0_gnn_a_dsts"][l])),
                      (we[:, l, :], w["L0_gnn_Wes"][l]),
                      (aed[:, l, :], w["L0_gnn_a_edges"][l].rearrange("(a n) -> a n", a=1).broadcast_to([16, D]))]
        loads += [(mid[:, i, :], w["L0_gnn_mid_ws"][i]) for i in range(3)]
        loads += [(bcol[:, i:i + 1], colvec(w["L0_gnn_biases"][i + 1])) for i in range(3)]
        loads += [(c.b0row[:], rowvec(w["L0_gnn_biases"][0])), (c.b4row[:], rowvec(w["L0_gnn_biases"][4])),
                  (c.b0col[:], colvec(w["L0_gnn_biases"][0])),
                  (c.W5[:, 0:D], w["L1_gnn_W"]), (c.blin[:, 0:D], rowvec(w["L1_gnn_b_lin"])),
                  (c.b5row[:], rowvec(w["L1_gnn_bias"])),
                  (al1[:].rearrange("p a b n -> p (a b n)"), w["L1_gnn_alpha"].rearrange("a h n -> a (h n)").broadcast_to([P, 256])),
                  (c.W2n[:], w["L2_gnn_nbr_w"]), (c.W2s[:], w["L2_gnn_self_w"]), (c.b2nrow[:], rowvec(w["L2_gnn_b"])),
                  (c.Ws[0][:, 0, :], w["L3_gnn_Ws0"]), (c.Wn[0][:, 0, :], w["L3_gnn_Wn0"]),
                  (c.b3row[:], rowvec(w["L3_gnn_b2"])), (c.bcol[2][:], colvec(w["L3_gnn_b2"]))]
        for f in range(2):
            loads += [(c.Ws[1][:, f, :], w["L3_gnn_Ws1"][f * P:(f + 1) * P, :]), (c.Wn[1][:, f, :], w["L3_gnn_Wn1"][f * P:(f + 1) * P, :]),
                      (c.Ws[2][:, f, :], w["L3_gnn_Ws2"][f * P:(f + 1) * P, :]), (c.Wn[2][:, f, :], w["L3_gnn_Wn2"][f * P:(f + 1) * P, :]),
                      (c.bcol[0][:, f:f + 1], colvec(w["L3_gnn_b0"][f * P:(f + 1) * P])),
                      (c.bcol[1][:, f:f + 1], colvec(w["L3_gnn_b1"][f * P:(f + 1) * P]))]

        @block.sync
        def _(sp):
            for dst, src in loads:
                sp.dma_start(dst, src).then_inc(S("w_in"), 16)
            sp.wait_ge(S("ea_clear"), 1)
            ea = w["edge_attr_16"]
            sp.dma_start(eat[0:qf, :, :], ea[0:qf * 256, :].rearrange("(q j) f -> q j f", j=256)).then_inc(S("ea_in"), 16)
            if rem:
                sp.dma_start(eat[qf:qf + 1, 0:rem, :], ea[qf * 256:d.E, :].rearrange("(q j) f -> q j f", q=1)).then_inc(S("ea_in2"), 16)

        @block.gpsimd
        def _(pool):
            pool.memset(eat[:], 0.0).then_inc(S("ea_clear"), 1)
            pool.memset(c.zero[:], 0.0).then_inc(S("zero"), 1)
            pool.wait_ge(S("zero"), 1)
            total = d.NP // P + 1
            for g in range(0, total, 64):
                n = min(64, total - g)
                pool.dma_start(c.NS.rearrange("(p a) f -> p a f", p=P)[:, g:g + n, :],
                               c.zero[:].rearrange("p (a f) -> p a f", a=1).broadcast_to([P, n, D])).then_inc(S("ns_zero"), 16)
            pool.wait_ge(S("ns_zero"), 16 * len(range(0, total, 64)))

        @block.vector
        def _(v):
            v.wait_ge(S("w_in"), 16 * len(loads))
            for l in range(5):
                if l:
                    v.wait_ge(S("w0_ext"), l)
                v.tensor_tensor(prod[:, 0:2, :], c.W0[:, l, 0:D].unsqueeze(1).broadcast_to([P, 2, D]), asd[:, l, :, :],
                                ALU.mult).then_inc(S("wa"), 1)
                v.wait_ge(S("wa"), l + 1)
                v.tensor_reduce(c.W0[:, l, D:D + 2], prod[:, 0:2, :], AX, ALU.add).then_inc(S("w0_ext"), 1)
            v.memset(c.W5[:, D:D + 8], 0.0)
            v.memset(c.blin[:, D:D + 8], 0.0).then_inc(S("ext_clear"), 1)
            for n, (t, pr) in enumerate(((c.W5, prod2), (c.blin, prodb))):
                v.tensor_tensor(pr[:].rearrange("p (a b) n -> p a (b n)", a=2), t[:, 0:D].unsqueeze(1).broadcast_to([P, 2, D]),
                                al1[:].rearrange("p a b n -> p a (b n)"), ALU.mult).then_inc(S("w5_prod"), 1)
                v.wait_ge(S("w5_prod"), n + 1)
                v.wait_ge(S("ext_clear"), 1)
                v.tensor_reduce(t[:, D:D + 2], pr[:, 0:2, :], AX, ALU.add)
                v.tensor_reduce(t[:, D + 6:D + 8], pr[:, 2:4, :], AX, ALU.add)
            for i in range(3):
                beta = math.log(THETA / (i + 1) + 1.0)
                v.tensor_scalar(mid[:, i, :], mid[:, i, :], beta, None, ALU.mult).then_inc(S("beta_m"), 1)
                v.wait_ge(S("beta_m"), i + 1)
                v.scalar_tensor_tensor(out=c.M[:, i, :], in0=c.ident[:], scalar=1.0 - beta, in1=mid[:, i, :],
                                       op0=ALU.mult, op1=ALU.add).then_inc(S("mid"), 1)
            v.wait_ge(S("w0_ext"), 5)
            v.tensor_tensor(prod[0:16, :, :], we[:], aed[:], ALU.mult).then_inc(S("we_prod"), 1)
            v.wait_ge(S("we_prod"), 1)
            v.tensor_reduce(vcol[:], prod[0:16, :, :], AX, ALU.add).then_inc(S("vcol"), 1)
            v.wait_ge(S("vcol"), 1)
            v.tensor_copy(vbc[:], vcol[:].unsqueeze(2).broadcast_to([16, 5, P])).then_inc(S("vbc"), 1)
            v.wait_ge(S("vrow_ps"), 1)
            v.tensor_copy(vrow[:], psv[:]).then_inc(S("vrow"), 1)
            v.wait_ge(S("vrow"), 1)
            v.wait_ge(S("ea_in"), 16)
            if rem:
                v.wait_ge(S("ea_in2"), 16)
            for l in range(5):
                if l:
                    v.wait_ge(S("el"), l)
                v.tensor_tensor(pe_prod[:], eat[:], vrow[:, l, :].unsqueeze(1).broadcast_to([P, 256, 16]), ALU.mult).then_inc(S("ea_prod"), 1)
                v.wait_ge(S("ea_prod"), l + 1)
                v.tensor_reduce(c.EL[:, l, :], pe_prod[:], AX, ALU.add).then_inc(S("el"), 1)
            v.wait_ge(S("bm_ps"), 1)
            v.tensor_scalar(c.bm[:], ps[:, 0:3], 1.0 - ALPHA, None, ALU.mult).then_inc(S("bm"), 1)

        @block.tensor
        def _(pe):
            pe.wait_ge(S("mid"), 3)
            pe.wait_ge(S("w_in"), 16 * len(loads))
            for i in range(3):
                last = pe.matmul(ps[:, i:i + 1], c.M[:, i, :], bcol[:, i:i + 1], start=True, stop=True)
            last.then_inc(S("bm_ps"), 1)
            pe.wait_ge(S("vbc"), 1)
            for l in range(5):
                last = pe.matmul(psv[:, l, :], vbc[:, l, :], c.ident[0:16, 0:16], start=True, stop=True)
            last.then_inc(S("vrow_ps"), 1)
    S.end()


class Norm:

    def __init__(self, st, nc, S, name, par):
        def sb(n, shape):
            return [st.enter_context(nc.sbuf_tensor(f"{S.tag}_{name}_{n}{i}", shape, F32)) for i in range(par)]
        self.S, self.name = S, name
        self.st, self.mv, self.ve = sb("st", [P, K4, 6]), sb("mv", [P, K4, 2]), sb("ve", [P, K4])
        self.sd, self.rs, self.nm = sb("sd", [P, K4]), sb("rs", [P, K4]), sb("nm", [P, K4])

    def stats(self, v, b, g, x):
        S, n = self.S, self.name
        for k in range(K4):
            last = v.bn_stats(self.st[b][:, k, :], x[:, k, :])
        last.then_inc(S(n + "_stats"), 1)

    def moments(self, v, b, g):
        S, n = self.S, self.name
        v.wait_ge(S(n + "_stats"), g + 1)
        v.sem_inc(S("dve_pass"), 1)
        for k in range(K4):
            last = v.bn_aggr(self.mv[b][:, k, :], self.st[b][:, k, :])
        last.then_inc(S(n + "_mv"), 1)

    def variance(self, v, b, g):
        S, n = self.S, self.name
        v.wait_ge(S(n + "_mv"), g + 1)
        v.tensor_scalar(self.ve[b][:], self.mv[b][:, :, 1], EPS, None, ALU.add).then_inc(S(n + "_var"), 1)

    def root(self, act, b, g):
        S, n = self.S, self.name
        act.wait_ge(S(n + "_var"), g + 1)
        act.activation(self.sd[b][:], self.ve[b][:], ACT.Sqrt).then_inc(S(n + "_sd"), 1)

    def recip(self, v, b, g):
        S, n = self.S, self.name
        v.wait_ge(S(n + "_sd"), g + 1)
        v.reciprocal(self.rs[b][:], self.sd[b][:]).then_inc(S(n + "_rs"), 1)

    def shift(self, v, b, g):
        S, n = self.S, self.name
        v.wait_ge(S(n + "_rs"), g + 1)
        v.scalar_tensor_tensor(out=self.nm[b][:], in0=self.mv[b][:, :, 0], scalar=-1.0, in1=self.rs[b][:],
                               op0=ALU.mult, op1=ALU.mult).then_inc(S(n + "_nm"), 1)

    def vector(self, v, gb, x):
        for g, b in gb:
            self.stats(v, b, g, x[b])
        for step in (self.moments, self.variance, self.recip, self.shift):
            for g, b in gb:
                step(v, b, g)

    def apply(self, act, b, g, out, x, done):
        S, n = self.S, self.name
        act.wait_ge(S(n + "_nm"), g + 1)
        for k in range(K4):
            last = act.activation(out[:, k, :], x[:, k, :], ACT.Relu, bias=self.nm[b][:, k:k + 1], scale=self.rs[b][:, k:k + 1])
        last.then_inc(done, 1)


def turn(pe, out, src, ident, done):
    for k in range(K4):
        last = pe.transpose(out[:, k * P:(k + 1) * P], src[:, k, :], ident)
    last.then_inc(done, 1)


def turn_back(pe, out, src, ident, done):
    for k in range(K4):
        last = pe.transpose(out[:, k, :], src[:, k * P:(k + 1) * P], ident)
    last.then_inc(done, 1)


def rows_of(pe, out, hT, w, done):
    for k in range(K4):
        last = pe.matmul(out[:, k, 0:w.shape[1]], hT[:, k * P:(k + 1) * P], w, start=True, stop=True)
    last.then_inc(done, 1)


FLY = 4


def node_groups(eng, nm, body):
    full = (nm - 2) // FLY
    rest = list(range(full * FLY, nm))
    if full:
        with eng.Fori(0, full) as i:
            body([(i * FLY + b, b) for b in range(FLY)])
    body([(g, b) for b, g in enumerate(rest)])


def node_groups_ahead(eng, nm, body):
    full = (nm - 2) // FLY
    rest = [(g, b) for b, g in enumerate(range(full * FLY, nm))]
    if full > 1:
        with eng.Fori(0, full - 1) as i:
            body([(i * FLY + b, b) for b in range(FLY)], [(i * FLY + FLY + b, b) for b in range(FLY)])
    if full:
        body([((full - 1) * FLY + b, b) for b in range(FLY)], rest)
    body(rest, [])


def first_group(nm):
    return [(b, b) for b in range(FLY if (nm - 2) // FLY else nm)]


def store_rows(sp, S, nm, n, table, g, b, buf, stores):
    if isinstance(g, int) and g == nm - 1:
        before = (b - 1) % FLY
        sp.wait_ge(S(f"st{before}"), ((g - 1 - before) // FLY) * stores * 16 + 16 * n)
    sp.sem_inc(S("sp_pass"), 1)
    sp.dma_start(table, buf).then_inc(S(f"st{b}"), 16)


def pool_alone(pool, c, issue, take, settle):
    U, n = c.d.U, c.d.EM // c.d.U
    for j in range(U):
        issue(j, j)
    if n > 1:
        with pool.Fori(1, n) as i:
            for j in range(U):
                take(i * U - U + j, j, i - 1)
            for j in range(U):
                settle(i * U - U + j, j, i - 1)
                issue(i * U + j, j)
    for j in range(U):
        take((n - 1) * U + j, j, n - 1)
    for j in range(U):
        settle((n - 1) * U + j, j, n - 1)


class PoolJobs:

    def __init__(self, st, nc, c, S, width=D):
        self.c, self.S = c, S

        def sb(name, shape, dt):
            return [st.enter_context(nc.sbuf_tensor(f"{S.tag}_{name}{j}", shape, dt)) for j in range(c.d.U)]
        self.ix, self.val = sb("pj_ix", [P, K4], I32), sb("pj_val", [P, K4], I32)
        self.got = sb("pj_got", [P, K4], I32)
        self.ring = sb("pj_ring", [P, K4, width], F32)
        self.base, self.ixs = [0] * c.d.U, 0

    def gate(self, pool):
        pool.sem_inc(self.S("pool_pass"), 1)

    def stage(self, pool, out_in, m):
        S, n = self.S, len(out_in)
        for out, src in out_in:
            pool.tensor_copy(out[:], chunk(src, m, K4)).then_inc(S("pj_ix"), 1)
        pool.wait_ge(S("pj_ix"), m * n + n + self.ixs)
        self.gate(pool)

    def landed(self, pool, j, r, each):
        pool.wait_ge(self.S(f"slot{j}"), r * each + each + self.base[j])
        self.gate(pool)

    def finish(self, copies, each):
        U, n = self.c.d.U, self.c.d.EM // self.c.d.U
        self.ixs += copies * self.c.d.EM
        for j in range(U):
            self.base[j] += n * each

    def slots_out(self, pool):
        c, S, d = self.c, self.S, self.c.d

        def issue(m, j):
            self.stage(pool, ((self.ix[j], c.canonI), (self.val[j], c.slotI)), m)
            for k in range(K4):
                pool.indirect_dma_start(out=c.POS, out_offset=bass.IndirectOffsetOnAxis(ap=self.ix[j][:, k:k + 1], axis=0),
                                        in_=self.val[j][:, k:k + 1], in_offset=None, bounds_check=d.N - 1,
                                        oob_is_err=False).then_inc(S(f"slot{j}"), 16)
        pool_alone(pool, c, issue, lambda m, j, r: None, lambda m, j, r: self.landed(pool, j, r, 64))
        self.finish(2, 64)

    def slots_in(self, pool, tmp):
        c, S = self.c, self.S

        def issue(m, j):
            self.stage(pool, ((self.ix[j], c.idxS),), m)
            for k in range(K4):
                pool.indirect_dma_start(out=self.got[j][:, k:k + 1], out_offset=None, in_=c.POS,
                                        in_offset=bass.IndirectOffsetOnAxis(ap=self.ix[j][:, k:k + 1], axis=0)
                                        ).then_inc(S(f"slot{j}"), 16)

        def take(m, j, r):
            self.landed(pool, j, r, 64)
            pool.tensor_copy(chunk(tmp, m, K4), self.got[j][:]).then_inc(S("pj_taken"), 1)

        def settle(m, j, r):
            pool.wait_ge(S("pj_taken"), m + 1)
            self.gate(pool)
        pool_alone(pool, c, issue, take, settle)
        self.finish(1, 64)
        pool.tensor_copy(c.idxS[:], tmp[:]).then_inc(S("pj_slots"), 1)
        pool.wait_ge(S("pj_slots"), 1)
        self.gate(pool)

    def dst_rows(self, pool, table, target):
        c, S = self.c, self.S

        def issue(m, j):
            self.stage(pool, ((self.ix[j], c.idxD),), m)
            for k in range(K4):
                pool.indirect_dma_start(out=self.ring[j][:, k, :], out_offset=None, in_=table,
                                        in_offset=bass.IndirectOffsetOnAxis(ap=self.ix[j][:, k:k + 1], axis=0)
                                        ).then_inc(S(f"slot{j}"), 16)

        def take(m, j, r):
            pool.wait_ge(S(f"slot{j}"), r * 80 + 64 + self.base[j])
            self.gate(pool)
            pool.dma_start(edge_rows(target, m), self.ring[j][:]).then_inc(S(f"slot{j}"), 16)
        pool_alone(pool, c, issue, take, lambda m, j, r: self.landed(pool, j, r, 80))
        self.finish(1, 80)


def nodes_gat(nc, c, x):
    d, S = c.d, Signals(nc, "gatn")
    N, NM = d.N, d.NM
    with ExitStack() as st:
        def each(name, shape, dt=F32):
            return [st.enter_context(nc.sbuf_tensor(f"{S.tag}_{name}{i}", shape, dt)) for i in range(FLY)]
        xin, r, x0, x0s = each("xin", [P, K4, D]), each("r", [P, K4, D]), each("x0", [P, K4, D]), each("x0s", [P, K4, D])
        rT, tT, z = each("rT", [P, MAC]), each("tT", [P, MAC]), each("z", [P, MAC])
        hp = [each(f"hp{l}_", [P, K4, c.TW[l]]) for l in range(6)]
        x1, x2 = each("x1", [P, K4, D]), each("x2", [P, K4, D])
        t = x0
        tmp = st.enter_context(nc.sbuf_tensor(f"{S.tag}_tmp", [P, d.ET], I32))
        jobs = PoolJobs(st, nc, c, S)
        ln0, ln1 = Norm(st, nc, S, "ln0", FLY), Norm(st, nc, S, "ln1", FLY)
        psR = [st.enter_context(nc.psum_tensor(f"{S.tag}_psR{i}", [P, MAC], F32)) for i in range(FLY)]
        psT = [st.enter_context(nc.psum_tensor(f"{S.tag}_psT{i}", [P, MAC], F32)) for i in range(FLY)]
        block = st.enter_context(nc.Block())

        def k4(q):
            return q[:].rearrange("p (k f) -> p k f", k=K4)

        def ext(q, n):
            return q[:, 0:K4 * n].rearrange("p (k f) -> p k f", k=K4)

        def row(t_, n=D):
            return t_[:].unsqueeze(1).broadcast_to([P, K4, n])

        @block.gpsimd
        def _(pool):
            jobs.slots_out(pool)
            jobs.slots_in(pool, tmp)
            jobs.dst_rows(pool, x, c.XD)

        @block.sync
        def _(sp):
            def load(gb):
                for g, b in gb:
                    sp.wait_ge(S("x1"), g + 1)
                    sp.sem_inc(S("sp_pass"), 1)
                    sp.dma_start(xin[b][:], node_rows(x, g, N)).then_inc(S(f"x_load{b}"), 16)

            def body(gb, ahead):
                for l in range(6):
                    if l == 5:
                        load(ahead)
                    for g, b in gb:
                        sp.wait_ge(S(f"hp{l}"), g + 1)
                        store_rows(sp, S, NM, l + 1, node_rows(c.HP[l][0:N, :], g, N), g, b, hp[l][b][:], 7)
                for g, b in gb:
                    sp.wait_ge(S("x2"), g + 1)
                    store_rows(sp, S, NM, 7, node_rows(c.X2[0:N, :], g, N), g, b, x2[b][:], 7)
                for g, b in gb:
                    sp.wait_ge(S(f"st{b}"), (g - b) * (112 // FLY) + 112)
                    sp.sem_inc(S("rows_free"), 1)
            load(first_group(NM))
            node_groups_ahead(sp, NM, body)

        @block.vector
        def _(v):
            v.sem_inc(S("x1"), FLY)
            v.sem_inc(S("hp5_free"), FLY)

            def body(gb):
                for g, b in gb:
                    v.wait_ge(S(f"x_load{b}"), (g - b) * (16 // FLY) + 16)
                ln0.vector(v, gb, xin)
                for g, b in gb:
                    v.wait_ge(S("hp0"), g + 1)
                    v.tensor_tensor(x0[b][:], hp[0][b][:, :, 0:D], row(c.b0row), ALU.add).then_inc(S("x0"), 1)
                for g, b in gb:
                    v.wait_ge(S("x0"), g + 1)
                    v.tensor_scalar(x0s[b][:], x0[b][:], ALPHA, None, ALU.mult).then_inc(S("x0s"), 1)
                for l in (1, 2, 3):
                    for g, b in gb:
                        v.wait_ge(S(f"hp{l}"), g + 1)
                        v.wait_ge(S("x0s"), g + 1)
                        v.scalar_tensor_tensor(out=t[b][:], in0=hp[l][b][:, :, 0:D], scalar=1.0 - ALPHA, in1=x0s[b][:],
                                               op0=ALU.mult, op1=ALU.add).then_inc(S(f"t{l}"), 1)
                    for g, b in gb:
                        v.wait_ge(S(f"z{l}"), g + 1)
                        v.scalar_tensor_tensor(out=tT[b][:], in0=z[b][:], scalar=0.01, in1=z[b][:],
                                               op0=ALU.mult, op1=ALU.max).then_inc(S(f"h{l}"), 1)
                for g, b in gb:
                    v.wait_ge(S("hp4"), g + 1)
                    v.tensor_tensor(x1[b][:], hp[4][b][:, :, 0:D], row(c.b4row), ALU.add).then_inc(S("x1a"), 1)
                for g, b in gb:
                    v.wait_ge(S("x1a"), g + 1)
                    v.tensor_tensor(x1[b][:], x1[b][:], xin[b][:], ALU.add).then_inc(S("x1"), 1)
                v.wait_ge(S("x1"), gb[-1][0] + 1 + FLY)
                ln1.vector(v, gb, x1)
                for g, b in gb:
                    v.wait_ge(S("rows5"), g + 1)
                    v.tensor_tensor(hp[5][b][:, :, 0:D], k4(psR[b]), row(c.blin[:, 0:D]), ALU.add)
                    v.tensor_tensor(hp[5][b][:, :, D:D + 8], ext(psT[b], 8), c.blin[:, D:D + 8].unsqueeze(1).broadcast_to([P, K4, 8]),
                                    ALU.add).then_inc(S("hp5"), 1)
                for g, b in gb:
                    v.wait_ge(S("hp5"), g + 1)
                    v.sem_inc(S("hp5_free"), 1)
                    v.tensor_tensor(x2[b][:], hp[5][b][:, :, 0:D], row(c.b5row), ALU.add).then_inc(S("x2a"), 1)
                for g, b in gb:
                    v.wait_ge(S("x2a"), g + 1)
                    v.tensor_tensor(x2[b][:], x2[b][:], x1[b][:], ALU.add).then_inc(S("x2"), 1)
            node_groups(v, NM, body)

        @block.scalar
        def _(act):
            act.sem_inc(S("rows_free"), FLY)

            def copies(gb, out, src, ready, done):
                for g, b in gb:
                    act.wait_ge(S(ready), g + 1)
                    act.activation(out[b][:], src[b][:], ACT.Copy).then_inc(S(done), 1)

            def row_copies(gb, l):
                for g, b in gb:
                    act.wait_ge(S(f"rows{l}"), g + 1)
                    act.activation(hp[l][b][:, :, 0:D], k4(psR[b]), ACT.Copy)
                    act.activation(hp[l][b][:, :, D:D + 2], ext(psT[b], 2), ACT.Copy).then_inc(S(f"hp{l}"), 1)

            def body(gb):
                for g, b in gb:
                    ln0.root(act, b, g)
                for g, b in gb:
                    ln0.apply(act, b, g, r[b], xin[b], S("r"))
                copies(gb, rT, psT, "rTp", "rT")
                act.wait_ge(S("rows_free"), gb[-1][0] + 1)
                for l in range(4):
                    row_copies(gb, l)
                    if l == 0:
                        copies(gb, rT, psT, "x0Tp", "x0T")
                    else:
                        copies(gb, rT, psT, f"tTp{l}", f"tT{l}")
                        for g, b in gb:
                            act.wait_ge(S(f"mid{l}"), g + 1)
                            act.activation(z[b][:], psR[b][:], ACT.Identity, bias=c.bm[:, l - 1:l]).then_inc(S(f"z{l}"), 1)
                row_copies(gb, 4)
                for g, b in gb:
                    ln1.root(act, b, g)
                for g, b in gb:
                    ln1.apply(act, b, g, r[b], x1[b], S("r1"))
                copies(gb, rT, psT, "r1Tp", "r1T")
            node_groups(act, NM, body)

        @block.tensor
        def _(pe):
            def project(gb, ready, src, w, n, done):
                for g, b in gb:
                    pe.wait_ge(S(ready), g + 1)
                    for k in range(K4):
                        pe.matmul(k4(psR[b])[:, k, :], src[b][:, k * P:(k + 1) * P], w[:, 0:D], start=True, stop=True)
                        last = pe.matmul(ext(psT[b], n)[:, k, :], src[b][:, k * P:(k + 1) * P], w[:, D:D + n], start=True, stop=True)
                    last.then_inc(S(done), 1)

            def turns(gb, ready, src, done):
                for g, b in gb:
                    pe.wait_ge(S(ready), g + 1)
                    turn(pe, psT[b], src[b], c.ident[:], S(done))

            def body(gb):
                for g, b in gb:
                    pe.wait_ge(S("r"), g + 1)
                    pe.wait_ge(S("hp5_free"), g + 1)
                    turn(pe, psT[b], r[b], c.ident[:], S("rTp"))
                project(gb, "rT", rT, c.W0[:, 0, :], 2, "rows0")
                turns(gb, "x0", x0, "x0Tp")
                for l in (1, 2, 3):
                    project(gb, "x0T" if l == 1 else f"h{l - 1}", rT if l == 1 else tT, c.W0[:, l, :], 2, f"rows{l}")
                    turns(gb, f"t{l}", t, f"tTp{l}")
                    for g, b in gb:
                        pe.wait_ge(S(f"tT{l}"), g + 1)
                        pe.matmul(psR[b][:], c.M[:, l - 1, :], rT[b][:], start=True, stop=True).then_inc(S(f"mid{l}"), 1)
                project(gb, "h3", tT, c.W0[:, 4, :], 2, "rows4")
                turns(gb, "r1", r, "r1Tp")
                project(gb, "r1T", rT, c.W5[:], 8, "rows5")
            node_groups(pe, NM, body)
    S.end()


class Runs:

    def __init__(self, st, nc, c, S):
        self.c, self.S = c, S
        self.low = st.enter_context(nc.sbuf_tensor(f"{S.tag}_low", [4, c.d.QP + 1], F32))
        self.zero = st.enter_context(nc.sbuf_tensor(f"{S.tag}_zero", [4, c.d.QP + 1], F32))
        self.back = st.enter_context(nc.sbuf_tensor(f"{S.tag}_back", [4, c.d.QP + 1], F32))
        self.psE = st.enter_context(nc.psum_tensor(f"{S.tag}_psE", [P, 512], F32))
        self.psC = st.enter_context(nc.psum_tensor(f"{S.tag}_psC", [P, 512], F32))

    def start(self, v):
        S = self.S
        v.memset(self.low[:], -BIG)
        v.memset(self.zero[:], 0.0)
        v.memset(self.back[:], 0.0).then_inc(S("edges_set"), 1)
        v.wait_ge(S("edges_set"), 1)

    def parts(self, kind):
        c, q = self.c, self.c.d.QP
        if kind == "sum":
            return c.contF, c.wholeF, c.runF, self.zero, 0.0, ALU.mult, ALU.add
        if kind == "max":
            return c.negF, c.negWholeF, c.negRunF, self.low, -BIG, ALU.add, ALU.max
        return c.contB, c.wholeB, c.runB, self.back, 0.0, ALU.mult, ALU.add

    def vector(self, v, name, kind, heads, out, vals):
        S, q = self.S, self.c.d.QP
        cont, whole, run, ends, init, op0, op1 = self.parts(kind)
        a = cont[0:q, 0:heads, :].rearrange("q h j -> q (h j)")
        o, x = out[0:q].rearrange("q h j -> q (h j)"), vals[0:q].rearrange("q h j -> q (h j)")
        if kind == "spread":
            v.tensor_tensor_scan(o[:, ::-1], a[:, ::-1], x[:, ::-1], init, op0, op1).then_inc(S(name + "_y"), 1)
            v.wait_ge(S(name + "_end"), 1)
            v.tensor_tensor_scan(ends[0:heads, 0:q][:, ::-1], whole[0:heads, :][:, ::-1], self.psE[0:heads, 0:q][:, ::-1],
                                 init, op0, op1).then_inc(S(name + "_c"), 1)
        else:
            v.tensor_tensor_scan(o, a, x, init, op0, op1).then_inc(S(name + "_y"), 1)
            v.wait_ge(S(name + "_end"), 1)
            v.tensor_tensor_scan(ends[0:heads, 1:q + 1], whole[0:heads, :], self.psE[0:heads, 0:q],
                                 init, op0, op1).then_inc(S(name + "_c"), 1)
        v.wait_ge(S(name + "_carry"), 1)
        for h in range(heads):
            last = v.scalar_tensor_tensor(out=out[0:q, h, :], in0=run[0:q, :], scalar=self.psC[0:q, h:h + 1],
                                          in1=out[0:q, h, :], op0=op0, op1=op1)
        last.then_inc(S(name), 1)
        v.wait_ge(S(name), 1)

    def tensor(self, pe, name, kind, heads, out):
        S, q, c = self.S, self.c.d.QP, self.c
        ends = self.parts(kind)[3]
        pe.wait_ge(S(name + "_y"), 1)
        edge = 0 if kind == "spread" else 255
        pe.transpose(self.psE[0:heads, 0:q], out[0:q, 0:heads, edge], c.ident[0:q, 0:q]).then_inc(S(name + "_end"), 1)
        pe.wait_ge(S(name + "_c"), 1)
        carried = ends[0:heads, 1:q + 1] if kind == "spread" else ends[0:heads, 0:q]
        pe.transpose(self.psC[0:q, 0:heads], carried, c.ident[0:heads, 0:heads]).then_inc(S(name + "_carry"), 1)


def edge_degrees(nc, c):
    d, S = c.d, Signals(nc, "degrees")
    q = d.QP
    with ExitStack() as st:
        def sb(name, h=1):
            return st.enter_context(nc.sbuf_tensor(f"{S.tag}_{name}", [P, h, 256], F32))
        one, deg, dl, deg_all, inv = sb("one"), sb("deg"), sb("dl"), sb("deg_all"), sb("inv")
        esum = [sb(f"esum{l}") for l in range(5)]
        runs = Runs(st, nc, c, S)
        ps = st.enter_context(nc.psum_tensor(f"{S.tag}_ps", [P, 2, P], F32))
        block = st.enter_context(nc.Block())

        @block.vector
        def _(v):
            runs.start(v)
            v.memset(one[:], 1.0).then_inc(S("one"), 1)
            v.wait_ge(S("one"), 1)
            runs.vector(v, "deg", "sum", 1, deg, one)
            v.tensor_tensor(dl[0:q, 0, :], deg[0:q, 0, :], c.last[0:q], ALU.mult).then_inc(S("dl"), 1)
            v.wait_ge(S("dl"), 1)
            runs.vector(v, "deg_all", "spread", 1, deg_all, dl)
            v.reciprocal(inv[0:q], deg_all[0:q]).then_inc(S("inv"), 1)
            v.wait_ge(S("inv"), 1)
            for l in range(5):
                runs.vector(v, f"esum{l}", "sum", 1, esum[l], c.EL[:, l:l + 1, :])
                v.tensor_tensor(c.loopEL[0:q, l, :], esum[l][0:q, 0, :], inv[0:q, 0, :], ALU.mult).then_inc(S("loop"), 1)
            v.wait_ge(S("inv_cols"), 1)
            for j in range(2):
                last = v.tensor_copy(c.invdeg[:, j::2], ps[:, j, 0:q])
            last.then_inc(S("invdeg"), 1)

        @block.tensor
        def _(pe):
            runs.tensor(pe, "deg", "sum", 1, deg)
            runs.tensor(pe, "deg_all", "spread", 1, deg_all)
            for l in range(5):
                runs.tensor(pe, f"esum{l}", "sum", 1, esum[l])
            pe.wait_ge(S("inv"), 1)
            for j in range(2):
                last = pe.transpose(ps[:, j, 0:q], inv[0:q, 0, j * P:(j + 1) * P], c.ident[0:q, 0:q])
            last.then_inc(S("inv_cols"), 1)
    S.end()


class Gather:

    def __init__(self, st, nc, c, S, width, dt=F32):
        self.c, self.S, self.U = c, S, c.d.U
        self.ring = [st.enter_context(nc.sbuf_tensor(f"{S.tag}_ring{j}", [P, K4, width], dt)) for j in range(self.U)]
        self.ix = [st.enter_context(nc.sbuf_tensor(f"{S.tag}_ix{j}", [P, K4], I32)) for j in range(self.U)]

    def rows(self, pool, table, idx):
        S, U = self.S, self.U
        pool.sem_inc(S("ring_free"), U)
        with pool.Fori(0, self.c.d.EM // U) as i:
            for j in range(U):
                m = i * U + j
                pool.wait_ge(S("ring_free"), m + 1)
                pool.sem_inc(S("pool_pass"), 1)
                pool.tensor_copy(self.ix[j][:], chunk(idx, m, K4)).then_inc(S("ix"), 1)
                pool.wait_ge(S("ix"), m + 1)
                pool.sem_inc(S("pool_pass"), 1)
                for k in range(K4):
                    pool.indirect_dma_start(out=self.ring[j][:, k, :], out_offset=None, in_=table,
                                            in_offset=bass.IndirectOffsetOnAxis(ap=self.ix[j][:, k:k + 1], axis=0)
                                            ).then_inc(S(f"slot{j}"), 16)

    def each(self, eng, use):
        with eng.Fori(0, self.c.d.EM // self.U) as i:
            for j in range(self.U):
                eng.wait_ge(self.S(f"slot{j}"), i * 64 + 64)
                use(i * self.U + j, j)


def rows_of_dst(nc, c, tag, table, target, scores=False):
    d, S = c.d, Signals(nc, tag)
    with ExitStack() as st:
        g = Gather(st, nc, c, S, table.shape[1])
        block = st.enter_context(nc.Block())

        @block.gpsimd
        def _(pool):
            g.rows(pool, table, c.idxD)

        @block.sync
        def _(sp):
            def store(m, j):
                sp.sem_inc(S("sp_pass"), 1)
                sp.dma_start(edge_rows(target, m), g.ring[j][:]).then_inc(S(f"out{j}"), 16)
            g.each(sp, store)

        @block.vector
        def _(v):
            def use(m, j):
                if scores:
                    v.tensor_copy(chunk(c.SL, m, K4), g.ring[j][:, :, D])
                    v.tensor_copy(chunk(c.SD, m, K4), g.ring[j][:, :, D + 1]).then_inc(S("cols"), 1)
                    v.wait_ge(S("cols"), m + 1)
            with v.Fori(0, d.EM // d.U) as i:
                for j in range(d.U):
                    v.wait_ge(S(f"slot{j}"), i * 64 + 64)
                    use(i * d.U + j, j)
                    v.wait_ge(S(f"out{j}"), i * 16 + 16)
                    v.sem_inc(S("ring_free"), 1)
    S.end()


def edge_setup(nc, c, x):
    edge_degrees(nc, c)
    rows_of_dst(nc, c, "hp0d", c.HP[0][0:c.d.N, :], c.HP[0][c.d.N:, :], scores=True)


def gather_sources(nc, c, l):
    d, S = c.d, Signals(nc, f"src{l}")
    H = 4 if l == 5 else 1
    with ExitStack() as st:
        g = Gather(st, nc, c, S, c.TW[l])
        block = st.enter_context(nc.Block())

        @block.gpsimd
        def _(pool):
            g.rows(pool, c.HP[l], c.idxS)

        @block.scalar
        def _(act):
            g.each(act, lambda m, j: act.activation(chunk(c.G, m, MAC).rearrange("p (k f) -> p k f", k=K4),
                                                    g.ring[j][:, :, 0:D], ACT.Copy).then_inc(S("g_copied"), 1))

        @block.vector
        def _(v):
            def use(m, j):
                v.tensor_copy(chunk(c.SS, m, K4 * H).rearrange("p (k h) -> p k h", h=H),
                              g.ring[j][:, :, D:D + H]).then_inc(S("s_copied"), 1)
                v.wait_ge(S("s_copied"), m + 1)
                v.wait_ge(S("g_copied"), m + 1)
                v.sem_inc(S("ring_free"), 1)
            g.each(v, use)
    S.end()


def attention(nc, c, l):
    d, S = c.d, Signals(nc, f"att{l}")
    H = 4 if l == 5 else 1
    q = d.QP
    with ExitStack() as st:
        def sb(name):
            return st.enter_context(nc.sbuf_tensor(f"{S.tag}_{name}", [P, H, 256], F32))
        s, sf, u, y, z = sb("s"), sb("sf"), sb("u"), sb("y"), sb("z")
        runs = Runs(st, nc, c, S)
        psS, psD, psL = (st.enter_context(nc.psum_tensor(f"{S.tag}_ps{n}", [P, H * 2, P], F32)) for n in "SDL")
        if H == 1:
            pad = st.enter_context(nc.psum_tensor(f"{S.tag}_pad", [P, 2, P], F32))
        block = st.enter_context(nc.Block())

        def rowsv(p):
            return p[0:q].rearrange("q (h j) e -> q h (j e)", h=H)

        def heads(t):
            return t[0:q].unsqueeze(1).broadcast_to([q, H, 256])

        def cols(t):
            return t[:, 0:d.ET * H].rearrange("p (t h) -> p t h", h=H)

        @block.tensor
        def _(pe):
            for ps, t in ((psD, c.SD), (psS, c.SS), (psL, c.SL)):
                for h in range(H):
                    for j in range(2):
                        last = pe.transpose(ps[0:q, h * 2 + j, :], cols(t)[:, j::2, h], c.ident[:])
                last.then_inc(S("turned"), 1)
            runs.tensor(pe, "d_all", "spread", H, z)
            runs.tensor(pe, "m", "max", H, y)
            runs.tensor(pe, "m_all", "spread", H, z)
            runs.tensor(pe, "den", "sum", H, y)
            runs.tensor(pe, "den_all", "spread", H, z)
            for ps, t in ((psS, s), (psD, sf)):
                pe.wait_ge(S("weights"), 1)
                for h in range(H):
                    for j in range(2):
                        last = pe.transpose(ps[:, h * 2 + j, 0:q], t[0:q, h, j * P:(j + 1) * P], c.ident[0:q, 0:q])
                last.then_inc(S("turned_back"), 1)

        @block.scalar
        def _(act):
            act.wait_ge(S("s_less"), 1)
            act.activation(s[0:q], s[0:q], ACT.Exp).then_inc(S("exp"), 1)
            act.wait_ge(S("sf_less"), 1)
            act.activation(sf[0:q], sf[0:q], ACT.Exp).then_inc(S("exp"), 1)

        @block.vector
        def _(v):
            n = [0]

            def then(ins):
                n[0] += 1
                ins.then_inc(S("step"), 1)
                v.wait_ge(S("step"), n[0])

            runs.start(v)
            v.wait_ge(S("turned"), 3)
            then(v.tensor_tensor(u[0:q], rowsv(psD), heads(c.last), ALU.mult))
            runs.vector(v, "d_all", "spread", H, z, u)
            then(v.tensor_tensor(s[0:q], z[0:q], rowsv(psS), ALU.add))
            then(v.tensor_tensor(sf[0:q], rowsv(psL), heads(c.negLast), ALU.add))
            then(v.tensor_tensor(sf[0:q], sf[0:q], rowsv(psD), ALU.add))
            if H == 1:
                then(v.tensor_tensor(s[0:q, 0, :], s[0:q, 0, :], c.EL[0:q, l, :], ALU.add))
                then(v.tensor_tensor(sf[0:q, 0, :], sf[0:q, 0, :], c.loopEL[0:q, l, :], ALU.add))
            for t in (s, sf):
                then(v.scalar_tensor_tensor(out=t[0:q], in0=t[0:q], scalar=0.2, in1=t[0:q], op0=ALU.mult, op1=ALU.max))
            then(v.tensor_tensor(u[0:q], s[0:q], sf[0:q], ALU.max))
            runs.vector(v, "m", "max", H, y, u)
            then(v.tensor_tensor(u[0:q], y[0:q], heads(c.last), ALU.mult))
            runs.vector(v, "m_all", "spread", H, z, u)
            v.tensor_tensor(s[0:q], s[0:q], z[0:q], ALU.subtract).then_inc(S("s_less"), 1)
            v.tensor_tensor(sf[0:q], sf[0:q], z[0:q], ALU.subtract).then_inc(S("sf_less"), 1)
            v.wait_ge(S("exp"), 2)
            then(v.tensor_tensor(u[0:q], s[0:q], sf[0:q], ALU.add))
            runs.vector(v, "den", "sum", H, y, u)
            then(v.tensor_tensor(u[0:q], y[0:q], heads(c.last), ALU.mult))
            runs.vector(v, "den_all", "spread", H, z, u)
            then(v.reciprocal(u[0:q], z[0:q]))
            v.tensor_tensor(s[0:q], s[0:q], u[0:q], ALU.mult)
            v.tensor_tensor(sf[0:q], sf[0:q], u[0:q], ALU.mult).then_inc(S("weights"), 1)
            v.wait_ge(S("turned_back"), 2)
            for ps, t in ((psS, c.AL), (psD, c.AF)):
                for h in range(H):
                    for j in range(2):
                        v.tensor_copy(cols(t)[:, j::2, h], ps[:, h * 2 + j, 0:q])
    S.end()


def gat_messages(nc, c, l):
    d, S = c.d, Signals(nc, f"msg{l}")
    H = 4 if l == 5 else 1
    TW = c.TW[l]
    with ExitStack() as st:
        def two(name, shape, dt=F32):
            return [st.enter_context(nc.sbuf_tensor(f"{S.tag}_{name}{i}", shape, dt)) for i in range(2)]

        def bank(name, shape):
            return [st.enter_context(nc.psum_tensor(f"{S.tag}_{name}{i}", shape, F32)) for i in range(2)]
        sf, hd, s32 = two("sf", [P, 2 * MAC], U8), two("hd", [P, K4, TW]), two("s32", [P, MAC])
        gw, hw, agg = two("gw", [P, MAC]), two("hw", [P, MAC]), two("agg", [P, MAC])
        extra = two("extra", [P, MAC])
        mix, z = two("mix", [P, MAC]), two("z", [P, MAC])
        hT = hw if l == 4 else z
        rows = two("rows", [P, K4, D + 8])
        ix = two("ix", [P, K4], I32)
        scrap = two("scrap", [P, 1])
        psA, psM, psR = bank("psA", [P, MAC]), bank("psM", [P, MAC]), bank("psR", [P, K4, 256])
        ln = Norm(st, nc, S, "ln", 2) if l == 4 else None
        block = st.enter_context(nc.Block())
        NW = 0 if l == 5 else (c.TW[l + 1])
        W_next = None if l == 5 else (c.W5[:] if l == 4 else c.W0[:, l + 1, :])
        used = "x0" if l == 0 else "mixed" if l < 4 else "x_sum"
        n_in = 48 if l else 32

        def k4(t):
            return t[:].rearrange("p (k f) -> p k f", k=K4)

        @block.sync
        def _(sp):
            def load(m, pars):
                for b in pars:
                    g = m + b
                    sp.wait_ge(S(used), g + 1)
                    sp.sem_inc(S("sp_pass"), 1)
                    sp.dma_start(sf[b][:], chunk(c.SF, g, 2 * MAC)).then_inc(S(f"in{b}"), 16)
                    sp.dma_start(hd[b][:], edge_rows(c.HP[l][d.N:, :], g)).then_inc(S(f"in{b}"), 16)
                    if 1 <= l <= 3:
                        sp.dma_start(extra[b][:], chunk(c.X0T, g, MAC)).then_inc(S(f"in{b}"), 16)
                    if l >= 4:
                        sp.dma_start(k4(extra[b]), edge_rows(c.XD, g)).then_inc(S(f"in{b}"), 16)
            pairs(sp, d.EM, load)

        def loaded(eng, g, b):
            eng.wait_ge(S(f"in{b}"), (g - b) * (n_in // 2) + n_in)

        @block.gpsimd
        def _(pool):
            def body(m, pars):
                for b in pars:
                    g = m + b
                    pool.wait_ge(S("msg"), g + 1)
                    pool.tensor_tensor(gw[b][:].rearrange("p (a f) -> p a f", f=D // H),
                                       chunk(c.G, g, MAC).rearrange("p (a f) -> p a f", f=D // H),
                                       chunk(c.AL, g, K4 * H).unsqueeze(2).broadcast_to([P, K4 * H, D // H]),
                                       ALU.mult).then_inc(S("gw"), 1)
                if l == 5:
                    for b in pars:
                        g = m + b
                        pool.wait_ge(S("x_sum"), g + 3)
                        pool.wait_ge(S(f"put{b}"), (g - b) * 32 + 16)
                        pool.sem_inc(S("pool_pass"), 1)
                        pool.tensor_copy(ix[b][:], chunk(c.canonI, g, K4)).then_inc(S("ix"), 1)
                        pool.wait_ge(S("ix"), g + 1)
                        pool.sem_inc(S("pool_pass"), 1)
                        for k in range(K4):
                            pool.indirect_dma_start(out=c.X2, out_offset=bass.IndirectOffsetOnAxis(ap=ix[b][:, k:k + 1], axis=0),
                                                    in_=mix[b][:, k * P:(k + 1) * P], in_offset=None, bounds_check=d.N - 1,
                                                    oob_is_err=False).then_inc(S(f"put{b}"), 16)
            if l == 5:
                for b in range(2):
                    pool.dma_start(scrap[b][:], c.ident[:, 0:1]).then_inc(S(f"put{b}"), 16)
            pairs(pool, d.EM, body)
            if l == 5:
                for b in range(2):
                    pool.wait_ge(S(f"put{b}"), 16 + 64 * ((d.EM + 1 - b) // 2))

        @block.vector
        def _(v):
            v.sem_inc(S(used), 2)
            v.sem_inc(S("cols"), 2)
            v.memset(agg[1][:, MAC - 1:MAC], 0.0).then_inc(S("agg3"), 1)

            def body(m, pars):
                for b in pars:
                    g = m + b
                    loaded(v, g, b)
                    v.wait_ge(S("msg"), g + 1)
                    v.tensor_tensor(hw[b][:].rearrange("p (a f) -> p a f", f=D // H),
                                    hd[b][:, :, 0:D].rearrange("p k (h f) -> p k h f", h=H) if H > 1 else hd[b][:, :, 0:D],
                                    chunk(c.AF, g, K4 * H).unsqueeze(2).broadcast_to([P, K4 * H, D // H]),
                                    ALU.mult).then_inc(S("hw"), 1)
                for b in pars:
                    g = m + b
                    v.wait_ge(S("msg"), g + 3)
                    for k in range(K4):
                        v.wait_ge(S(f"agg{(k - 1) % 4}"), g + 1)
                        before = agg[b][:, k * P - 1:k * P] if k else agg[1 - b][:, MAC - 1:MAC]
                        v.scalar_tensor_tensor(out=agg[b][:, k * P:(k + 1) * P], in0=sf[b][:, MAC + k * P:MAC + (k + 1) * P],
                                               scalar=before, in1=psA[b][:, k * P:(k + 1) * P],
                                               op0=ALU.mult, op1=ALU.add).then_inc(S(f"agg{k}"), 1)
                for b in pars:
                    g = m + b
                    if l == 0:
                        v.wait_ge(S("agg3"), g + 2)
                        v.tensor_scalar(hT[b][:], agg[b][:], c.b0col[:], None, ALU.add).then_inc(S("x0"), 1)
                        v.wait_ge(S("x0"), g + 3)
                        v.wait_ge(S(f"x0_out{b}"), (g - b) * 8 + 16)
                        v.tensor_scalar(mix[b][:], hT[b][:], ALPHA, None, ALU.mult).then_inc(S("x0s"), 1)
                    elif l < 4:
                        v.wait_ge(S("agg3"), g + 2)
                        v.scalar_tensor_tensor(out=mix[b][:], in0=agg[b][:], scalar=1.0 - ALPHA, in1=extra[b][:],
                                               op0=ALU.mult, op1=ALU.add).then_inc(S("mixed"), 1)
                    else:
                        v.wait_ge(S("turned"), g + 1)
                        bias = c.b4row if l == 4 else c.b5row
                        if l == 4:
                            v.wait_ge(S(f"x_out{b}"), (g - b) * 8 + 16)
                        else:
                            v.wait_ge(S(f"put{b}"), (g - b) * 32 + 16)
                        v.tensor_tensor(k4(mix[b]), k4(psM[b]), bias[:].unsqueeze(1).broadcast_to([P, K4, D]), ALU.add).then_inc(S("x_bias"), 1)
                        v.wait_ge(S("x_bias"), g + 1)
                        v.tensor_tensor(mix[b][:], mix[b][:], extra[b][:], ALU.add).then_inc(S("x_sum"), 1)
                if 1 <= l <= 3:
                    for b in pars:
                        g = m + b
                        v.wait_ge(S("z"), g + 1)
                        v.scalar_tensor_tensor(out=hT[b][:], in0=z[b][:], scalar=0.01, in1=z[b][:],
                                               op0=ALU.mult, op1=ALU.max).then_inc(S("hT"), 1)
                if l == 4:
                    for b in pars:
                        v.wait_ge(S("x_sum"), m + b + 3)
                    ln.vector(v, [(m + b, b) for b in pars], [k4(t) for t in mix])
                    for b in pars:
                        g = m + b
                        v.wait_ge(S("projected"), g + 1)
                        v.wait_ge(S(f"rows_out{b}"), (g - b) * 8 + 16)
                        v.tensor_tensor(rows[b][:], psR[b][:, :, 0:D + 8], c.blin[:].unsqueeze(1).broadcast_to([P, K4, D + 8]),
                                        ALU.add).then_inc(S("rows"), 1)
                if l < 5:
                    HN = 4 if l == 4 else 1
                    for b in pars:
                        g = m + b
                        v.wait_ge(S("rows"), g + 1)
                        v.tensor_copy(chunk(c.SL, g, K4 * HN).rearrange("p (k h) -> p k h", h=HN), rows[b][:, :, D:D + HN])
                        v.tensor_copy(chunk(c.SD, g, K4 * HN).rearrange("p (k h) -> p k h", h=HN),
                                      rows[b][:, :, D + HN:D + 2 * HN]).then_inc(S("cols"), 1)
            pairs(v, d.EM, body)

        @block.scalar
        def _(act):
            for b in range(2):
                for name in (["x0_out"] if l == 0 else ["x_out"] if l == 4 else []) + (["rows_out"] if l < 5 else []):
                    act.dma_start(scrap[b][:], c.ident[:, 0:1]).then_inc(S(f"{name}{b}"), 16)
                    act.wait_ge(S(f"{name}{b}"), 16)

            def body(m, pars):
                for b in pars:
                    g = m + b
                    loaded(act, g, b)
                    act.wait_ge(S("msg"), g + 1)
                    act.activation(s32[b][:], sf[b][:, 0:MAC], ACT.Copy).then_inc(S("s32"), 1)
                if l == 0:
                    for b in pars:
                        g = m + b
                        act.wait_ge(S("x0s"), g + 1)
                        act.dma_start(chunk(c.X0T, g, MAC), mix[b][:]).then_inc(S(f"x0_out{b}"), 16)
                if 1 <= l <= 3:
                    for b in pars:
                        g = m + b
                        act.wait_ge(S("mid"), g + 1)
                        act.activation(z[b][:], psM[b][:], ACT.Identity, bias=c.bm[:, l - 1:l]).then_inc(S("z"), 1)
                if l == 4:
                    for b in pars:
                        g = m + b
                        act.wait_ge(S("x_sum"), g + 3)
                        act.dma_start(edge_rows(c.XD, g), k4(mix[b])).then_inc(S(f"x_out{b}"), 16)
                    for b in pars:
                        ln.root(act, b, m + b)
                    for b in pars:
                        ln.apply(act, b, m + b, k4(z[b]), k4(mix[b]), S("r"))
                    for b in pars:
                        g = m + b
                        act.wait_ge(S("rT_ps"), g + 1)
                        act.activation(hT[b][:], psA[b][:], ACT.Copy).then_inc(S("hT"), 1)
                if l < 4:
                    for b in pars:
                        g = m + b
                        act.wait_ge(S("projected"), g + 1)
                        act.wait_ge(S("cols"), g + 1)
                        act.wait_ge(S(f"rows_out{b}"), (g - b) * 8 + 16)
                        act.activation(rows[b][:, :, 0:NW], psR[b][:, :, 0:NW], ACT.Copy).then_inc(S("rows"), 1)
                if l < 5:
                    for b in pars:
                        g = m + b
                        act.wait_ge(S("rows"), g + 1)
                        act.dma_start(edge_rows(c.HP[l + 1][d.N:, :], g), rows[b][:, :, 0:NW]).then_inc(S(f"rows_out{b}"), 16)
            pairs(act, d.EM, body)
            for b in range(2):
                for name in (["x0_out"] if l == 0 else ["x_out"] if l == 4 else []) + (["rows_out"] if l < 5 else []):
                    act.wait_ge(S(f"{name}{b}"), 16 + 16 * ((d.EM + 1 - b) // 2))

        @block.tensor
        def _(pe):
            pe.sem_inc(S("msg"), 2)

            def body(m, pars):
                for b in pars:
                    g = m + b
                    pe.wait_ge(S("gw"), g + 1)
                    pe.wait_ge(S("hw"), g + 1)
                    pe.wait_ge(S("s32"), g + 1)
                    if l == 4:
                        pe.wait_ge(S("agg3"), g + 1)
                    for k in range(K4):
                        col = slice(k * P, (k + 1) * P)
                        pe.matmul(psA[b][:, col], gw[b][:, col], s32[b][:, col], start=True, stop=False)
                        last = pe.matmul(psA[b][:, col], hw[b][:, col], c.ident[:], start=False, stop=True)
                    last.then_inc(S("msg"), 1)
                if l == 0:
                    ready, base = "x0", 3
                elif l < 4:
                    for b in pars:
                        g = m + b
                        pe.wait_ge(S("mixed"), g + 3)
                        pe.matmul(psM[b][:], c.M[:, l - 1, :], mix[b][:], start=True, stop=True).then_inc(S("mid"), 1)
                    ready, base = "hT", 1
                else:
                    for b in pars:
                        g = m + b
                        pe.wait_ge(S("agg3"), g + 2)
                        turn_back(pe, k4(psM[b]), agg[b], c.ident[:], S("turned"))
                    if l == 4:
                        for b in pars:
                            g = m + b
                            pe.wait_ge(S("r"), g + 1)
                            turn(pe, psA[b], k4(z[b]), c.ident[:], S("rT_ps"))
                    ready, base = "hT", 1
                if l < 5:
                    for b in pars:
                        g = m + b
                        pe.wait_ge(S(ready), g + base)
                        rows_of(pe, psR[b], hT[b], W_next, S("projected"))
            pairs(pe, d.EM, body)
    S.end()


def sum_by_source(nc, c):
    d, S = c.d, Signals(nc, "bysrc")
    with ExitStack() as st:
        def two(name, shape, dt=F32):
            return [st.enter_context(nc.sbuf_tensor(f"{S.tag}_{name}{i}", shape, dt)) for i in range(2)]
        x, r, rows = two("x", [P, K4, D]), two("r", [P, K4, D]), two("rows", [P, K4, D])
        sbc, same = two("sbc", [P, MAC]), two("same", [P, MAC])
        gix, pix = two("gix", [P, K4], I32), two("pix", [P, K4], I32)
        scrap = two("scrap", [P, 1])
        ln = Norm(st, nc, S, "ln", 2)
        ps = [st.enter_context(nc.psum_tensor(f"{S.tag}_ps{i}", [P, K4, D], F32)) for i in range(2)]
        block = st.enter_context(nc.Block())

        @block.gpsimd
        def _(pool):
            def gathers(g, b):
                pool.wait_ge(S("r"), g + 1)
                pool.sem_inc(S("pool_pass"), 1)
                pool.tensor_copy(gix[b][:], chunk(c.idxD, g, K4)).then_inc(S("gix"), 1)
                pool.wait_ge(S("gix"), g + 1)
                pool.sem_inc(S("pool_pass"), 1)
                for k in range(K4):
                    pool.indirect_dma_start(out=x[b][:, k, :], out_offset=None, in_=c.X2,
                                            in_offset=bass.IndirectOffsetOnAxis(ap=gix[b][:, k:k + 1], axis=0)
                                            ).then_inc(S(f"slot{b}"), 16)

            def adds(g, b):
                pool.wait_ge(S("summed"), g + 1)
                pool.wait_ge(S("put"), g * 64 + 16)
                pool.sem_inc(S("pool_pass"), 1)
                pool.tensor_copy(pix[b][:], chunk(c.accI, g, K4)).then_inc(S("pix"), 1)
                pool.wait_ge(S("pix"), g + 1)
                for k in range(K4):
                    pool.wait_ge(S("put"), g * 64 + k * 16 + 16)
                    pool.sem_inc(S("pool_pass"), 1)
                    pool.indirect_dma_start(out=c.NS, out_offset=bass.IndirectOffsetOnAxis(ap=pix[b][:, k:k + 1], axis=0),
                                            in_=rows[b][:, k, :], in_offset=None, bounds_check=d.NP + P - 1,
                                            oob_is_err=True, compute_op=ALU.add).then_inc(S("put"), 16)
            pool.dma_start(scrap[0][:], c.ident[:, 0:1]).then_inc(S("put"), 16)
            gathers(0, 0)
            with pool.Fori(0, d.EM // 2) as i:
                for b in range(2):
                    gathers(i * 2 + b + 1, 1 - b)
                    adds(i * 2 + b, b)
            adds(d.EM - 1, 0)
            pool.wait_ge(S("put"), d.EM * 64 + 16)

        @block.sync
        def _(sp):
            def body(m, pars):
                for b in pars:
                    g = m + b
                    sp.wait_ge(S("same"), g + 1)
                    sp.sem_inc(S("sp_pass"), 1)
                    sp.dma_start(sbc[b][:], chunk(c.srcRow.rearrange("(a e) -> a e", a=1), g, MAC).broadcast_to([P, MAC])).then_inc(S(f"s_in{b}"), 16)
            pairs(sp, d.EM, body)

        @block.vector
        def _(v):
            v.sem_inc(S("same"), 2)

            def body(m, pars):
                for b in pars:
                    g = m + b
                    v.wait_ge(S(f"s_in{b}"), (g - b) * 8 + 16)
                    v.wait_ge(S("summing"), g + 1)
                    for k in range(K4):
                        col = slice(k * P, (k + 1) * P)
                        last = v.tensor_scalar(same[b][:, col], sbc[b][:, col], c.srcF[:, bass.ds(g * 4 + k, 1)], None, ALU.is_equal)
                    last.then_inc(S("same"), 1)
                for b in pars:
                    v.wait_ge(S(f"slot{b}"), m * 32 + 64)
                ln.vector(v, [(m + b, b) for b in pars], x)
            pairs(v, d.EM, body)

        @block.scalar
        def _(act):
            act.sem_inc(S("r"), 2)

            def body(m, pars):
                for b in pars:
                    ln.root(act, b, m + b)
                for b in pars:
                    act.wait_ge(S("summing"), m + b + 1)
                    ln.apply(act, b, m + b, r[b], x[b], S("r"))
                for b in pars:
                    g = m + b
                    act.wait_ge(S("summing"), g + 3)
                    act.wait_ge(S("rows_free"), g + 1)
                    act.activation(rows[b][:], ps[b][:], ACT.Copy).then_inc(S("summed"), 1)
            pairs(act, d.EM, body)

        @block.tensor
        def _(pe):
            pe.sem_inc(S("summing"), 2)
            pe.sem_inc(S("rows_free"), 2)

            def body(m, pars):
                for b in pars:
                    g = m + b
                    pe.wait_ge(S("r"), g + 3)
                    pe.wait_ge(S("same"), g + 3)
                    pe.wait_ge(S("ps_free"), g + 1)
                    for k in range(K4):
                        last = pe.matmul(ps[b][:, k, :], same[b][:, k * P:(k + 1) * P], r[b][:, k, :], start=True, stop=True)
                    last.then_inc(S("summing"), 1)
                for b in pars:
                    g = m + b
                    pe.wait_ge(S("summed"), g + 1)
                    pe.sem_inc(S("ps_free"), 1)
                    pe.wait_ge(S("put"), g * 64 + 80)
                    pe.sem_inc(S("rows_free"), 1)
            pe.sem_inc(S("ps_free"), 2)
            pairs(pe, d.EM, body)
    S.end()


def nodes_sage(nc, c, out):
    d, S = c.d, Signals(nc, "sagen")
    N, NM = d.N, d.NM
    with ExitStack() as st:
        def two(name, shape, dt=F32):
            return [st.enter_context(nc.sbuf_tensor(f"{S.tag}_{name}{i}", shape, dt)) for i in range(2)]
        xin, xk, ns, r, th = two("xin", [P, K4, D]), two("xk", [P, K4, D]), two("ns", [P, K4, D]), two("r", [P, K4, D]), two("th", [P, K4, D])
        nsT, rT, nb = two("nsT", [P, MAC]), two("rT", [P, MAC]), two("nb", [P, K4, D])
        xa, x3, r3, fa, fin = (two(n, [P, K4, D]) for n in ("xa", "x3", "r3", "fa", "fin"))
        hT = [[two(f"h{s}T{o}", [P, MAC]) for o in range(2)] for s in range(2)]
        hrow = [two(f"h{s}row", [P, K4, 2 * D]) for s in range(2)]
        ln0, ln1 = Norm(st, nc, S, "ln0", 2), Norm(st, nc, S, "ln1", 2)

        def bank(name):
            return [st.enter_context(nc.psum_tensor(f"{S.tag}_{name}{i}", [P, MAC], F32)) for i in range(2)]
        psT, psW, psO = bank("psT"), bank("psW"), [bank("psOa"), bank("psOb")]
        block = st.enter_context(nc.Block())

        def k4(t):
            return t[:].rearrange("p (k f) -> p k f", k=K4)

        def macros(eng, body):
            if NM // 2 - 1:
                with eng.Fori(0, NM // 2 - 1) as i:
                    body(i * 2, ((i * 2, 0), (i * 2 + 1, 1)))
            body(NM - 2, ((NM - 2, 0), (NM - 1, 1)))

        @block.gpsimd
        def _(pool):
            pool.sem_inc(S("xin_free"), 2)

            def body(m, gb):
                for g, b in gb:
                    pool.wait_ge(S("xin_free"), g + 1)
                    pool.wait_ge(S("ns_turned"), g + 1)
                    pool.sem_inc(S("pool_pass"), 1)
                    pool.dma_start(xin[b][:], node_rows(c.X2, g, N)).then_inc(S(f"x_in{b}"), 16)
                    pool.dma_start(ns[b][:], node_rows(c.NS[0:N, :], g, N)).then_inc(S(f"soft_ns{b}"), 16)
                for g, b in gb:
                    pool.wait_ge(S("r"), g + 1)
                    pool.wait_ge(S("xk_used"), g + 1)
                    pool.sem_inc(S("pool_pass"), 1)
                    pool.tensor_copy(xk[b][:], xin[b][:]).then_inc(S("xk"), 1)
                    pool.wait_ge(S("xk"), g + 1)
                    pool.sem_inc(S("xin_free"), 1)
            macros(pool, body)

        @block.sync
        def _(sp):
            def body(m, gb):
                n = 0
                for ready, buf, table in (("x3", x3, c.X3), ("r3", r3, c.R3[0:N, :]), ("h0row", hrow[0], c.H[0][0:N, :]),
                                          ("h1row", hrow[1], c.H[1][0:N, :]), ("fin", fin, out)):
                    n += 1
                    for g, b in gb:
                        sp.wait_ge(S(ready), g + 1)
                        if isinstance(g, int) and g == NM - 1:
                            sp.wait_ge(S("st0"), ((NM - 1) // 2) * 80 + 16 * n)
                        sp.sem_inc(S("sp_pass"), 1)
                        sp.dma_start(node_rows(table, g, N), buf[b][:]).then_inc(S(f"st{b}"), 16)
                for g, b in gb:
                    sp.wait_ge(S(f"st{b}"), (g - b) * 40 + 80)
                    sp.sem_inc(S("rows_free"), 1)
            macros(sp, body)

        @block.vector
        def _(v):
            v.sem_inc(S("xk_used"), 2)
            v.sem_inc(S("ps_free"), 2)

            def body(m, gb):
                for g, b in gb:
                    v.wait_ge(S(f"x_in{b}"), (g - b) * 8 + 16)
                ln0.vector(v, gb, xin)
                for g, b in gb:
                    v.wait_ge(S("nbr"), g + 1)
                    v.tensor_tensor(nb[b][:], k4(psO[1][b]), c.b2nrow[:].unsqueeze(1).broadcast_to([P, K4, D]), ALU.add).then_inc(S("nb"), 1)
                for g, b in gb:
                    v.wait_ge(S("self"), g + 1)
                    v.wait_ge(S("xk"), g + 1)
                    v.tensor_tensor(xa[b][:], k4(psO[0][b]), xk[b][:], ALU.add).then_inc(S("xk_used"), 1)
                for g, b in gb:
                    v.wait_ge(S("xk_used"), g + 3)
                    v.wait_ge(S("th"), g + 1)
                    v.wait_ge(S("rows_free"), g + 1)
                    v.tensor_tensor(x3[b][:], xa[b][:], th[b][:], ALU.add).then_inc(S("x3"), 1)
                for g, b in gb:
                    v.wait_ge(S("x3"), g + 1)
                ln1.vector(v, gb, x3)
                for s in range(2):
                    for g, b in gb:
                        v.wait_ge(S(f"back{s}"), g + 1)
                        v.tensor_copy(hrow[s][b][:, :, 0:D], k4(psT[b]))
                        v.tensor_copy(hrow[s][b][:, :, D:2 * D], k4(psW[b])).then_inc(S(f"h{s}row"), 1)
                for g, b in gb:
                    v.wait_ge(S("last"), g + 1)
                    v.tensor_tensor(fa[b][:], k4(psO[0][b]), c.b3row[:].unsqueeze(1).broadcast_to([P, K4, D]), ALU.add).then_inc(S("ps_free"), 1)
                for g, b in gb:
                    v.wait_ge(S("ps_free"), g + 3)
                    v.scalar_tensor_tensor(out=fin[b][:], in0=fa[b][:], scalar=0.0, in1=x3[b][:],
                                           op0=ALU.max, op1=ALU.add).then_inc(S("fin"), 1)
            macros(v, body)

        @block.scalar
        def _(act):
            act.sem_inc(S("rows_free"), 2)

            def copies(gb, out_, src, ready, done):
                for g, b in gb:
                    act.wait_ge(S(ready), g + 1)
                    act.activation(out_[b][:], src[b][:], ACT.Copy).then_inc(S(done), 1)

            def body(m, gb):
                for g, b in gb:
                    act.wait_ge(S("ns_turned"), g + 3)
                    act.activation(nsT[b][:], psT[b][:], ACT.Copy).then_inc(S("nsT"), 1)
                for g, b in gb:
                    ln0.root(act, b, g)
                for g, b in gb:
                    ln0.apply(act, b, g, r[b], xin[b], S("r"))
                copies(gb, rT, psT, "rTp", "rT")
                for g, b in gb:
                    act.wait_ge(S("nb"), g + 1)
                    act.activation(th[b][:], nb[b][:], ACT.Tanh).then_inc(S("th"), 1)
                for g, b in gb:
                    ln1.root(act, b, g)
                for g, b in gb:
                    act.wait_ge(S("rows_free"), g + 1)
                    ln1.apply(act, b, g, r3[b], x3[b], S("r3"))
                copies(gb, rT, psT, "r3Tp", "r3T")
                for s in range(2):
                    for o in range(2):
                        for g, b in gb:
                            act.wait_ge(S(f"hid{s}{o}"), g + 1)
                            act.activation(hT[s][o][b][:], psO[o][b][:], ACT.Relu, bias=c.bcol[s][:, o:o + 1]).then_inc(S(f"relu{s}{o}"), 1)
            macros(act, body)

        @block.tensor
        def _(pe):
            pe.sem_inc(S("ns_turned"), 2)

            def body(m, gb):
                for g, b in gb:
                    pe.wait_ge(S(f"soft_ns{b}"), (g - b) * 8 + 16)
                    pe.wait_ge(S("ps_free"), g + 1)
                    turn(pe, psT[b], ns[b], c.ident[:], S("ns_turned"))
                for g, b in gb:
                    pe.wait_ge(S("nsT"), g + 1)
                    rows_of(pe, k4(psO[1][b]), nsT[b], c.W2n[:], S("nbr"))
                for g, b in gb:
                    pe.wait_ge(S("r"), g + 1)
                    turn(pe, psT[b], r[b], c.ident[:], S("rTp"))
                for g, b in gb:
                    pe.wait_ge(S("rT"), g + 1)
                    rows_of(pe, k4(psO[0][b]), rT[b], c.W2s[:], S("self"))
                for g, b in gb:
                    pe.wait_ge(S("r3"), g + 1)
                    turn(pe, psT[b], r3[b], c.ident[:], S("r3Tp"))
                for g, b in gb:
                    pe.wait_ge(S("r3T"), g + 1)
                    for o in range(2):
                        pe.matmul(psO[o][b][:], c.Ws[0][:, 0, o * P:(o + 1) * P], rT[b][:], start=True, stop=True).then_inc(S(f"hid0{o}"), 1)
                for s in range(2):
                    for g, b in gb:
                        pe.wait_ge(S(f"relu{s}0"), g + 1)
                        pe.wait_ge(S(f"relu{s}1"), g + 1)
                        if s:
                            pe.wait_ge(S("h0row"), g + 1)
                        for o, ps in ((0, psT), (1, psW)):
                            for k in range(K4):
                                last = pe.transpose(k4(ps[b])[:, k, :], hT[s][o][b][:, k * P:(k + 1) * P], c.ident[:])
                        last.then_inc(S(f"back{s}"), 1)
                    for g, b in gb:
                        if s == 0:
                            for o in range(2):
                                for f in range(2):
                                    last = pe.matmul(psO[o][b][:], c.Ws[1][:, f, o * P:(o + 1) * P], hT[0][f][b][:], start=(f == 0), stop=(f == 1))
                                last.then_inc(S(f"hid1{o}"), 1)
                        else:
                            for k in range(K4):
                                for f in range(2):
                                    last = pe.matmul(k4(psO[0][b])[:, k, :], hT[1][f][b][:, k * P:(k + 1) * P], c.Ws[2][:, f, :],
                                                     start=(f == 0), stop=(f == 1))
                            last.then_inc(S("last"), 1)
            macros(pe, body)
    S.end()


def sage_edges(nc, c, s, out):
    d, S = c.d, Signals(nc, f"sage{s}")
    FI, FO = (1, 2, 2)[s], (2, 2, 1)[s]
    table = (c.R3, c.H[0], c.H[1])[s]
    with ExitStack() as st:
        def two(name, shape, dt=F32):
            return [st.enter_context(nc.sbuf_tensor(f"{S.tag}_{name}{i}", shape, dt)) for i in range(2)]

        def bank(name):
            return [st.enter_context(nc.psum_tensor(f"{S.tag}_{name}{i}", [P, MAC], F32)) for i in range(2)]
        ring, gw = two("ring", [P, K4, FI * D]), two("gw", [P, K4, FI * D])
        gix, six = two("gix", [P, K4], I32), two("six", [P, K4], I32)
        sf, s32 = two("sf", [P, 2 * MAC], U8), two("s32", [P, MAC])
        agg = [two(f"agg{f}_", [P, MAC]) for f in range(FI)]
        own = [two(f"own{f}_", [P, MAC]) for f in range(FI)]
        hd, xd = two("hd", [P, K4, D]), two("xd", [P, K4, D])
        new = [two(f"new{o}_", [P, MAC]) for o in range(FO)]
        rows = two("rows", [P, K4, FO * D])
        scrap = two("scrap", [P, 1])
        psA, psO = [bank("psA0"), bank("psA1")], [bank("psO0"), bank("psO1")]
        block = st.enter_context(nc.Block())
        n_in = 16 * (2 if s == 0 else 3 if s == 1 else 4)
        stores = [f"new_out{o}_" for o in range(FO)] + ["rows_out"] if s < 2 else []

        def k4(t):
            return t[:].rearrange("p (k f) -> p k f", k=K4)

        @block.gpsimd
        def _(pool):
            def gathers(m, pars):
                for b in pars:
                    g = m + b
                    pool.wait_ge(S("gw"), g + 1)
                    pool.sem_inc(S("pool_pass"), 1)
                    pool.tensor_copy(gix[b][:], chunk(c.idxS, g, K4)).then_inc(S("gix"), 1)
                    pool.wait_ge(S("gix"), g + 1)
                    pool.sem_inc(S("pool_pass"), 1)
                    for k in range(K4):
                        pool.indirect_dma_start(out=ring[b][:, k, :], out_offset=None, in_=table,
                                                in_offset=bass.IndirectOffsetOnAxis(ap=gix[b][:, k:k + 1], axis=0)
                                                ).then_inc(S(f"slot{b}"), 16)

            def scatters(m, pars):
                for b in pars if s == 2 else ():
                    g = m + b
                    pool.wait_ge(S("result"), g + 1)
                    pool.wait_ge(S(f"put{b}"), (g - b) * 32 + 16)
                    pool.sem_inc(S("pool_pass"), 1)
                    pool.tensor_copy(six[b][:], chunk(c.canonI, g, K4)).then_inc(S("six"), 1)
                    pool.wait_ge(S("six"), g + 1)
                    pool.sem_inc(S("pool_pass"), 1)
                    for k in range(K4):
                        pool.indirect_dma_start(out=out, out_offset=bass.IndirectOffsetOnAxis(ap=six[b][:, k:k + 1], axis=0),
                                                in_=rows[b][:, k, :], in_offset=None, bounds_check=d.N - 1,
                                                oob_is_err=False).then_inc(S(f"put{b}"), 16)
            if s == 2:
                for b in range(2):
                    pool.dma_start(scrap[b][:], c.ident[:, 0:1]).then_inc(S(f"put{b}"), 16)
            gathers(0, (0, 1))
            if d.EM // 2 > 1:
                with pool.Fori(1, d.EM // 2) as i:
                    gathers(i * 2, (0, 1))
                    scatters(i * 2 - 2, (0, 1))
            gathers(d.EM - 1, (0,))
            scatters(d.EM - 3, (0, 1))
            scatters(d.EM - 1, (0,))
            if s == 2:
                for b in range(2):
                    pool.wait_ge(S(f"put{b}"), 16 + 64 * ((d.EM + 1 - b) // 2))

        @block.sync
        def _(sp):
            def load(m, pars):
                for b in pars:
                    g = m + b
                    sp.wait_ge(S("dense"), g + 1)
                    if s == 2:
                        sp.wait_ge(S("result2"), g + 1)
                    sp.sem_inc(S("sp_pass"), 1)
                    sp.dma_start(sf[b][:], chunk(c.SF, g, 2 * MAC)).then_inc(S(f"in{b}"), 16)
                    if s == 0:
                        sp.dma_start(hd[b][:], edge_rows(c.R3[d.N:, :], g)).then_inc(S(f"in{b}"), 16)
                    else:
                        for f in range(2):
                            sp.dma_start(own[f][b][:], chunk(c.HT[s - 1][f * P:(f + 1) * P, :], g, MAC)).then_inc(S(f"in{b}"), 16)
                    if s == 2:
                        sp.dma_start(xd[b][:], edge_rows(c.XD, g)).then_inc(S(f"in{b}"), 16)
            pairs(sp, d.EM, load)

        def loaded(eng, g, b):
            eng.wait_ge(S(f"in{b}"), (g - b) * (n_in // 2) + n_in)

        @block.vector
        def _(v):
            v.sem_inc(S("gw"), 2)
            for f in range(FI):
                last = v.memset(agg[f][1][:, MAC - 1:MAC], 0.0)
            last.then_inc(S("agg3"), 1)
            if s == 2:
                v.sem_inc(S("result2"), 2)

            def body(m, pars):
                for b in pars:
                    g = m + b
                    v.wait_ge(S(f"slot{b}"), (g - b) * 32 + 64)
                    v.wait_ge(S("sums"), g + 1)
                    v.tensor_tensor(gw[b][:], ring[b][:], chunk(c.invdeg, g, K4).unsqueeze(2).broadcast_to([P, K4, FI * D]),
                                    ALU.mult).then_inc(S("gw"), 1)
                for b in pars:
                    g = m + b
                    loaded(v, g, b)
                    v.wait_ge(S("sums"), g + 3)
                    for k in range(K4):
                        v.wait_ge(S(f"agg{(k - 1) % 4}"), g + 1)
                        for f in range(FI):
                            before = agg[f][b][:, k * P - 1:k * P] if k else agg[f][1 - b][:, MAC - 1:MAC]
                            last = v.scalar_tensor_tensor(out=agg[f][b][:, k * P:(k + 1) * P], in0=sf[b][:, MAC + k * P:MAC + (k + 1) * P],
                                                          scalar=before, in1=psA[f][b][:, k * P:(k + 1) * P], op0=ALU.mult, op1=ALU.add)
                        last.then_inc(S(f"agg{k}"), 1)
                for b in pars:
                    g = m + b
                    v.wait_ge(S("back"), g + 1)
                    if s < 2:
                        v.wait_ge(S(f"rows_out{b}"), (g - b) * 8 + 16)
                        for o in range(2):
                            last = v.tensor_copy(rows[b][:, :, o * D:(o + 1) * D], k4(psA[o][b]))
                        last.then_inc(S("rows"), 1)
                    else:
                        v.wait_ge(S(f"put{b}"), (g - b) * 32 + 16)
                        v.tensor_tensor(rows[b][:], k4(psA[0][b]), xd[b][:], ALU.add).then_inc(S("result"), 1)
                        v.wait_ge(S("result"), g + 1)
                        v.sem_inc(S("result2"), 1)
            pairs(v, d.EM, body)

        @block.scalar
        def _(act):
            for b in range(2):
                for name in stores:
                    act.dma_start(scrap[b][:], c.ident[:, 0:1]).then_inc(S(f"{name}{b}"), 16)
                    act.wait_ge(S(f"{name}{b}"), 16)

            def body(m, pars):
                for b in pars:
                    g = m + b
                    loaded(act, g, b)
                    act.wait_ge(S("sums"), g + 1)
                    act.activation(s32[b][:], sf[b][:, 0:MAC], ACT.Copy).then_inc(S("s32"), 1)
                if s == 0:
                    for b in pars:
                        g = m + b
                        act.wait_ge(S("own_turned"), g + 1)
                        act.activation(own[0][b][:], psA[1][b][:], ACT.Copy).then_inc(S("own"), 1)
                for b in pars:
                    g = m + b
                    act.wait_ge(S("dense"), g + 3)
                    for o in range(FO):
                        if s < 2:
                            act.wait_ge(S(f"new_out{o}_{b}"), (g - b) * 8 + 16)
                        act.activation(new[o][b][:], psO[o][b][:], ACT.Relu, bias=c.bcol[s][:, o:o + 1]).then_inc(S("new"), 1)
                if s < 2:
                    for b in pars:
                        g = m + b
                        act.wait_ge(S("new"), (g + 1) * FO)
                        for o in range(2):
                            act.dma_start(chunk(c.HT[s][o * P:(o + 1) * P, :], g, MAC), new[o][b][:]).then_inc(S(f"new_out{o}_{b}"), 16)
                    for b in pars:
                        g = m + b
                        act.wait_ge(S("rows"), g + 1)
                        act.dma_start(edge_rows(c.H[s][d.N:, :], g), rows[b][:]).then_inc(S(f"rows_out{b}"), 16)
            pairs(act, d.EM, body)
            for b in range(2):
                for name in stores:
                    act.wait_ge(S(f"{name}{b}"), 16 + 16 * ((d.EM + 1 - b) // 2))

        @block.tensor
        def _(pe):
            pe.sem_inc(S("sums"), 2)
            pe.sem_inc(S("dense"), 2)

            def body(m, pars):
                for b in pars:
                    g = m + b
                    pe.wait_ge(S("gw"), g + 3)
                    pe.wait_ge(S("s32"), g + 1)
                    pe.wait_ge(S("psA_free"), g + 1)
                    for f in range(FI):
                        for k in range(K4):
                            col = slice(k * P, (k + 1) * P)
                            last = pe.matmul(psA[f][b][:, col], gw[b][:, k, f * D:(f + 1) * D], s32[b][:, col], start=True, stop=True)
                    last.then_inc(S("sums"), 1)
                    if s == 0:
                        loaded(pe, g, b)
                        turn(pe, psA[1][b], hd[b], c.ident[:], S("own_turned"))
                for b in pars:
                    g = m + b
                    if s == 0:
                        pe.wait_ge(S("own"), g + 1)
                    else:
                        loaded(pe, g, b)
                    pe.wait_ge(S("agg3"), g + 2)
                    for o in range(FO):
                        for f in range(FI):
                            col = slice(o * P, (o + 1) * P)
                            pe.matmul(psO[o][b][:], c.Ws[s][:, f, col], own[f][b][:], start=(f == 0), stop=False)
                            last = pe.matmul(psO[o][b][:], c.Wn[s][:, f, col], agg[f][b][:], start=False, stop=(f == FI - 1))
                    last.then_inc(S("dense"), 1)
                for b in pars:
                    g = m + b
                    pe.wait_ge(S("new"), (g + 1) * FO)
                    for o in range(FO):
                        for k in range(K4):
                            last = pe.transpose(k4(psA[o][b])[:, k, :], new[o][b][:, k * P:(k + 1) * P], c.ident[:])
                    last.then_inc(S("back"), 1)
                for b in pars:
                    g = m + b
                    pe.wait_ge(S("rows" if s < 2 else "result"), g + 1)
                    pe.sem_inc(S("psA_free"), 1)
            pe.sem_inc(S("psA_free"), 2)
            pairs(pe, d.EM, body)
    S.end()


class Context:
    pass


def graph_kernel(nc, w, out, stop=99):
    c = Context()
    c.d = d = Dims(w["x"].shape[0], w["src"].shape[0])
    rows = d.N + d.EP
    c.TW = [D + 2] * 5 + [D + 8]
    with ExitStack() as st:
        def sb(name, shape, dt=F32):
            return st.enter_context(nc.sbuf_tensor(name, shape, dt))

        def dram(name, shape, dt=F32):
            return nc.dram_tensor(name, shape, dt).ap()
        c.HP = [dram(f"hp_table{l}", (rows, c.TW[l])) for l in range(6)]
        c.X2 = out if stop < 4 else dram("x2_table", (d.N, D))
        c.X3, c.R3 = dram("x3_table", (d.N, D)), dram("r3_table", (rows, D))
        c.H = [dram(f"hidden_table{i}", (rows, 2 * D)) for i in range(2)]
        c.NS = dram("sum_by_src", (d.NP + P, D))
        c.POS = dram("slot_table", (d.NP, 1), I32)
        c.dstRow, c.srcRow = dram("dst_row", (d.EP,)), dram("src_row", (d.EP,))
        c.SF = dram("same_dst_tiles", (P, d.EM * 2 * MAC), U8)
        c.XD = dram("x_of_dst", (d.EP, D))
        c.X0T = dram("x0_of_dst_T", (P, d.EP))
        c.HT = [dram("h1_of_dst_T", (2 * P, d.EP)), dram("h2_of_dst_T", (2 * P, d.EP))]

        c.ident, c.upper, c.zero = sb("ident", [P, P]), sb("upper", [P, P]), sb("zero", [P, D])
        c.contF, c.contB, c.negF = sb("contF", [P, 4, 256]), sb("contB", [P, 4, 256]), sb("negF", [P, 4, 256])
        c.runF, c.runB, c.negRunF = sb("runF", [P, 256]), sb("runB", [P, 256]), sb("negRunF", [P, 256])
        c.last, c.negLast = sb("last", [P, 256]), sb("negLast", [P, 256])
        c.wholeF, c.wholeB, c.negWholeF = sb("wholeF", [4, d.QP]), sb("wholeB", [4, d.QP]), sb("negWholeF", [4, d.QP])
        c.EL, c.loopEL = sb("EL", [P, 5, 256]), sb("loopEL", [P, 5, 256])
        c.dstF, c.srcF, c.invdeg = sb("dstF", [P, d.ET]), sb("srcF", [P, d.ET]), sb("invdeg", [P, d.ET])
        c.canonI, c.idxD, c.idxS, c.accI, c.slotI = (sb(n, [P, d.ET], I32) for n in ("canonI", "idxD", "idxS", "accI", "slotI"))
        c.SS, c.SD, c.SL, c.AL, c.AF = (sb(n, [P, d.ET * 4]) for n in ("score_src", "score_dst", "score_self", "alpha", "alpha_self"))
        c.W0, c.W5, c.M = sb("W0", [P, 5, D + 2]), sb("W5", [P, D + 8]), sb("M", [P, 3, D])
        c.b0row, c.b4row, c.b5row, c.blin = sb("b0row", [P, D]), sb("b4row", [P, D]), sb("b5row", [P, D]), sb("blin", [P, D + 8])
        c.b0col, c.bm = sb("b0col", [P, 1]), sb("bm", [P, 3])
        c.W2n, c.W2s, c.b2nrow = sb("W2n", [P, D]), sb("W2s", [P, D]), sb("b2nrow", [P, D])
        c.Ws = [sb("Ws0", [P, 1, 256]), sb("Ws1", [P, 2, 256]), sb("Ws2", [P, 2, D])]
        c.Wn = [sb("Wn0", [P, 1, 256]), sb("Wn1", [P, 2, 256]), sb("Wn2", [P, 2, D])]
        c.bcol = [sb("bcol0", [P, 2]), sb("bcol1", [P, 2]), sb("bcol2", [P, 1])]
        c.b3row = sb("b3row", [P, D])

        Signals.kept = [st.enter_context(nc.semaphore(f"soft_dma{i}")) for i in range(12)]
        prepare_edges(nc, c, w["src"], w["dst"], w["edge_attr_16"])
        prepare_tiles(nc, c)
        prepare_weights(nc, c, w)
        nodes_gat(nc, c, w["x"])
        if stop == 1:
            return
        edge_setup(nc, c, w["x"])
        with nc.sbuf_tensor("source_rows", [P, d.ET * D], F32) as c.G:
            for l in range(6):
                gather_sources(nc, c, l)
                attention(nc, c, l)
                gat_messages(nc, c, l)
        if stop == 3:
            return
        sum_by_source(nc, c)
        nodes_sage(nc, c, out)
        rows_of_dst(nc, c, "r3d", c.R3[0:d.N, :], c.R3[d.N:, :])
        rows_of_dst(nc, c, "x3d", c.X3, c.XD)
        for s in range(3):
            sage_edges(nc, c, s, out)


def kernel(**inputs):
    import numpy as _np
    import concourse.bacc as _bacc
    from concourse import mybir as _mybir
    from concourse.bass_utils import run_bass_kernel_spmd as _run

    nc = _bacc.Bacc("TRN2", target_bir_lowering=False, num_devices=1)
    arrays, w = {}, {}
    for name in inputs:
        a = _np.ascontiguousarray(inputs[name])
        arrays[f"in_{name}_dram"] = a
        w[name] = nc.dram_tensor(f"in_{name}_dram", a.shape, _mybir.dt.from_np(a.dtype), kind="ExternalInput").ap()
    out = nc.dram_tensor("out_dram", w["x"].shape, F32, kind="ExternalOutput").ap()
    graph_kernel(nc, w, out)
    r = _run(nc, [arrays], core_ids=[0])
    return r.results[0]["out_dram"]
```

```python
import math
from contextlib import ExitStack

import concourse.bass as bass
from concourse import mybir

F32 = mybir.dt.float32
I32 = mybir.dt.int32
U8 = mybir.dt.uint8
ACT = mybir.ActivationFunctionType
ALU = mybir.AluOpType
AX = mybir.AxisListType.X

P = 128
D = 128
MAC = 512
K4 = MAC // P
BIG = 1.0e30
SKIP = 1.0e6
EPS = 1e-5
ALPHA, THETA = 0.2, 0.2


class Signals:

    SOFT = ("slot", "put", "x_in", "ns_zero", "soft")
    kept = []

    def __init__(self, nc, tag):
        self.nc, self.tag, self.stack, self.named, self.taken = nc, tag, ExitStack(), {}, 0

    def __call__(self, name):
        if name not in self.named:
            if name.startswith(self.SOFT):
                self.named[name] = self.kept[self.taken]
                self.taken += 1
            else:
                self.named[name] = self.stack.enter_context(self.nc.semaphore(f"{self.tag}_{name}"))
        return self.named[name]

    def end(self):
        if self.taken:
            first = min(s.num for s in self.kept)
            self.nc.gpsimd.dma_reset(range(first, first + len(self.kept)))
        for s in self.named.values():
            self.nc.gpsimd.sem_clear(s)
        self.nc.all_engine_barrier()
        self.stack.close()


def node_rows(t, g, n):
    if isinstance(g, int):
        r = min(g * MAC, n - MAC)
        return t[r:r + MAC, :].rearrange("(p k) f -> p k f", k=K4)
    v = t[0:n // MAC * MAC, :].rearrange("(g p k) f -> g p k f", p=P, k=K4)
    return v[bass.ds(g, 1)].rearrange("a p k f -> p (a k) f")


def edge_rows(t, m):
    v = t.rearrange("(m k p) f -> m p k f", p=P, k=K4)
    return v[m] if isinstance(m, int) else v[bass.ds(m, 1)].rearrange("a p k f -> p (a k) f")


def chunk(t, m, w):
    return t[:, m * w:(m + 1) * w] if isinstance(m, int) else t[:, bass.ds(m * w, w)]


class Dims:
    def __init__(self, n, e):
        self.N, self.E = n, e
        self.NM = -(-n // MAC)
        self.NM += self.NM % 2
        self.NP = self.NM * MAC
        self.EM = -(-e // MAC)
        self.ET, self.EP, self.QP = 4 * self.EM, MAC * self.EM, 2 * self.EM
        self.U = 7 if self.EM % 7 == 0 else 1
        assert n >= (self.NM - 1) * MAC and self.QP <= P


def pairs(nc_eng, count, body):
    if count // 2 > 0:
        with nc_eng.Fori(0, count // 2) as i:
            body(i * 2, (0, 1))
    if count % 2:
        body(count - 1, (0,))


def prepare_edges(nc, c, src, dst, ea):
    d, S = c.d, Signals(nc, "edges")
    QP, ET, E, NP = d.QP, d.ET, d.E, d.NP
    qf, rem = E // 256, E % 256
    n1 = (E - 1) // 256
    with ExitStack() as st:
        def sb(name, shape, dt=F32):
            return st.enter_context(nc.sbuf_tensor(f"{S.tag}_{name}", shape, dt))
        di, si = sb("di", [P, 256], I32), sb("si", [P, 256], I32)
        nfi, pli = sb("nfi", [P, 1], I32), sb("pli", [P, 1], I32)
        nf, pl = sb("nf", [P, 1]), sb("pl", [P, 1])
        dR, sR = sb("dR", [P, 256]), sb("sR", [P, 256])
        t1, t2, t3, t4, nl = (sb(x, [P, 256]) for x in ("t1", "t2", "t3", "t4", "nl"))
        wf = sb("wf", [P, 4])
        wb = sb("wb", [P, 4])
        posi = sb("posi", [P, NP // P], I32)
        ps = st.enter_context(nc.psum_tensor("pe_ps", [P, 8, 128], F32))
        block = st.enter_context(nc.Block())

        @block.gpsimd
        def _(pool):
            pool.memset(di[:], -1).then_inc(S("cleared"), 1)
            pool.memset(si[:], -1).then_inc(S("cleared"), 1)
            pool.memset(nfi[:], -2).then_inc(S("cleared"), 1)
            pool.memset(pli[:], -3).then_inc(S("cleared"), 1)
            pool.memset(c.ident[:], 0.0).then_inc(S("zeroed"), 1)
            pool.memset(c.upper[:], 0.0).then_inc(S("zeroed"), 1)
            pool.wait_ge(S("zeroed"), 2)
            pool.affine_select(out=c.ident[:], in_=c.ident[:], compare_op=ALU.not_equal, fill=1.0, base=0,
                               pattern=[[-1, P]], channel_multiplier=1).then_inc(S("ident"), 1)
            pool.affine_select(out=c.upper[:], in_=c.upper[:], compare_op=ALU.is_ge, fill=1.0, base=0,
                               pattern=[[-1, MAC]], channel_multiplier=1).then_inc(S("upper"), 1)
            pool.iota(posi[:], pattern=[[1, NP // P]], base=0, channel_multiplier=NP // P).then_inc(S("pos"), 1)
            pool.iota(c.slotI[:], pattern=[[P, ET]], base=d.N, channel_multiplier=1).then_inc(S("slots"), 1)

        @block.sync
        def _(sp):
            sp.wait_ge(S("cleared"), 4)
            for n, (t, a) in enumerate(((di, dst), (si, src))):
                sp.dma_start(t[0:qf, :], a[0:qf * 256].rearrange("(q j) -> q j", j=256)).then_inc(S("idx_full"), 16)
                if rem:
                    sp.dma_start(t[qf:qf + 1, 0:rem], a[qf * 256:E].rearrange("(q j) -> q j", q=1)).then_inc(S("idx_rem"), 16)
            sp.dma_start(nfi[0:n1, :], dst[256:256 * n1 + 1:256].rearrange("(q j) -> q j", j=1), allow_slow_non_contiguous=True).then_inc(S("nf_in"), 16)
            n2 = E // 256
            sp.dma_start(pli[1:min(n2, QP - 1) + 1, :],
                         dst[255:255 + 256 * (min(n2, QP - 1) - 1) + 1:256].rearrange("(q j) -> q j", j=1),
                         allow_slow_non_contiguous=True).then_inc(S("pl_in"), 16)
            sp.wait_ge(S("pos"), 1)
            sp.dma_start(c.POS.rearrange("(p c) a -> p (c a)", p=P), posi[:]).then_inc(S("pos_out"), 16)
            sp.wait_ge(S("rows"), 1)
            sp.dma_start(c.dstRow.rearrange("(q j) -> q j", j=256), dR[0:QP, :]).then_inc(S("row_out"), 16)
            sp.dma_start(c.srcRow.rearrange("(q j) -> q j", j=256), sR[0:QP, :]).then_inc(S("row_out"), 16)
            sp.wait_ge(S("pos_out"), 16)
            sp.wait_ge(S("row_out"), 32)

        @block.vector
        def _(v):
            v.wait_ge(S("idx_full"), 32)
            if rem:
                v.wait_ge(S("idx_rem"), 32)
            v.wait_ge(S("nf_in"), 16)
            v.wait_ge(S("pl_in"), 16)
            v.tensor_copy(sR[:], si[:]).then_inc(S("c0"), 1)
            v.tensor_copy(nf[:], nfi[:]).then_inc(S("c1"), 1)
            v.tensor_copy(pl[:], pli[:]).then_inc(S("c2"), 1)
            v.tensor_copy(dR[:], di[:]).then_inc(S("rows"), 1)
            v.wait_ge(S("rows"), 1)
            v.memset(c.contF[:, :, 0:1], 0.0)
            v.memset(c.contB[:, :, 255:256], 0.0)
            for h in range(4):
                v.tensor_tensor(c.contF[:, h, 1:256], dR[:, 1:256], dR[:, 0:255], ALU.is_equal)
                last = v.tensor_tensor(c.contB[:, h, 0:255], dR[:, 0:255], dR[:, 1:256], ALU.is_equal)
            last.then_inc(S("cont"), 1)
            v.tensor_scalar(c.runF[:], dR[:], pl[:], None, ALU.is_equal).then_inc(S("runF"), 1)
            v.tensor_scalar(c.runB[:], dR[:], nf[:], None, ALU.is_equal).then_inc(S("runB"), 1)
            v.wait_ge(S("cont"), 1)
            v.tensor_scalar(c.negF[:], c.contF[:], 1.0, BIG, ALU.subtract, ALU.mult).then_inc(S("m1"), 1)
            v.tensor_scalar(c.last[:, 0:255], c.contB[:, 0, 0:255], -1.0, 1.0, ALU.mult, ALU.add)
            v.tensor_scalar(c.last[:, 255:256], dR[:, 255:256], nf[:], None, ALU.not_equal).then_inc(S("last"), 1)
            v.wait_ge(S("runF"), 1)
            v.wait_ge(S("runB"), 1)
            v.tensor_scalar(c.negRunF[:], c.runF[:], 1.0, BIG, ALU.subtract, ALU.mult).then_inc(S("m2"), 1)
            for h in range(4):
                v.tensor_copy(wf[:, h:h + 1], c.runF[:, 255:256])
                last = v.tensor_copy(wb[:, h:h + 1], c.runB[:, 0:1])
            last.then_inc(S("whole"), 1)
            v.wait_ge(S("last"), 1)
            v.tensor_scalar(c.negLast[:], c.last[:], 1.0, BIG, ALU.subtract, ALU.mult).then_inc(S("m3"), 1)
            v.tensor_scalar(nl[:], c.last[:], -SKIP, SKIP, ALU.mult, ALU.add).then_inc(S("nl"), 1)
            v.tensor_scalar(t1[:], dR[:], 0.0, SKIP, ALU.is_lt, ALU.mult).then_inc(S("t1"), 1)
            v.wait_ge(S("nl"), 1)
            v.tensor_tensor(t2[:], nl[:], dR[:], ALU.add).then_inc(S("t2"), 1)
            v.wait_ge(S("t1"), 1)
            v.wait_ge(S("t2"), 1)
            v.tensor_tensor(t3[:], t1[:], t2[:], ALU.add).then_inc(S("canon_rows"), 1)
            v.wait_ge(S("c0"), 1)
            v.wait_ge(S("columns"), 1)
            for j in range(2):
                v.tensor_copy(c.dstF[:, j::2], ps[:, j, 0:QP])
                v.tensor_copy(c.srcF[:, j::2], ps[:, 2 + j, 0:QP])
                last = v.tensor_copy(c.canonI[:, j::2], ps[:, 4 + j, 0:QP])
            last.then_inc(S("cols"), 1)
            v.wait_ge(S("cols"), 1)
            v.tensor_scalar(c.idxD[:], c.dstF[:], 0.0, None, ALU.max).then_inc(S("m4"), 1)
            v.tensor_scalar(c.idxS[:], c.srcF[:], 0.0, None, ALU.max).then_inc(S("m5"), 1)
            v.wait_ge(S("chains"), 1)
            v.tensor_copy(c.wholeF[:], ps[0:4, 6, 0:QP]).then_inc(S("wF"), 1)
            v.tensor_copy(c.wholeB[:], ps[0:4, 7, 0:QP]).then_inc(S("m6"), 1)
            v.wait_ge(S("wF"), 1)
            v.tensor_scalar(c.negWholeF[:], c.wholeF[:], 1.0, BIG, ALU.subtract, ALU.mult).then_inc(S("m7"), 1)

        @block.tensor
        def _(pe):
            pe.wait_ge(S("ident"), 1)
            pe.wait_ge(S("rows"), 1)
            pe.wait_ge(S("c0"), 1)
            pe.wait_ge(S("canon_rows"), 1)
            for n, r in enumerate((dR, sR, t3)):
                for j in range(2):
                    last = pe.transpose(ps[:, 2 * n + j, 0:QP], r[0:QP, j * P:(j + 1) * P], c.ident[0:QP, 0:QP])
            last.then_inc(S("columns"), 1)
            pe.wait_ge(S("whole"), 1)
            pe.wait_ge(S("cols"), 1)
            pe.transpose(ps[0:4, 6, 0:QP], wf[0:QP, :], c.ident[0:QP, 0:QP])
            pe.transpose(ps[0:4, 7, 0:QP], wb[0:QP, :], c.ident[0:QP, 0:QP]).then_inc(S("chains"), 1)
    S.end()


def prepare_tiles(nc, c):
    d, S = c.d, Signals(nc, "tiles")
    with ExitStack() as st:
        def sb(name, shape, dt=F32):
            return st.enter_context(nc.sbuf_tensor(f"{S.tag}_{name}", shape, dt))
        db = [sb(f"db{i}", [P, MAC]) for i in range(2)]
        sbc = [sb(f"sbc{i}", [P, MAC]) for i in range(2)]
        sf = [sb(f"sf{i}", [P, 2 * MAC], U8) for i in range(2)]
        tail = [sb(f"tail{i}", [P, 1]) for i in range(2)]
        junk, dup = [sb(f"junk{i}", [P, K4, MAC]) for i in range(2)], [sb(f"dup{i}", [P, K4]) for i in range(2)]
        spareI, spareF = sb("spareI", [P, d.EM, K4], I32), sb("spareF", [P, d.ET])
        dupF, a1, a2 = sb("dupF", [P, d.ET]), sb("a1", [P, d.ET]), sb("a2", [P, d.ET])
        block = st.enter_context(nc.Block())

        def bcast(row, m):
            v = row.rearrange("(a e) -> a e", a=1)
            return chunk(v, m, MAC).broadcast_to([P, MAC])

        @block.sync
        def _(sp):
            def load(m, pars):
                for b in pars:
                    g = m + b
                    sp.wait_ge(S("bfree"), g + 1)
                    sp.sem_inc(S("sp_pass"), 1)
                    sp.dma_start(db[b][:], bcast(c.dstRow, g)).then_inc(S(f"d_in{b}"), 16)
                    sp.dma_start(sbc[b][:], bcast(c.srcRow, g)).then_inc(S(f"s_in{b}"), 16)
            pairs(sp, d.EM, load)

        @block.scalar
        def _(act):
            def store(m, pars):
                for b in pars:
                    g = m + b
                    act.wait_ge(S("sf_done"), g + 1)
                    act.dma_start(chunk(c.SF, g, 2 * MAC), sf[b][:]).then_inc(S(f"sf_out{b}"), 16)
                    act.wait_ge(S(f"sf_out{b}"), (g - b) * 8 + 16)
                    act.sem_inc(S("sf_free"), 1)
            pairs(act, d.EM, store)

        @block.vector
        def _(v):
            v.memset(tail[1][:], -3.0).then_inc(S("tail"), 1)
            v.sem_inc(S("bfree"), 2)
            v.sem_inc(S("sf_free"), 2)

            def tiles(m, pars):
                for b in pars:
                    g = m + b
                    v.wait_ge(S(f"d_in{b}"), (g - b) * 8 + 16)
                    v.wait_ge(S(f"s_in{b}"), (g - b) * 8 + 16)
                    v.wait_ge(S("sf_free"), g + 1)
                    v.wait_ge(S("tail"), g + 1)
                    for k in range(K4):
                        col = slice(k * P, (k + 1) * P)
                        v.tensor_scalar(sf[b][:, col], db[b][:, col], c.dstF[:, bass.ds(g * 4 + k, 1)], None, ALU.is_equal)
                        before = db[b][:, k * P - 1:k * P] if k else tail[1 - b][:]
                        last = v.tensor_scalar(sf[b][:, MAC + k * P:MAC + (k + 1) * P], db[b][:, col], before, None, ALU.is_equal)
                    last.then_inc(S("sf_done"), 1)
                    v.tensor_copy(tail[b][:], db[b][:, MAC - 1:MAC]).then_inc(S("tail"), 1)
                    for k in range(K4):
                        last = v.scalar_tensor_tensor(out=junk[b][:, k, k * P:], in0=sbc[b][:, k * P:],
                                                      scalar=c.srcF[:, bass.ds(g * 4 + k, 1)], in1=c.upper[:, 0:MAC - k * P],
                                                      op0=ALU.is_equal, op1=ALU.mult, accum_out=dup[b][:, k:k + 1])
                    last.then_inc(S("dup"), 1)
                    v.wait_ge(S("dup"), g + 1)
                    v.tensor_copy(chunk(dupF, g, K4), dup[b][:]).then_inc(S("bfree"), 1)
            pairs(v, d.EM, tiles)
            v.wait_ge(S("bfree"), d.EM + 2)
            v.tensor_scalar(a1[:], dupF[:], 0.5, None, ALU.is_gt).then_inc(S("a1"), 1)
            v.tensor_scalar(a2[:], c.srcF[:], 0.0, None, ALU.is_lt).then_inc(S("a2"), 1)
            v.wait_ge(S("spare"), 1)
            v.tensor_copy(spareF[:], spareI[:].rearrange("p m k -> p (m k)")).then_inc(S("spareF"), 1)
            v.wait_ge(S("a2"), 1)
            v.tensor_tensor(a1[:], a1[:], a2[:], ALU.max).then_inc(S("a3"), 1)
            v.wait_ge(S("spareF"), 1)
            v.wait_ge(S("a3"), 1)
            v.tensor_tensor(a2[:], spareF[:], c.srcF[:], ALU.subtract).then_inc(S("a4"), 1)
            v.wait_ge(S("a4"), 1)
            v.tensor_tensor(a2[:], a2[:], a1[:], ALU.mult).then_inc(S("a5"), 1)
            v.wait_ge(S("a5"), 1)
            v.tensor_tensor(c.accI[:], a2[:], c.srcF[:], ALU.add).then_inc(S("a6"), 1)

        @block.gpsimd
        def _(pool):
            pool.iota(spareI[:], pattern=[[0, d.EM], [P, K4]], base=d.NP, channel_multiplier=1).then_inc(S("spare"), 1)
    S.end()


def prepare_weights(nc, c, w):
    d, S = c.d, Signals(nc, "weights")
    QP, EL_ROWS = d.QP, 256
    qf, rem = d.E // 256, d.E % 256
    with ExitStack() as st:
        def sb(name, shape, dt=F32):
            return st.enter_context(nc.sbuf_tensor(f"{S.tag}_{name}", shape, dt))
        asd = sb("asd", [P, 5, 2, D])
        al1 = sb("al1", [P, 2, 2, 64])
        aed, we = sb("aed", [16, 5, D]), sb("we", [16, 5, D])
        prod = sb("prod", [P, 5, D])
        prod2 = sb("prod2", [P, 4, 64])
        prodb = sb("prodb", [P, 4, 64])
        vcol = sb("vcol", [16, 5])
        vbc = sb("vbc", [16, 5, P])
        vrow = sb("vrow", [P, 5, 16])
        eat = sb("eat", [P, 256, 16])
        pe_prod = sb("ea_prod", [P, 256, 16])
        bcol = sb("bcol", [P, 3])
        mid = sb("mid", [P, 3, D])
        wT = sb("wT", [P, 3, D])
        ps = st.enter_context(nc.psum_tensor("w_ps", [P, 512], F32))
        psw = st.enter_context(nc.psum_tensor("wT_ps", [P, 4, D], F32))
        psm = st.enter_context(nc.psum_tensor("wm_ps", [P, 4, D], F32))
        psv = st.enter_context(nc.psum_tensor("v_ps", [P, 5, 16], F32))
        block = st.enter_context(nc.Block())

        def rowvec(a):
            return a.rearrange("(a n) -> a n", a=1).broadcast_to([P, a.shape[0]])

        def colvec(a):
            return a.rearrange("(p a) -> p a", a=1)

        loads = []
        for l in range(5):
            loads += [(c.W0[:, l, 0:D], w["L0_gnn_Ws"][l]),
                      (asd[:, l, 0, :], rowvec(w["L0_gnn_a_srcs"][l])), (asd[:, l, 1, :], rowvec(w["L0_gnn_a_dsts"][l])),
                      (we[:, l, :], w["L0_gnn_Wes"][l]),
                      (aed[:, l, :], w["L0_gnn_a_edges"][l].rearrange("(a n) -> a n", a=1).broadcast_to([16, D]))]
        loads += [(mid[:, i, :], w["L0_gnn_mid_ws"][i]) for i in range(3)]
        loads += [(bcol[:, i:i + 1], colvec(w["L0_gnn_biases"][i + 1])) for i in range(3)]
        loads += [(c.b0row[:], rowvec(w["L0_gnn_biases"][0])), (c.b4row[:], rowvec(w["L0_gnn_biases"][4])),
                  (c.b0col[:], colvec(w["L0_gnn_biases"][0])),
                  (c.W5[:, 0:D], w["L1_gnn_W"]), (c.blin[:, 0:D], rowvec(w["L1_gnn_b_lin"])),
                  (c.b5row[:], rowvec(w["L1_gnn_bias"])),
                  (al1[:].rearrange("p a b n -> p (a b n)"), w["L1_gnn_alpha"].rearrange("a h n -> a (h n)").broadcast_to([P, 256])),
                  (c.W2n[:], w["L2_gnn_nbr_w"]), (c.W2s[:], w["L2_gnn_self_w"]), (c.b2nrow[:], rowvec(w["L2_gnn_b"])),
                  (c.Ws[0][:, 0, :], w["L3_gnn_Ws0"]), (c.Wn[0][:, 0, :], w["L3_gnn_Wn0"]),
                  (c.b3row[:], rowvec(w["L3_gnn_b2"])), (c.bcol[2][:], colvec(w["L3_gnn_b2"]))]
        for f in range(2):
            loads += [(c.Ws[1][:, f, :], w["L3_gnn_Ws1"][f * P:(f + 1) * P, :]), (c.Wn[1][:, f, :], w["L3_gnn_Wn1"][f * P:(f + 1) * P, :]),
                      (c.Ws[2][:, f, :], w["L3_gnn_Ws2"][f * P:(f + 1) * P, :]), (c.Wn[2][:, f, :], w["L3_gnn_Wn2"][f * P:(f + 1) * P, :]),
                      (c.bcol[0][:, f:f + 1], colvec(w["L3_gnn_b0"][f * P:(f + 1) * P])),
                      (c.bcol[1][:, f:f + 1], colvec(w["L3_gnn_b1"][f * P:(f + 1) * P]))]

        @block.sync
        def _(sp):
            for dst, src in loads:
                sp.dma_start(dst, src).then_inc(S("w_in"), 16)
            sp.wait_ge(S("ea_clear"), 1)
            ea = w["edge_attr_16"]
            sp.dma_start(eat[0:qf, :, :], ea[0:qf * 256, :].rearrange("(q j) f -> q j f", j=256)).then_inc(S("ea_in"), 16)
            if rem:
                sp.dma_start(eat[qf:qf + 1, 0:rem, :], ea[qf * 256:d.E, :].rearrange("(q j) f -> q j f", q=1)).then_inc(S("ea_in2"), 16)

        @block.gpsimd
        def _(pool):
            pool.memset(eat[:], 0.0).then_inc(S("ea_clear"), 1)
            pool.memset(c.zero[:], 0.0).then_inc(S("zero"), 1)
            pool.wait_ge(S("zero"), 1)
            total = d.NP // P + K4
            for g in range(0, total, 64):
                n = min(64, total - g)
                pool.dma_start(c.NS.rearrange("(p a) f -> p a f", p=P)[:, g:g + n, :],
                               c.zero[:].rearrange("p (a f) -> p a f", a=1).broadcast_to([P, n, D])).then_inc(S("ns_zero"), 16)
            pool.wait_ge(S("ns_zero"), 16 * len(range(0, total, 64)))

        @block.vector
        def _(v):
            v.wait_ge(S("w_in"), 16 * len(loads))
            for l in range(5):
                if l:
                    v.wait_ge(S("w0_ext"), l)
                v.tensor_tensor(prod[:, 0:2, :], c.W0[:, l, 0:D].unsqueeze(1).broadcast_to([P, 2, D]), asd[:, l, :, :],
                                ALU.mult).then_inc(S("wa"), 1)
                v.wait_ge(S("wa"), l + 1)
                v.tensor_reduce(c.W0[:, l, D:D + 2], prod[:, 0:2, :], AX, ALU.add).then_inc(S("w0_ext"), 1)
            v.memset(c.W5[:, D:D + 8], 0.0)
            v.memset(c.blin[:, D:D + 8], 0.0).then_inc(S("ext_clear"), 1)
            for n, (t, pr) in enumerate(((c.W5, prod2), (c.blin, prodb))):
                v.tensor_tensor(pr[:].rearrange("p (a b) n -> p a (b n)", a=2), t[:, 0:D].unsqueeze(1).broadcast_to([P, 2, D]),
                                al1[:].rearrange("p a b n -> p a (b n)"), ALU.mult).then_inc(S("w5_prod"), 1)
                v.wait_ge(S("w5_prod"), n + 1)
                v.wait_ge(S("ext_clear"), 1)
                v.tensor_reduce(t[:, D:D + 2], pr[:, 0:2, :], AX, ALU.add)
                v.tensor_reduce(t[:, D + 6:D + 8], pr[:, 2:4, :], AX, ALU.add)
            for i in range(3):
                beta = math.log(THETA / (i + 1) + 1.0)
                v.tensor_scalar(mid[:, i, :], mid[:, i, :], beta, None, ALU.mult).then_inc(S("beta_m"), 1)
                v.wait_ge(S("beta_m"), i + 1)
                v.scalar_tensor_tensor(out=c.M[:, i, :], in0=c.ident[:], scalar=1.0 - beta, in1=mid[:, i, :],
                                       op0=ALU.mult, op1=ALU.add).then_inc(S("mid"), 1)
            v.wait_ge(S("wT_ps"), 1)
            v.tensor_copy(wT[:], psw[:, 0:3, :]).then_inc(S("wT"), 1)
            v.wait_ge(S("mid"), 3)
            v.tensor_scalar(c.AM[:], c.M[:], ALPHA, None, ALU.mult).then_inc(S("am"), 1)
            v.wait_ge(S("wm_ps"), 1)
            v.wait_ge(S("am"), 1)
            v.scalar_tensor_tensor(out=c.WM[:, 0, :], in0=psm[:, 0, :], scalar=1.0 - ALPHA, in1=c.AM[:, 0, :],
                                   op0=ALU.mult, op1=ALU.add)
            v.tensor_scalar(c.WM[:, 1:3, :], psm[:, 1:3, :], 1.0 - ALPHA, None, ALU.mult)
            v.wait_ge(S("w0_ext"), 5)
            v.tensor_tensor(prod[0:16, :, :], we[:], aed[:], ALU.mult).then_inc(S("we_prod"), 1)
            v.wait_ge(S("we_prod"), 1)
            v.tensor_reduce(vcol[:], prod[0:16, :, :], AX, ALU.add).then_inc(S("vcol"), 1)
            v.wait_ge(S("vcol"), 1)
            v.tensor_copy(vbc[:], vcol[:].unsqueeze(2).broadcast_to([16, 5, P])).then_inc(S("vbc"), 1)
            v.wait_ge(S("vrow_ps"), 1)
            v.tensor_copy(vrow[:], psv[:]).then_inc(S("vrow"), 1)
            v.wait_ge(S("vrow"), 1)
            v.wait_ge(S("ea_in"), 16)
            if rem:
                v.wait_ge(S("ea_in2"), 16)
            for l in range(5):
                if l:
                    v.wait_ge(S("el"), l)
                v.tensor_tensor(pe_prod[:], eat[:], vrow[:, l, :].unsqueeze(1).broadcast_to([P, 256, 16]), ALU.mult).then_inc(S("ea_prod"), 1)
                v.wait_ge(S("ea_prod"), l + 1)
                v.tensor_reduce(c.EL[:, l, :], pe_prod[:], AX, ALU.add).then_inc(S("el"), 1)
            v.wait_ge(S("bm_ps"), 1)
            v.tensor_scalar(c.bm[:], ps[:, 0:3], 1.0 - ALPHA, None, ALU.mult).then_inc(S("bm"), 1)

        @block.tensor
        def _(pe):
            pe.wait_ge(S("w_in"), 16 * len(loads))
            for i in range(3):
                last = pe.transpose(psw[:, i, :], c.W0[:, i + 1, 0:D], c.ident[:])
            last.then_inc(S("wT_ps"), 1)
            pe.wait_ge(S("mid"), 3)
            pe.wait_ge(S("wT"), 1)
            for i in range(3):
                last = pe.matmul(psm[:, i, :], wT[:, i, :], c.M[:, i, :], start=True, stop=True)
            last.then_inc(S("wm_ps"), 1)
            for i in range(3):
                last = pe.matmul(ps[:, i:i + 1], c.M[:, i, :], bcol[:, i:i + 1], start=True, stop=True)
            last.then_inc(S("bm_ps"), 1)
            pe.wait_ge(S("vbc"), 1)
            for l in range(5):
                last = pe.matmul(psv[:, l, :], vbc[:, l, :], c.ident[0:16, 0:16], start=True, stop=True)
            last.then_inc(S("vrow_ps"), 1)
    S.end()


class Norm:

    def __init__(self, st, nc, S, name, par):
        def sb(n, shape):
            return [st.enter_context(nc.sbuf_tensor(f"{S.tag}_{name}_{n}{i}", shape, F32)) for i in range(par)]
        self.S, self.name = S, name
        self.st, self.mv, self.ve = sb("st", [P, K4, 6]), sb("mv", [P, K4, 2]), sb("ve", [P, K4])
        self.sd, self.rs, self.nm = sb("sd", [P, K4]), sb("rs", [P, K4]), sb("nm", [P, K4])

    def stats(self, v, b, g, x):
        S, n = self.S, self.name
        for k in range(K4):
            last = v.bn_stats(self.st[b][:, k, :], x[:, k, :])
        last.then_inc(S(n + "_stats"), 1)

    def moments(self, v, b, g):
        S, n = self.S, self.name
        v.wait_ge(S(n + "_stats"), g + 1)
        v.sem_inc(S("dve_pass"), 1)
        for k in range(K4):
            last = v.bn_aggr(self.mv[b][:, k, :], self.st[b][:, k, :])
        last.then_inc(S(n + "_mv"), 1)

    def variance(self, v, b, g):
        S, n = self.S, self.name
        v.wait_ge(S(n + "_mv"), g + 1)
        v.tensor_scalar(self.ve[b][:], self.mv[b][:, :, 1], EPS, None, ALU.add).then_inc(S(n + "_var"), 1)

    def root(self, act, b, g):
        S, n = self.S, self.name
        act.wait_ge(S(n + "_var"), g + 1)
        act.activation(self.sd[b][:], self.ve[b][:], ACT.Sqrt).then_inc(S(n + "_sd"), 1)

    def recip(self, v, b, g):
        S, n = self.S, self.name
        v.wait_ge(S(n + "_sd"), g + 1)
        v.reciprocal(self.rs[b][:], self.sd[b][:]).then_inc(S(n + "_rs"), 1)

    def shift(self, v, b, g):
        S, n = self.S, self.name
        v.wait_ge(S(n + "_rs"), g + 1)
        v.scalar_tensor_tensor(out=self.nm[b][:], in0=self.mv[b][:, :, 0], scalar=-1.0, in1=self.rs[b][:],
                               op0=ALU.mult, op1=ALU.mult).then_inc(S(n + "_nm"), 1)

    def vector(self, v, gb, x):
        for g, b in gb:
            self.stats(v, b, g, x[b])
        for step in (self.moments, self.variance, self.recip, self.shift):
            for g, b in gb:
                step(v, b, g)

    def apply(self, act, b, g, out, x, done):
        S, n = self.S, self.name
        act.wait_ge(S(n + "_nm"), g + 1)
        for k in range(K4):
            last = act.activation(out[:, k, :], x[:, k, :], ACT.Relu, bias=self.nm[b][:, k:k + 1], scale=self.rs[b][:, k:k + 1])
        last.then_inc(done, 1)


def turn(pe, out, src, ident, done):
    for k in range(K4):
        last = pe.transpose(out[:, k * P:(k + 1) * P], src[:, k, :], ident)
    last.then_inc(done, 1)


def turn_back(pe, out, src, ident, done):
    for k in range(K4):
        last = pe.transpose(out[:, k, :], src[:, k * P:(k + 1) * P], ident)
    last.then_inc(done, 1)


def rows_of(pe, out, hT, w, done):
    for k in range(K4):
        last = pe.matmul(out[:, k, 0:w.shape[1]], hT[:, k * P:(k + 1) * P], w, start=True, stop=True)
    last.then_inc(done, 1)


FLY = 4


def node_group(nm, i):
    full = (nm - 2) // FLY
    if i < full:
        return [(i * FLY + b, b) for b in range(FLY)]
    return [(g, b) for b, g in enumerate(range(full * FLY, nm))] if i == full else []


def node_groups_two_ahead(eng, nm, body):
    full = (nm - 2) // FLY
    if full > 2:
        with eng.Fori(0, full - 2) as i:
            body(*([((i + n) * FLY + b, b) for b in range(FLY)] for n in range(3)))
    for i in range(max(full - 2, 0), full + 1):
        body(*(node_group(nm, i + n) for n in range(3)))


def store_rows(sp, S, nm, n, table, g, b, buf, stores, name="st"):
    if isinstance(g, int) and g == nm - 1:
        before = (b - 1) % FLY
        sp.wait_ge(S(f"{name}{before}"), ((g - 1 - before) // FLY) * stores * 16 + 16 * n)
    sp.sem_inc(S("sp_pass"), 1)
    sp.dma_start(table, buf).then_inc(S(f"{name}{b}"), 16)


def pool_alone(pool, c, issue, take, settle):
    U, n = c.d.U, c.d.EM // c.d.U
    for j in range(U):
        issue(j, j)
    if n > 1:
        with pool.Fori(1, n) as i:
            for j in range(U):
                take(i * U - U + j, j, i - 1)
            for j in range(U):
                settle(i * U - U + j, j, i - 1)
                issue(i * U + j, j)
    for j in range(U):
        take((n - 1) * U + j, j, n - 1)
    for j in range(U):
        settle((n - 1) * U + j, j, n - 1)


class PoolJobs:

    def __init__(self, st, nc, c, S, width=D):
        self.c, self.S = c, S

        def sb(name, shape, dt):
            return [st.enter_context(nc.sbuf_tensor(f"{S.tag}_{name}{j}", shape, dt)) for j in range(c.d.U)]
        self.ix, self.val = sb("pj_ix", [P, K4], I32), sb("pj_val", [P, K4], I32)
        self.got = sb("pj_got", [P, K4], I32)
        self.ring = sb("pj_ring", [P, K4, width], F32)
        self.base, self.ixs = [0] * c.d.U, 0

    def gate(self, pool):
        pool.sem_inc(self.S("pool_pass"), 1)

    def stage(self, pool, out_in, m):
        S, n = self.S, len(out_in)
        for out, src in out_in:
            pool.tensor_copy(out[:], chunk(src, m, K4)).then_inc(S("pj_ix"), 1)
        pool.wait_ge(S("pj_ix"), m * n + n + self.ixs)
        self.gate(pool)

    def landed(self, pool, j, r, each):
        pool.wait_ge(self.S(f"slot{j}"), r * each + each + self.base[j])
        self.gate(pool)

    def finish(self, copies, each):
        U, n = self.c.d.U, self.c.d.EM // self.c.d.U
        self.ixs += copies * self.c.d.EM
        for j in range(U):
            self.base[j] += n * each

    def slots_out(self, pool):
        c, S, d = self.c, self.S, self.c.d

        def issue(m, j):
            self.stage(pool, ((self.ix[j], c.canonI), (self.val[j], c.slotI)), m)
            for k in range(K4):
                pool.indirect_dma_start(out=c.POS, out_offset=bass.IndirectOffsetOnAxis(ap=self.ix[j][:, k:k + 1], axis=0),
                                        in_=self.val[j][:, k:k + 1], in_offset=None, bounds_check=d.N - 1,
                                        oob_is_err=False).then_inc(S(f"slot{j}"), 16)
        pool_alone(pool, c, issue, lambda m, j, r: None, lambda m, j, r: self.landed(pool, j, r, 64))
        self.finish(2, 64)

    def slots_in(self, pool, tmp):
        c, S = self.c, self.S

        def issue(m, j):
            self.stage(pool, ((self.ix[j], c.idxS),), m)
            for k in range(K4):
                pool.indirect_dma_start(out=self.got[j][:, k:k + 1], out_offset=None, in_=c.POS,
                                        in_offset=bass.IndirectOffsetOnAxis(ap=self.ix[j][:, k:k + 1], axis=0)
                                        ).then_inc(S(f"slot{j}"), 16)

        def take(m, j, r):
            self.landed(pool, j, r, 64)
            pool.tensor_copy(chunk(tmp, m, K4), self.got[j][:]).then_inc(S("pj_taken"), 1)

        def settle(m, j, r):
            pool.wait_ge(S("pj_taken"), m + 1)
            self.gate(pool)
        pool_alone(pool, c, issue, take, settle)
        self.finish(1, 64)
        pool.tensor_copy(c.idxS[:], tmp[:]).then_inc(S("pj_slots"), 1)
        pool.wait_ge(S("pj_slots"), 1)
        self.gate(pool)

    def dst_rows(self, pool, table, target):
        c, S = self.c, self.S

        def issue(m, j):
            self.stage(pool, ((self.ix[j], c.idxD),), m)
            for k in range(K4):
                pool.indirect_dma_start(out=self.ring[j][:, k, :], out_offset=None, in_=table,
                                        in_offset=bass.IndirectOffsetOnAxis(ap=self.ix[j][:, k:k + 1], axis=0)
                                        ).then_inc(S(f"slot{j}"), 16)

        def take(m, j, r):
            pool.wait_ge(S(f"slot{j}"), r * 80 + 64 + self.base[j])
            self.gate(pool)
            pool.dma_start(edge_rows(target, m), self.ring[j][:]).then_inc(S(f"slot{j}"), 16)
        pool_alone(pool, c, issue, take, lambda m, j, r: self.landed(pool, j, r, 80))
        self.finish(1, 80)


def nodes_gat(nc, c, x):
    d, S = c.d, Signals(nc, "gatn")
    N, NM = d.N, d.NM
    with ExitStack() as st:
        def each(name, shape, dt=F32):
            return [st.enter_context(nc.sbuf_tensor(f"{S.tag}_{name}{i}", shape, dt)) for i in range(FLY)]
        xin, xb, r = each("xin", [P, K4, D]), each("xb", [P, K4, D]), each("r", [P, K4, D])
        rT, x0T = each("rT", [P, MAC]), each("x0T", [P, MAC])
        r1, r1T = r, rT
        hT = [None, each("h1T", [P, MAC]), each("h2T", [P, MAC])]
        hT.append(hT[1])
        hp = [each(f"hp{l}_", [P, K4, c.TW[l]]) for l in range(6)]
        x1 = xb
        x1b = x2 = each("x2", [P, K4, D])
        tmp = st.enter_context(nc.sbuf_tensor(f"{S.tag}_tmp", [P, d.ET], I32))
        jobs = PoolJobs(st, nc, c, S)
        ln0, ln1 = Norm(st, nc, S, "ln0", FLY), Norm(st, nc, S, "ln1", FLY)
        psR = [st.enter_context(nc.psum_tensor(f"{S.tag}_psR{i}", [P, MAC], F32)) for i in range(FLY)]
        psT = [st.enter_context(nc.psum_tensor(f"{S.tag}_psT{i}", [P, MAC], F32)) for i in range(FLY)]
        block = st.enter_context(nc.Block())

        def k4(q):
            return q[:].rearrange("p (k f) -> p k f", k=K4)

        def ext(q, n):
            return q[:, 0:K4 * n].rearrange("p (k f) -> p k f", k=K4)

        def row(t_, n=D):
            return t_[:].unsqueeze(1).broadcast_to([P, K4, n])

        @block.gpsimd
        def _(pool):
            jobs.slots_out(pool)
            jobs.slots_in(pool, tmp)
            jobs.dst_rows(pool, x, c.XD)

        @block.sync
        def _(sp):
            def load(gb):
                for g, b in gb:
                    sp.wait_ge(S("xb"), g + 1)
                    sp.sem_inc(S("sp_pass"), 1)
                    sp.dma_start(xin[b][:], node_rows(x, g, N)).then_inc(S(f"x_load{b}"), 16)

            def first_out(gb):
                for g, b in gb:
                    sp.wait_ge(S("hp0"), g + 1)
                    store_rows(sp, S, NM, 1, node_rows(c.HP[0][0:N, :], g, N), g, b, hp[0][b][:], 1, "first_out")

            def table(gb, n, ready, buf, t):
                for g, b in gb:
                    sp.wait_ge(S(ready), g + 1)
                    store_rows(sp, S, NM, n, node_rows(t, g, N), g, b, buf[b][:], 6, "st")

            def body(gb, ahead, after):
                table(gb, 1, "hp1", hp[1], c.HP[1][0:N, :])
                table(gb, 2, "hp2", hp[2], c.HP[2][0:N, :])
                for g, b in gb:
                    sp.wait_ge(S(f"first_out{b}"), (g - b) * (16 // FLY) + 16)
                    sp.sem_inc(S("hp0_free"), 1)
                table(gb, 3, "hp3", hp[3], c.HP[3][0:N, :])
                table(gb, 4, "hp4", hp[4], c.HP[4][0:N, :])
                first_out(ahead)
                load(after)
                table(gb, 5, "hp5", hp[5], c.HP[5][0:N, :])
                table(gb, 6, "x2", x2, c.X2)
                for g, b in gb:
                    sp.wait_ge(S(f"st{b}"), (g - b) * (96 // FLY) + 96)
                    sp.sem_inc(S("rows_free"), 1)
            load(node_group(NM, 0))
            load(node_group(NM, 1))
            first_out(node_group(NM, 0))
            node_groups_two_ahead(sp, NM, body)

        @block.vector
        def _(v):
            v.sem_inc(S("xb"), FLY)
            v.sem_inc(S("hp5_used"), FLY)

            def loaded(gb):
                for g, b in gb:
                    v.wait_ge(S(f"x_load{b}"), (g - b) * (16 // FLY) + 16)

            def leaky(gb, l):
                for g, b in gb:
                    v.wait_ge(S(f"z{l}"), g + 1)
                    v.scalar_tensor_tensor(out=hT[l][b][:], in0=hT[l][b][:], scalar=0.01, in1=hT[l][b][:],
                                           op0=ALU.mult, op1=ALU.max).then_inc(S(f"h{l}"), 1)

            def residual(gb, follows):
                for g, b in gb:
                    v.wait_ge(S("r"), g + 1)
                    if follows:
                        v.wait_ge(S("r1"), g + 1 - FLY)
                        v.wait_ge(S("x1b"), g + 1 - FLY)
                    v.tensor_tensor(xb[b][:], xin[b][:], row(c.b4row), ALU.add).then_inc(S("xb"), 1)

            def norm_first(gb):
                loaded(gb)
                for g, b in gb:
                    ln0.stats(v, b, g, xin[b])
                for step in (ln0.moments, ln0.variance):
                    for g, b in gb:
                        step(v, b, g)

            def norm_last(gb):
                for step in (ln0.recip, ln0.shift):
                    for g, b in gb:
                        step(v, b, g)

            def body(gb, ahead, after):
                leaky(gb, 1)
                norm_first(ahead)
                norm_last(ahead)
                leaky(gb, 2)
                leaky(gb, 3)
                for some in (gb[:2], gb[2:]):
                    for g, b in some:
                        v.wait_ge(S("hp4"), g + 1)
                        v.wait_ge(S("xb"), g + 1 + FLY)
                        v.tensor_tensor(x1[b][:], hp[4][b][:, :, 0:D], xb[b][:], ALU.add).then_inc(S("x1"), 1)
                    if some:
                        v.wait_ge(S("x1"), some[-1][0] + 1)
                        ln1.vector(v, some, x1)
                for g, b in gb:
                    v.tensor_tensor(x1b[b][:], x1[b][:], row(c.b5row), ALU.add).then_inc(S("x1b"), 1)
                residual(ahead, True)
                for g, b in gb:
                    v.wait_ge(S("rows5"), g + 1)
                    v.tensor_tensor(hp[5][b][:, :, 0:D], k4(psR[b]), row(c.blin[:, 0:D]), ALU.add)
                    v.tensor_tensor(hp[5][b][:, :, D:D + 8], ext(psT[b], 8), c.blin[:, D:D + 8].unsqueeze(1).broadcast_to([P, K4, 8]),
                                    ALU.add).then_inc(S("hp5"), 1)
                for g, b in gb:
                    v.wait_ge(S("hp5"), g + 1)
                    v.sem_inc(S("hp5_used"), 1)
                    v.wait_ge(S("x1b"), g + 1)
                    v.tensor_tensor(x2[b][:], hp[5][b][:, :, 0:D], x1b[b][:], ALU.add).then_inc(S("x2"), 1)
            norm_first(node_group(NM, 0))
            norm_last(node_group(NM, 0))
            residual(node_group(NM, 0), False)
            node_groups_two_ahead(v, NM, body)

        @block.scalar
        def _(act):
            act.sem_inc(S("rows_free"), FLY)
            act.sem_inc(S("hp0_free"), FLY)

            def copies(gb, out, src, ready, done):
                for g, b in gb:
                    act.wait_ge(S(ready), g + 1)
                    act.activation(out[b][:], src[b][:], ACT.Copy).then_inc(S(done), 1)

            def row_copy(g, b, l):
                act.wait_ge(S(f"rows{l}"), g + 1)
                act.activation(hp[l][b][:, :, 0:D], k4(psR[b]), ACT.Copy)
                act.activation(hp[l][b][:, :, D:D + 2], ext(psT[b], 2), ACT.Copy).then_inc(S(f"hp{l}"), 1)

            def hidden(gb, l):
                for g, b in gb:
                    act.wait_ge(S(f"mid{l}"), g + 1)
                    act.activation(hT[l][b][:], psT[b][:], ACT.Identity, bias=c.bm[:, l - 1:l]).then_inc(S(f"z{l}"), 1)

            def first_rows(gb):
                for g, b in gb:
                    act.wait_ge(S("x0Tp"), g + 1)
                    act.activation(x0T[b][:], psT[b][:], ACT.Identity, bias=c.b0col[:]).then_inc(S("x0T"), 1)

            def body(gb, ahead, after):
                hidden(gb, 1)
                act.wait_ge(S("rows_free"), gb[-1][0] + 1)
                for g, b in gb:
                    row_copy(g, b, 1)
                for g, b in ahead:
                    ln0.root(act, b, g)
                hidden(gb, 2)
                for g, b in gb:
                    row_copy(g, b, 2)
                    if b < len(ahead):
                        ln0.apply(act, b, ahead[b][0], r[b], xin[b], S("r"))
                hidden(gb, 3)
                for g, b in gb:
                    row_copy(g, b, 3)
                copies(ahead, rT, psT, "rTp", "rT")
                for g, b in gb[:3]:
                    row_copy(g, b, 4)
                for g, b in gb[:2]:
                    ln1.root(act, b, g)
                for g, b in gb[3:]:
                    row_copy(g, b, 4)
                first_rows(ahead)
                for g, b in gb[2:]:
                    ln1.root(act, b, g)
                if ahead:
                    act.wait_ge(S("hp0_free"), ahead[-1][0] + 1)
                for g, b in gb:
                    ln1.apply(act, b, g, r1[b], x1[b], S("r1"))
                    if b < len(ahead):
                        row_copy(ahead[b][0], b, 0)
                copies(gb, r1T, psT, "r1Tp", "r1T")
            for g, b in node_group(NM, 0):
                ln0.root(act, b, g)
            for g, b in node_group(NM, 0):
                ln0.apply(act, b, g, r[b], xin[b], S("r"))
            copies(node_group(NM, 0), rT, psT, "rTp", "rT")
            first_rows(node_group(NM, 0))
            act.wait_ge(S("hp0_free"), node_group(NM, 0)[-1][0] + 1)
            for g, b in node_group(NM, 0):
                row_copy(g, b, 0)
            node_groups_two_ahead(act, NM, body)

        @block.tensor
        def _(pe):
            def project(g, b, src, w, n, done):
                for k in range(K4):
                    pe.matmul(k4(psR[b])[:, k, :], src[b][:, k * P:(k + 1) * P], w[:, 0:D], start=True, stop=True)
                    last = pe.matmul(ext(psT[b], n)[:, k, :], src[b][:, k * P:(k + 1) * P], w[:, D:D + n], start=True, stop=True)
                last.then_inc(S(done), 1)

            def first_turn(gb, follows):
                for g, b in gb:
                    pe.wait_ge(S("r"), g + 1)
                    if follows:
                        pe.wait_ge(S("hp3"), g + 1 - FLY)
                    turn(pe, psT[b], r[b], c.ident[:], S("rTp"))

            def first_layer(gb, follows):
                for g, b in gb:
                    pe.wait_ge(S("rT"), g + 1)
                    if follows:
                        pe.wait_ge(S("hp4"), g + 1 - FLY)
                    pe.matmul(psT[b][:], c.W0[:, 0, 0:D], rT[b][:], start=True, stop=True).then_inc(S("x0Tp"), 1)
                for g, b in gb:
                    pe.wait_ge(S("x0T"), g + 1)
                    project(g, b, rT, c.W0[:, 0, :], 2, "rows0")

            def body(gb, ahead, after):
                for l in (1, 2, 3):
                    for g, b in gb:
                        if l == 1:
                            pe.wait_ge(S("hp0"), g + 1)
                            pe.wait_ge(S("hp5_used"), g + 1)
                            pe.matmul(psT[b][:], c.WM[:, 0, :], x0T[b][:], start=True, stop=True).then_inc(S("mid1"), 1)
                        else:
                            pe.wait_ge(S(f"h{l - 1}"), g + 1)
                            pe.wait_ge(S(f"hp{l - 1}"), g + 1)
                            pe.matmul(psT[b][:], c.AM[:, l - 1, :], x0T[b][:], start=True, stop=False)
                            pe.matmul(psT[b][:], c.WM[:, l - 1, :], hT[l - 1][b][:], start=False, stop=True).then_inc(S(f"mid{l}"), 1)
                    for g, b in gb:
                        pe.wait_ge(S(f"z{l}"), g + 1)
                        project(g, b, x0T if l == 1 else hT[l - 1], c.W0[:, l, :], 2, f"rows{l}")
                first_turn(ahead, True)
                for g, b in gb:
                    pe.wait_ge(S("h3"), g + 1)
                    if b < len(ahead):
                        pe.wait_ge(S("rT"), ahead[b][0] + 1)
                    pe.wait_ge(S("hp3"), g + 1)
                    project(g, b, hT[3], c.W0[:, 4, :], 2, "rows4")
                first_layer(ahead, True)
                for g, b in gb:
                    pe.wait_ge(S("r1"), g + 1)
                    if b < len(ahead):
                        pe.wait_ge(S("hp0"), ahead[b][0] + 1)
                    pe.wait_ge(S("hp4"), g + 1)
                    turn(pe, psT[b], r1[b], c.ident[:], S("r1Tp"))
                for g, b in gb:
                    pe.wait_ge(S("r1T"), g + 1)
                    project(g, b, r1T, c.W5[:], 8, "rows5")
            first_turn(node_group(NM, 0), False)
            first_layer(node_group(NM, 0), False)
            node_groups_two_ahead(pe, NM, body)
    S.end()


class Runs:

    def __init__(self, st, nc, c, S):
        self.c, self.S = c, S
        self.low = st.enter_context(nc.sbuf_tensor(f"{S.tag}_low", [4, c.d.QP + 1], F32))
        self.zero = st.enter_context(nc.sbuf_tensor(f"{S.tag}_zero", [4, c.d.QP + 1], F32))
        self.back = st.enter_context(nc.sbuf_tensor(f"{S.tag}_back", [4, c.d.QP + 1], F32))
        self.psE = st.enter_context(nc.psum_tensor(f"{S.tag}_psE", [P, 512], F32))
        self.psC = st.enter_context(nc.psum_tensor(f"{S.tag}_psC", [P, 512], F32))

    def start(self, v):
        S = self.S
        v.memset(self.low[:], -BIG)
        v.memset(self.zero[:], 0.0)
        v.memset(self.back[:], 0.0).then_inc(S("edges_set"), 1)
        v.wait_ge(S("edges_set"), 1)

    def parts(self, kind):
        c, q = self.c, self.c.d.QP
        if kind == "sum":
            return c.contF, c.wholeF, c.runF, self.zero, 0.0, ALU.mult, ALU.add
        if kind == "max":
            return c.negF, c.negWholeF, c.negRunF, self.low, -BIG, ALU.add, ALU.max
        return c.contB, c.wholeB, c.runB, self.back, 0.0, ALU.mult, ALU.add

    def vector(self, v, name, kind, heads, out, vals):
        S, q = self.S, self.c.d.QP
        cont, whole, run, ends, init, op0, op1 = self.parts(kind)
        a = cont[0:q, 0:heads, :].rearrange("q h j -> q (h j)")
        o, x = out[0:q].rearrange("q h j -> q (h j)"), vals[0:q].rearrange("q h j -> q (h j)")
        if kind == "spread":
            v.tensor_tensor_scan(o[:, ::-1], a[:, ::-1], x[:, ::-1], init, op0, op1).then_inc(S(name + "_y"), 1)
            v.wait_ge(S(name + "_end"), 1)
            v.tensor_tensor_scan(ends[0:heads, 0:q][:, ::-1], whole[0:heads, :][:, ::-1], self.psE[0:heads, 0:q][:, ::-1],
                                 init, op0, op1).then_inc(S(name + "_c"), 1)
        else:
            v.tensor_tensor_scan(o, a, x, init, op0, op1).then_inc(S(name + "_y"), 1)
            v.wait_ge(S(name + "_end"), 1)
            v.tensor_tensor_scan(ends[0:heads, 1:q + 1], whole[0:heads, :], self.psE[0:heads, 0:q],
                                 init, op0, op1).then_inc(S(name + "_c"), 1)
        v.wait_ge(S(name + "_carry"), 1)
        for h in range(heads):
            last = v.scalar_tensor_tensor(out=out[0:q, h, :], in0=run[0:q, :], scalar=self.psC[0:q, h:h + 1],
                                          in1=out[0:q, h, :], op0=op0, op1=op1)
        last.then_inc(S(name), 1)
        v.wait_ge(S(name), 1)

    def tensor(self, pe, name, kind, heads, out):
        S, q, c = self.S, self.c.d.QP, self.c
        ends = self.parts(kind)[3]
        pe.wait_ge(S(name + "_y"), 1)
        edge = 0 if kind == "spread" else 255
        pe.transpose(self.psE[0:heads, 0:q], out[0:q, 0:heads, edge], c.ident[0:q, 0:q]).then_inc(S(name + "_end"), 1)
        pe.wait_ge(S(name + "_c"), 1)
        carried = ends[0:heads, 1:q + 1] if kind == "spread" else ends[0:heads, 0:q]
        pe.transpose(self.psC[0:q, 0:heads], carried, c.ident[0:heads, 0:heads]).then_inc(S(name + "_carry"), 1)


def edge_degrees(nc, c):
    d, S = c.d, Signals(nc, "degrees")
    q = d.QP
    with ExitStack() as st:
        def sb(name, h=1):
            return st.enter_context(nc.sbuf_tensor(f"{S.tag}_{name}", [P, h, 256], F32))
        one, deg, dl, deg_all, inv = sb("one"), sb("deg"), sb("dl"), sb("deg_all"), sb("inv")
        esum = [sb(f"esum{l}") for l in range(5)]
        runs = Runs(st, nc, c, S)
        ps = st.enter_context(nc.psum_tensor(f"{S.tag}_ps", [P, 2, P], F32))
        block = st.enter_context(nc.Block())

        @block.vector
        def _(v):
            runs.start(v)
            v.memset(one[:], 1.0).then_inc(S("one"), 1)
            v.wait_ge(S("one"), 1)
            runs.vector(v, "deg", "sum", 1, deg, one)
            v.tensor_tensor(dl[0:q, 0, :], deg[0:q, 0, :], c.last[0:q], ALU.mult).then_inc(S("dl"), 1)
            v.wait_ge(S("dl"), 1)
            runs.vector(v, "deg_all", "spread", 1, deg_all, dl)
            v.reciprocal(inv[0:q], deg_all[0:q]).then_inc(S("inv"), 1)
            v.wait_ge(S("inv"), 1)
            for l in range(5):
                runs.vector(v, f"esum{l}", "sum", 1, esum[l], c.EL[:, l:l + 1, :])
                v.tensor_tensor(c.loopEL[0:q, l, :], esum[l][0:q, 0, :], inv[0:q, 0, :], ALU.mult).then_inc(S("loop"), 1)
            v.wait_ge(S("inv_cols"), 1)
            for j in range(2):
                last = v.tensor_copy(c.invdeg[:, j::2], ps[:, j, 0:q])
            last.then_inc(S("invdeg"), 1)

        @block.tensor
        def _(pe):
            runs.tensor(pe, "deg", "sum", 1, deg)
            runs.tensor(pe, "deg_all", "spread", 1, deg_all)
            for l in range(5):
                runs.tensor(pe, f"esum{l}", "sum", 1, esum[l])
            pe.wait_ge(S("inv"), 1)
            for j in range(2):
                last = pe.transpose(ps[:, j, 0:q], inv[0:q, 0, j * P:(j + 1) * P], c.ident[0:q, 0:q])
            last.then_inc(S("inv_cols"), 1)
    S.end()


class Gather:

    def __init__(self, st, nc, c, S, width, dt=F32):
        self.c, self.S, self.U = c, S, c.d.U
        self.ring = [st.enter_context(nc.sbuf_tensor(f"{S.tag}_ring{j}", [P, K4, width], dt)) for j in range(self.U)]
        self.ix = [st.enter_context(nc.sbuf_tensor(f"{S.tag}_ix{j}", [P, K4], I32)) for j in range(self.U)]

    def rows(self, pool, table, idx):
        S, U = self.S, self.U
        pool.sem_inc(S("ring_free"), U)
        with pool.Fori(0, self.c.d.EM // U) as i:
            for j in range(U):
                m = i * U + j
                pool.wait_ge(S("ring_free"), m + 1)
                pool.sem_inc(S("pool_pass"), 1)
                pool.tensor_copy(self.ix[j][:], chunk(idx, m, K4)).then_inc(S("ix"), 1)
                pool.wait_ge(S("ix"), m + 1)
                pool.sem_inc(S("pool_pass"), 1)
                for k in range(K4):
                    pool.indirect_dma_start(out=self.ring[j][:, k, :], out_offset=None, in_=table,
                                            in_offset=bass.IndirectOffsetOnAxis(ap=self.ix[j][:, k:k + 1], axis=0)
                                            ).then_inc(S(f"slot{j}"), 16)

    def each(self, eng, use):
        with eng.Fori(0, self.c.d.EM // self.U) as i:
            for j in range(self.U):
                eng.wait_ge(self.S(f"slot{j}"), i * 64 + 64)
                use(i * self.U + j, j)


def rows_of_dst(nc, c, tag, table, target, scores=False):
    d, S = c.d, Signals(nc, tag)
    with ExitStack() as st:
        g = Gather(st, nc, c, S, table.shape[1])
        block = st.enter_context(nc.Block())

        @block.gpsimd
        def _(pool):
            g.rows(pool, table, c.idxD)

        @block.sync
        def _(sp):
            def store(m, j):
                sp.sem_inc(S("sp_pass"), 1)
                sp.dma_start(edge_rows(target, m), g.ring[j][:]).then_inc(S(f"out{j}"), 16)
            g.each(sp, store)

        @block.vector
        def _(v):
            def use(m, j):
                if scores:
                    v.tensor_copy(chunk(c.SL, m, K4), g.ring[j][:, :, D])
                    v.tensor_copy(chunk(c.SD, m, K4), g.ring[j][:, :, D + 1]).then_inc(S("cols"), 1)
                    v.wait_ge(S("cols"), m + 1)
            with v.Fori(0, d.EM // d.U) as i:
                for j in range(d.U):
                    v.wait_ge(S(f"slot{j}"), i * 64 + 64)
                    use(i * d.U + j, j)
                    v.wait_ge(S(f"out{j}"), i * 16 + 16)
                    v.sem_inc(S("ring_free"), 1)
    S.end()


def gather_sources(nc, c, l):
    d, S = c.d, Signals(nc, f"src{l}")
    H = 4 if l == 5 else 1
    with ExitStack() as st:
        g = Gather(st, nc, c, S, c.TW[l])
        block = st.enter_context(nc.Block())

        @block.gpsimd
        def _(pool):
            g.rows(pool, c.HP[l], c.idxS)

        @block.scalar
        def _(act):
            g.each(act, lambda m, j: act.activation(chunk(c.G, m, MAC).rearrange("p (k f) -> p k f", k=K4),
                                                    g.ring[j][:, :, 0:D], ACT.Copy).then_inc(S("g_copied"), 1))

        @block.vector
        def _(v):
            def use(m, j):
                v.tensor_copy(chunk(c.SS, m, K4 * H).rearrange("p (k h) -> p k h", h=H),
                              g.ring[j][:, :, D:D + H]).then_inc(S("s_copied"), 1)
                v.wait_ge(S("s_copied"), m + 1)
                v.wait_ge(S("g_copied"), m + 1)
                v.sem_inc(S("ring_free"), 1)
            g.each(v, use)
    S.end()


def attention(nc, c, l):
    d, S = c.d, Signals(nc, f"att{l}")
    H = 4 if l == 5 else 1
    q = d.QP
    with ExitStack() as st:
        def sb(name):
            return st.enter_context(nc.sbuf_tensor(f"{S.tag}_{name}", [P, H, 256], F32))
        s, sf, u, y, z = sb("s"), sb("sf"), sb("u"), sb("y"), sb("z")
        runs = Runs(st, nc, c, S)
        psS, psD, psL = (st.enter_context(nc.psum_tensor(f"{S.tag}_ps{n}", [P, H * 2, P], F32)) for n in "SDL")
        if H == 1:
            pad = st.enter_context(nc.psum_tensor(f"{S.tag}_pad", [P, 2, P], F32))
        block = st.enter_context(nc.Block())

        def rowsv(p):
            return p[0:q].rearrange("q (h j) e -> q h (j e)", h=H)

        def heads(t):
            return t[0:q].unsqueeze(1).broadcast_to([q, H, 256])

        def cols(t):
            return t[:, 0:d.ET * H].rearrange("p (t h) -> p t h", h=H)

        @block.tensor
        def _(pe):
            for ps, t in ((psD, c.SD), (psS, c.SS), (psL, c.SL)):
                for h in range(H):
                    for j in range(2):
                        last = pe.transpose(ps[0:q, h * 2 + j, :], cols(t)[:, j::2, h], c.ident[:])
                last.then_inc(S("turned"), 1)
            runs.tensor(pe, "d_all", "spread", H, z)
            runs.tensor(pe, "m", "max", H, y)
            runs.tensor(pe, "m_all", "spread", H, z)
            runs.tensor(pe, "den", "sum", H, y)
            runs.tensor(pe, "den_all", "spread", H, z)
            for ps, t in ((psS, s), (psD, sf)):
                pe.wait_ge(S("weights"), 1)
                for h in range(H):
                    for j in range(2):
                        last = pe.transpose(ps[:, h * 2 + j, 0:q], t[0:q, h, j * P:(j + 1) * P], c.ident[0:q, 0:q])
                last.then_inc(S("turned_back"), 1)

        @block.scalar
        def _(act):
            act.wait_ge(S("s_less"), 1)
            act.activation(s[0:q], s[0:q], ACT.Exp).then_inc(S("exp"), 1)
            act.wait_ge(S("sf_less"), 1)
            act.activation(sf[0:q], sf[0:q], ACT.Exp).then_inc(S("exp"), 1)

        @block.vector
        def _(v):
            n = [0]

            def then(ins):
                n[0] += 1
                ins.then_inc(S("step"), 1)
                v.wait_ge(S("step"), n[0])

            runs.start(v)
            v.wait_ge(S("turned"), 3)
            then(v.tensor_tensor(u[0:q], rowsv(psD), heads(c.last), ALU.mult))
            runs.vector(v, "d_all", "spread", H, z, u)
            then(v.tensor_tensor(s[0:q], z[0:q], rowsv(psS), ALU.add))
            then(v.tensor_tensor(sf[0:q], rowsv(psL), heads(c.negLast), ALU.add))
            then(v.tensor_tensor(sf[0:q], sf[0:q], rowsv(psD), ALU.add))
            if H == 1:
                then(v.tensor_tensor(s[0:q, 0, :], s[0:q, 0, :], c.EL[0:q, l, :], ALU.add))
                then(v.tensor_tensor(sf[0:q, 0, :], sf[0:q, 0, :], c.loopEL[0:q, l, :], ALU.add))
            for t in (s, sf):
                then(v.scalar_tensor_tensor(out=t[0:q], in0=t[0:q], scalar=0.2, in1=t[0:q], op0=ALU.mult, op1=ALU.max))
            then(v.tensor_tensor(u[0:q], s[0:q], sf[0:q], ALU.max))
            runs.vector(v, "m", "max", H, y, u)
            then(v.tensor_tensor(u[0:q], y[0:q], heads(c.last), ALU.mult))
            runs.vector(v, "m_all", "spread", H, z, u)
            v.tensor_tensor(s[0:q], s[0:q], z[0:q], ALU.subtract).then_inc(S("s_less"), 1)
            v.tensor_tensor(sf[0:q], sf[0:q], z[0:q], ALU.subtract).then_inc(S("sf_less"), 1)
            v.wait_ge(S("exp"), 2)
            then(v.tensor_tensor(u[0:q], s[0:q], sf[0:q], ALU.add))
            runs.vector(v, "den", "sum", H, y, u)
            then(v.tensor_tensor(u[0:q], y[0:q], heads(c.last), ALU.mult))
            runs.vector(v, "den_all", "spread", H, z, u)
            then(v.reciprocal(u[0:q], z[0:q]))
            v.tensor_tensor(s[0:q], s[0:q], u[0:q], ALU.mult)
            v.tensor_tensor(sf[0:q], sf[0:q], u[0:q], ALU.mult).then_inc(S("weights"), 1)
            v.wait_ge(S("turned_back"), 2)
            for ps, t in ((psS, c.AL), (psD, c.AF)):
                for h in range(H):
                    for j in range(2):
                        v.tensor_copy(cols(t)[:, j::2, h], ps[:, h * 2 + j, 0:q])
    S.end()


def pairs_ahead(eng, count, body):
    even = count // 2 * 2
    if even > 2:
        with eng.Fori(0, even // 2 - 1) as i:
            body(i * 2, (0, 1), (0, 1))
    if even:
        body(even - 2, (0, 1), tuple(range(count - even)))
    if count - even:
        body(even, (0,), ())


def gat_messages(nc, c, l):
    d, S = c.d, Signals(nc, f"msg{l}")
    H = 4 if l == 5 else 1
    TW = c.TW[l]
    with ExitStack() as st:
        def two(name, shape, dt=F32):
            return [st.enter_context(nc.sbuf_tensor(f"{S.tag}_{name}{i}", shape, dt)) for i in range(2)]

        def bank(name, shape):
            return [st.enter_context(nc.psum_tensor(f"{S.tag}_{name}{i}", shape, F32)) for i in range(2)]
        same, carried = two("same", [P, MAC], U8), two("carried", [P, MAC], U8)
        hd, s32 = two("hd", [P, K4, TW]), two("s32", [P, MAC])
        gw, hw, agg = two("gw", [P, MAC]), two("hw", [P, MAC]), two("agg", [P, MAC])
        extra = two("extra", [P, MAC])
        mix, z = two("mix", [P, MAC]), two("z", [P, MAC])
        hT = extra if l == 4 else z
        rows = two("rows", [P, K4, D + 8])
        ix = two("ix", [P, K4], I32)
        scrap = two("scrap", [P, 1])
        psA, psM, psR = bank("psA", [P, MAC]), bank("psM", [P, MAC]), bank("psR", [P, K4, 256])
        ln = Norm(st, nc, S, "ln", 2) if l == 4 else None
        block = st.enter_context(nc.Block())
        NW = 0 if l == 5 else (c.TW[l + 1])
        W_next = None if l == 5 else (c.W5[:] if l == 4 else c.W0[:, l + 1, :])
        extra_used = "mixed" if l < 4 else "projected" if l == 4 else "x_sum"

        def k4(t):
            return t[:].rearrange("p (k f) -> p k f", k=K4)

        def loaded(eng, what, g, b):
            eng.wait_ge(S(f"{what}_in{b}"), (g - b) * 8 + 16)

        @block.sync
        def _(sp):
            def fetch(what, buf, src, free, g, b):
                sp.wait_ge(S(free), g + 1)
                sp.sem_inc(S("sp_pass"), 1)
                sp.dma_start(buf, src).then_inc(S(f"{what}_in{b}"), 16)

            def early(m, pars):
                for b in pars:
                    g = m + b
                    fetch("same", same[b][:], chunk(c.SF, g * 2, MAC), "s32", g, b)
                    fetch("hd", hd[b][:], edge_rows(c.HP[l][d.N:, :], g), "hw", g, b)

            def late(m, pars):
                for b in pars:
                    g = m + b
                    fetch("carried", carried[b][:], chunk(c.SF, g * 2 + 1, MAC), "agg3", g, b)

            def body(m, pars, ahead):
                early(m + 2, ahead)
                for b in pars:
                    g = m + b
                    if 1 <= l <= 3:
                        fetch("extra", extra[b][:], chunk(c.X0T, g, MAC), extra_used, g, b)
                    if l >= 4:
                        fetch("extra", k4(extra[b]), edge_rows(c.XD, g), extra_used, g, b)
                late(m + 2, ahead)
            early(0, tuple(range(min(2, d.EM))))
            late(0, tuple(range(min(2, d.EM))))
            pairs_ahead(sp, d.EM, body)

        @block.gpsimd
        def _(pool):
            def weigh(m, pars):
                for b in pars:
                    g = m + b
                    pool.wait_ge(S("msg"), g + 1)
                    pool.tensor_tensor(gw[b][:].rearrange("p (a f) -> p a f", f=D // H),
                                       chunk(c.G, g, MAC).rearrange("p (a f) -> p a f", f=D // H),
                                       chunk(c.AL, g, K4 * H).unsqueeze(2).broadcast_to([P, K4 * H, D // H]),
                                       ALU.mult).then_inc(S("gw"), 1)

            def body(m, pars, ahead):
                weigh(m + 2, ahead)
                if l == 5:
                    for b in pars:
                        g = m + b
                        pool.wait_ge(S("x_sum"), g + 3)
                        pool.wait_ge(S(f"put{b}"), (g - b) * 32 + 16)
                        pool.sem_inc(S("pool_pass"), 1)
                        pool.tensor_copy(ix[b][:], chunk(c.canonI, g, K4)).then_inc(S("ix"), 1)
                        pool.wait_ge(S("ix"), g + 1)
                        pool.sem_inc(S("pool_pass"), 1)
                        for k in range(K4):
                            pool.indirect_dma_start(out=c.X2, out_offset=bass.IndirectOffsetOnAxis(ap=ix[b][:, k:k + 1], axis=0),
                                                    in_=mix[b][:, k * P:(k + 1) * P], in_offset=None, bounds_check=d.N - 1,
                                                    oob_is_err=False).then_inc(S(f"put{b}"), 16)
            if l == 5:
                for b in range(2):
                    pool.dma_start(scrap[b][:], c.ident[:, 0:1]).then_inc(S(f"put{b}"), 16)
            weigh(0, tuple(range(min(2, d.EM))))
            pairs_ahead(pool, d.EM, body)
            if l == 5:
                for b in range(2):
                    pool.wait_ge(S(f"put{b}"), 16 + 64 * ((d.EM + 1 - b) // 2))

        @block.vector
        def _(v):
            v.sem_inc(S("hw"), 2)
            v.sem_inc(S("agg3"), 1)
            if l:
                v.sem_inc(S("mixed" if l < 4 else "x_sum"), 2)
            else:
                v.sem_inc(S("x0"), 2)
            v.sem_inc(S("cols"), 2)
            v.memset(agg[1][:, MAC - 1:MAC], 0.0).then_inc(S("agg3"), 1)

            def own_rows(m, pars):
                for b in pars:
                    g = m + b
                    loaded(v, "hd", g, b)
                    v.wait_ge(S("msg"), g + 1)
                    v.tensor_tensor(hw[b][:].rearrange("p (a f) -> p a f", f=D // H),
                                    hd[b][:, :, 0:D].rearrange("p k (h f) -> p k h f", h=H) if H > 1 else hd[b][:, :, 0:D],
                                    chunk(c.AF, g, K4 * H).unsqueeze(2).broadcast_to([P, K4 * H, D // H]),
                                    ALU.mult).then_inc(S("hw"), 1)

            def carry(m, pars):
                for b in pars:
                    g = m + b
                    loaded(v, "carried", g, b)
                    v.wait_ge(S("msg"), g + 3)
                    for k in range(K4):
                        v.wait_ge(S(f"agg{(k - 1) % 4}"), g + (1 if k else 2))
                        before = agg[b][:, k * P - 1:k * P] if k else agg[1 - b][:, MAC - 1:MAC]
                        v.scalar_tensor_tensor(out=agg[b][:, k * P:(k + 1) * P], in0=carried[b][:, k * P:(k + 1) * P],
                                               scalar=before, in1=psA[b][:, k * P:(k + 1) * P],
                                               op0=ALU.mult, op1=ALU.add).then_inc(S(f"agg{k}"), 1)

            def body(m, pars, ahead):
                if l >= 4:
                    own_rows(m + 2, ahead)
                for b in pars:
                    g = m + b
                    if 1 <= l:
                        loaded(v, "extra", g, b)
                    if l == 0:
                        v.wait_ge(S("agg3"), g + 3)
                        v.tensor_scalar(hT[b][:], agg[b][:], c.b0col[:], None, ALU.add).then_inc(S("x0"), 1)
                    elif l < 4:
                        v.wait_ge(S("agg3"), g + 3)
                        v.scalar_tensor_tensor(out=mix[b][:], in0=agg[b][:], scalar=1.0 - ALPHA, in1=extra[b][:],
                                               op0=ALU.mult, op1=ALU.add).then_inc(S("mixed"), 1)
                    else:
                        v.wait_ge(S("turned"), g + 1)
                        bias = c.b4row if l == 4 else c.b5row
                        if l == 4:
                            v.wait_ge(S(f"x_out{b}"), (g - b) * 8 + 16)
                        else:
                            v.wait_ge(S(f"put{b}"), (g - b) * 32 + 16)
                        v.tensor_tensor(k4(mix[b]), k4(psM[b]), bias[:].unsqueeze(1).broadcast_to([P, K4, D]), ALU.add).then_inc(S("x_bias"), 1)
                        v.wait_ge(S("x_bias"), g + 1)
                        v.tensor_tensor(mix[b][:], mix[b][:], extra[b][:], ALU.add).then_inc(S("x_sum"), 1)
                if l == 0:
                    for b in pars:
                        g = m + b
                        v.wait_ge(S("x0"), g + 3)
                        v.wait_ge(S(f"x0_out{b}"), (g - b) * 8 + 16)
                        v.tensor_scalar(mix[b][:], hT[b][:], ALPHA, None, ALU.mult).then_inc(S("x0s"), 1)
                if l < 4:
                    own_rows(m + 2, ahead)
                if 1 <= l <= 3:
                    for b in pars:
                        g = m + b
                        v.wait_ge(S("z"), g + 1)
                        v.scalar_tensor_tensor(out=hT[b][:], in0=z[b][:], scalar=0.01, in1=z[b][:],
                                               op0=ALU.mult, op1=ALU.max).then_inc(S("hT"), 1)
                if l == 4:
                    v.wait_ge(S("x_sum"), m + pars[-1] + 3)
                    ln.vector(v, [(m + b, b) for b in pars], [k4(t) for t in mix])
                carry(m + 2, ahead)
                if l == 4:
                    for b in pars:
                        g = m + b
                        v.wait_ge(S("projected"), g + 3)
                        v.wait_ge(S(f"rows_out{b}"), (g - b) * 8 + 16)
                        v.tensor_tensor(rows[b][:], psR[b][:, :, 0:D + 8], c.blin[:].unsqueeze(1).broadcast_to([P, K4, D + 8]),
                                        ALU.add).then_inc(S("rows"), 1)
                if l < 5:
                    HN = 4 if l == 4 else 1
                    for b in pars:
                        g = m + b
                        v.wait_ge(S("rows"), g + 1)
                        v.tensor_copy(chunk(c.SL, g, K4 * HN).rearrange("p (k h) -> p k h", h=HN), rows[b][:, :, D:D + HN])
                        v.tensor_copy(chunk(c.SD, g, K4 * HN).rearrange("p (k h) -> p k h", h=HN),
                                      rows[b][:, :, D + HN:D + 2 * HN]).then_inc(S("cols"), 1)
            own_rows(0, tuple(range(min(2, d.EM))))
            carry(0, tuple(range(min(2, d.EM))))
            pairs_ahead(v, d.EM, body)

        @block.scalar
        def _(act):
            act.sem_inc(S("s32"), 2)
            for b in range(2):
                for name in (["x0_out"] if l == 0 else ["x_out"] if l == 4 else []) + (["rows_out"] if l < 5 else []):
                    act.dma_start(scrap[b][:], c.ident[:, 0:1]).then_inc(S(f"{name}{b}"), 16)
                    act.wait_ge(S(f"{name}{b}"), 16)

            def widen(m, pars):
                for b in pars:
                    g = m + b
                    loaded(act, "same", g, b)
                    act.wait_ge(S("msg"), g + 1)
                    act.activation(s32[b][:], same[b][:], ACT.Copy).then_inc(S("s32"), 1)

            def body(m, pars, ahead):
                widen(m + 2, ahead)
                if l == 0:
                    for b in pars:
                        g = m + b
                        act.wait_ge(S("x0s"), g + 1)
                        act.dma_start(chunk(c.X0T, g, MAC), mix[b][:]).then_inc(S(f"x0_out{b}"), 16)
                if 1 <= l <= 3:
                    for b in pars:
                        g = m + b
                        act.wait_ge(S("mid"), g + 1)
                        act.activation(z[b][:], psM[b][:], ACT.Identity, bias=c.bm[:, l - 1:l]).then_inc(S("z"), 1)
                if l == 4:
                    for b in pars:
                        g = m + b
                        act.wait_ge(S("x_sum"), g + 3)
                        act.dma_start(edge_rows(c.XD, g), k4(mix[b])).then_inc(S(f"x_out{b}"), 16)
                    for b in pars:
                        ln.root(act, b, m + b)
                    for b in pars:
                        ln.apply(act, b, m + b, k4(z[b]), k4(mix[b]), S("r"))
                    for b in pars:
                        g = m + b
                        act.wait_ge(S("rT_ps"), g + 1)
                        act.activation(hT[b][:], psM[b][:], ACT.Copy).then_inc(S("hT"), 1)
                if l < 4:
                    for b in pars:
                        g = m + b
                        act.wait_ge(S("projected"), g + 3)
                        act.wait_ge(S("cols"), g + 1)
                        act.wait_ge(S(f"rows_out{b}"), (g - b) * 8 + 16)
                        act.activation(rows[b][:, :, 0:NW], psR[b][:, :, 0:NW], ACT.Copy).then_inc(S("rows"), 1)
                if l < 5:
                    for b in pars:
                        g = m + b
                        act.wait_ge(S("rows"), g + 1)
                        act.dma_start(edge_rows(c.HP[l + 1][d.N:, :], g), rows[b][:, :, 0:NW]).then_inc(S(f"rows_out{b}"), 16)
            widen(0, tuple(range(min(2, d.EM))))
            pairs_ahead(act, d.EM, body)
            for b in range(2):
                for name in (["x0_out"] if l == 0 else ["x_out"] if l == 4 else []) + (["rows_out"] if l < 5 else []):
                    act.wait_ge(S(f"{name}{b}"), 16 + 16 * ((d.EM + 1 - b) // 2))

        @block.tensor
        def _(pe):
            pe.sem_inc(S("msg"), 2)
            if l < 5:
                pe.sem_inc(S("projected"), 2)

            def sums(m, pars):
                for b in pars:
                    g = m + b
                    pe.wait_ge(S("gw"), g + 1)
                    pe.wait_ge(S("hw"), g + 3)
                    pe.wait_ge(S("s32"), g + 3)
                    pe.wait_ge(S("agg3"), g + 1)
                    for k in range(K4):
                        col = slice(k * P, (k + 1) * P)
                        pe.matmul(psA[b][:, col], gw[b][:, col], s32[b][:, col], start=True, stop=False)
                        last = pe.matmul(psA[b][:, col], hw[b][:, col], c.ident[:], start=False, stop=True)
                    last.then_inc(S("msg"), 1)

            def body(m, pars, ahead):
                if 1 <= l <= 3:
                    for b in pars:
                        g = m + b
                        pe.wait_ge(S("mixed"), g + 3)
                        pe.matmul(psM[b][:], c.M[:, l - 1, :], mix[b][:], start=True, stop=True).then_inc(S("mid"), 1)
                if l >= 4:
                    for b in pars:
                        g = m + b
                        pe.wait_ge(S("agg3"), g + 3)
                        turn_back(pe, k4(psM[b]), agg[b], c.ident[:], S("turned"))
                sums(m + 2, ahead)
                if l == 4:
                    for b in pars:
                        g = m + b
                        pe.wait_ge(S("r"), g + 1)
                        turn(pe, psM[b], k4(z[b]), c.ident[:], S("rT_ps"))
                if l < 5:
                    for b in pars:
                        g = m + b
                        pe.wait_ge(S("hT" if l else "x0"), g + (1 if l else 3))
                        rows_of(pe, psR[b], hT[b], W_next, S("projected"))
            sums(0, tuple(range(min(2, d.EM))))
            pairs_ahead(pe, d.EM, body)
    S.end()


def singly(body):
    return lambda m, pars: [body(m, (b,)) for b in pars]


def sum_by_source(nc, c):
    d, S = c.d, Signals(nc, "bysrc")
    with ExitStack() as st:
        def two(name, shape, dt=F32):
            return [st.enter_context(nc.sbuf_tensor(f"{S.tag}_{name}{i}", shape, dt)) for i in range(2)]
        x, r, rows = two("x", [P, K4, D]), two("r", [P, K4, D]), two("rows", [P, K4, D])
        sbc, same = two("sbc", [P, MAC]), two("same", [P, K4, MAC])
        gix, pix = two("gix", [P, K4], I32), two("pix", [P, K4], I32)
        scrap = st.enter_context(nc.sbuf_tensor(f"{S.tag}_scrap", [P, K4 + 1], F32))
        ln = Norm(st, nc, S, "ln", 2)
        ps = [st.enter_context(nc.psum_tensor(f"{S.tag}_ps{i}", [P, K4, D], F32)) for i in range(2)]
        block = st.enter_context(nc.Block())

        @block.gpsimd
        def _(pool):
            def gathers(g, b):
                pool.wait_ge(S("r"), g + 1)
                pool.sem_inc(S("pool_pass"), 1)
                pool.tensor_copy(gix[b][:], chunk(c.idxD, g, K4)).then_inc(S("gix"), 1)
                pool.wait_ge(S("gix"), g + 1)
                pool.sem_inc(S("pool_pass"), 1)
                for k in range(K4):
                    pool.indirect_dma_start(out=x[b][:, k, :], out_offset=None, in_=c.X2,
                                            in_offset=bass.IndirectOffsetOnAxis(ap=gix[b][:, k:k + 1], axis=0)
                                            ).then_inc(S(f"slot{b}"), 16)

            def adds(g, b):
                pool.wait_ge(S("summed"), g + 1)
                pool.wait_ge(S("put"), g * 64 + 80)
                pool.sem_inc(S("pool_pass"), 1)
                pool.tensor_copy(pix[b][:], chunk(c.accI, g, K4)).then_inc(S("pix"), 1)
                pool.wait_ge(S("pix"), g + 1)
                pool.sem_inc(S("pool_pass"), 1)
                for k in range(K4):
                    pool.indirect_dma_start(out=c.NS, out_offset=bass.IndirectOffsetOnAxis(ap=pix[b][:, k:k + 1], axis=0),
                                            in_=rows[b][:, k, :], in_offset=None, bounds_check=d.NP + MAC - 1,
                                            oob_is_err=True, compute_op=ALU.add).then_inc(S("put"), 16)
            for k in range(K4 + 1):
                pool.dma_start(scrap[:, k:k + 1], c.ident[:, 0:1]).then_inc(S("put"), 16)
            for g in range(min(2, d.EM)):
                gathers(g, g)
            if d.EM // 2 > 1:
                with pool.Fori(0, d.EM // 2 - 1) as i:
                    for b in range(2):
                        gathers(i * 2 + b + 2, b)
                        adds(i * 2 + b, b)
            for g in range(max(d.EM // 2 - 1, 0) * 2, d.EM):
                if g + 2 < d.EM:
                    gathers(g + 2, g % 2)
                adds(g, g % 2)
            pool.wait_ge(S("put"), d.EM * 64 + 80)

        @block.sync
        def _(sp):
            def body(m, pars):
                for b in pars:
                    g = m + b
                    sp.wait_ge(S("same"), g + 1)
                    sp.sem_inc(S("sp_pass"), 1)
                    sp.dma_start(sbc[b][:], chunk(c.srcRow.rearrange("(a e) -> a e", a=1), g, MAC).broadcast_to([P, MAC])).then_inc(S(f"s_in{b}"), 16)
            pairs(sp, d.EM, singly(body))

        @block.vector
        def _(v):
            v.sem_inc(S("same"), 2)

            def body(m, pars):
                for b in pars:
                    g = m + b
                    v.wait_ge(S(f"s_in{b}"), (g - b) * 8 + 16)
                    v.wait_ge(S("summing"), g + 1)
                    for k in range(K4):
                        last = v.tensor_scalar(same[b][:, k, :], sbc[b][:], c.srcF[:, bass.ds(g * 4 + k, 1)], None, ALU.is_equal)
                    last.then_inc(S("same"), 1)
                for b in pars:
                    v.wait_ge(S(f"slot{b}"), m * 32 + 64)
                ln.vector(v, [(m + b, b) for b in pars], x)
            pairs(v, d.EM, singly(body))

        @block.scalar
        def _(act):
            act.sem_inc(S("r"), 2)

            def body(m, pars):
                for b in pars:
                    ln.root(act, b, m + b)
                for b in pars:
                    act.wait_ge(S("summing"), m + b + 1)
                    ln.apply(act, b, m + b, r[b], x[b], S("r"))
                for b in pars:
                    g = m + b
                    act.wait_ge(S("summing"), g + 3)
                    act.wait_ge(S("put"), g * 64 + 16)
                    act.activation(rows[b][:], ps[b][:], ACT.Copy).then_inc(S("summed"), 1)
            pairs(act, d.EM, singly(body))

        @block.tensor
        def _(pe):
            pe.sem_inc(S("summing"), 2)

            def body(m, pars):
                for b in pars:
                    g = m + b
                    pe.wait_ge(S("r"), g + 3)
                    pe.wait_ge(S("same"), g + 3)
                    pe.wait_ge(S("ps_free"), g + 1)
                    for k in range(K4):
                        for e in range(K4):
                            last = pe.matmul(ps[b][:, k, :], same[b][:, e, k * P:(k + 1) * P], r[b][:, e, :],
                                             start=(e == 0), stop=(e == K4 - 1))
                    last.then_inc(S("summing"), 1)
                for b in pars:
                    g = m + b
                    pe.wait_ge(S("summed"), g + 1)
                    pe.sem_inc(S("ps_free"), 1)
            pe.sem_inc(S("ps_free"), 2)
            pairs(pe, d.EM, singly(body))
    S.end()


def nodes_sage(nc, c, out):
    d, S = c.d, Signals(nc, "sagen")
    N, NM = d.N, d.NM
    with ExitStack() as st:
        def each(name, shape, dt=F32):
            return [st.enter_context(nc.sbuf_tensor(f"{S.tag}_{name}{i}", shape, dt)) for i in range(FLY)]
        xin, ns, r, rT, nsT = each("xin", [P, K4, D]), each("ns", [P, K4, D]), each("r", [P, K4, D]), each("rT", [P, MAC]), each("nsT", [P, MAC])
        nb, x3, x3k, fin = (each(n, [P, K4, D]) for n in ("nb", "x3", "x3_kept", "fin"))
        r3, r3T = r, rT
        hT = [each(f"hT{o}_", [P, MAC]) for o in range(2)]
        hrow = [each(f"h{s}row", [P, K4, 2 * D]) for s in range(2)]
        ln0, ln1 = Norm(st, nc, S, "ln0", FLY), Norm(st, nc, S, "ln1", FLY)
        psA = [st.enter_context(nc.psum_tensor(f"{S.tag}_psA{i}", [P, MAC], F32)) for i in range(FLY)]
        psB = [st.enter_context(nc.psum_tensor(f"{S.tag}_psB{i}", [P, MAC], F32)) for i in range(FLY)]
        ps = (psA, psB)
        block = st.enter_context(nc.Block())

        def k4(t):
            return t[:].rearrange("p (k f) -> p k f", k=K4)

        def row(t):
            return t[:].unsqueeze(1).broadcast_to([P, K4, D])

        first, second = node_group(NM, 0), node_group(NM, 1)

        @block.gpsimd
        def _(pool):
            def keep(gb, follows):
                for g, b in gb:
                    pool.wait_ge(S("x3"), g + 1)
                    if follows:
                        pool.wait_ge(S("fin"), g + 1 - FLY)
                    pool.sem_inc(S("pool_pass"), 1)
                    pool.tensor_copy(x3k[b][:], x3[b][:]).then_inc(S("x3_kept"), 1)
            pool.sem_inc(S("x3_kept"), FLY)
            keep(first, False)
            node_groups_two_ahead(pool, NM, lambda gb, ahead, after: keep(ahead, True))

        @block.sync
        def _(sp):
            def load(gb, follows):
                for g, b in gb:
                    if follows:
                        sp.wait_ge(S("nsT"), g + 1 - FLY)
                        sp.sem_inc(S("sp_pass"), 1)
                    sp.dma_start(ns[b][:], node_rows(c.NS[0:N, :], g, N)).then_inc(S(f"ns_load{b}"), 16)
                for g, b in gb:
                    if follows:
                        sp.wait_ge(S("xa"), g + 1 - FLY)
                        sp.sem_inc(S("sp_pass"), 1)
                    sp.dma_start(xin[b][:], node_rows(c.X2, g, N)).then_inc(S(f"x_load{b}"), 16)

            def table(gb, n, ready, buf, t, stores, name):
                for g, b in gb:
                    sp.wait_ge(S(ready), g + 1)
                    store_rows(sp, S, NM, n, node_rows(t, g, N), g, b, buf[b][:], stores, name)

            def landed(gb, name, stores, free):
                for g, b in gb:
                    sp.wait_ge(S(f"{name}{b}"), (g - b) * (16 * stores // FLY) + 16 * stores)
                    sp.sem_inc(S(free), 1)

            def front_out(gb):
                table(gb, 1, "x3", x3, c.X3, 2, "front_st")
                table(gb, 2, "r3", r3, c.R3, 2, "front_st")

            def body(gb, ahead, after):
                table(gb, 1, "h0row", hrow[0], c.H[0][0:N, :], 3, "st")
                load(after, True)
                front_out(ahead)
                table(gb, 2, "h1row", hrow[1], c.H[1][0:N, :], 3, "st")
                landed(ahead, "front_st", 2, "front_free")
                table(gb, 3, "fin", fin, out, 3, "st")
                landed(gb, "st", 3, "rows_free")
            load(first, False)
            load(second, True)
            front_out(first)
            landed(first, "front_st", 2, "front_free")
            node_groups_two_ahead(sp, NM, body)

        @block.vector
        def _(v):
            v.sem_inc(S("fa"), FLY)

            def ln0_moments(gb):
                for g, b in gb:
                    v.wait_ge(S(f"x_load{b}"), (g - b) * (16 // FLY) + 16)
                for g, b in gb:
                    ln0.stats(v, b, g, xin[b])
                for step in (ln0.moments, ln0.variance):
                    for g, b in gb:
                        step(v, b, g)

            def ln0_scales(gb):
                for step in (ln0.recip, ln0.shift):
                    for g, b in gb:
                        step(v, b, g)

            def front(gb):
                for g, b in gb:
                    v.wait_ge(S("nbr"), g + 1)
                    v.tensor_tensor(nb[b][:], k4(psA[b]), row(c.b2nrow), ALU.add).then_inc(S("nb"), 1)
                for g, b in gb:
                    v.wait_ge(S("self"), g + 1)
                    v.wait_ge(S("x3_kept"), g + 1)
                    v.tensor_tensor(x3[b][:], k4(psB[b]), xin[b][:], ALU.add).then_inc(S("xa"), 1)
                for g, b in gb:
                    v.wait_ge(S("th"), g + 1)
                    v.wait_ge(S("xa"), g + 1)
                    v.tensor_tensor(x3[b][:], x3[b][:], nb[b][:], ALU.add).then_inc(S("x3"), 1)
                if gb:
                    v.wait_ge(S("x3"), gb[-1][0] + 1)
                    ln1.vector(v, gb, x3)

            def hidden_rows(gb, s):
                for g, b in gb:
                    v.wait_ge(S(f"back{s}"), g + 1)
                    if s == 0:
                        v.wait_ge(S("rows_free"), g + 1)
                    v.tensor_copy(hrow[s][b][:, :, 0:D], k4(psA[b]))
                    v.tensor_copy(hrow[s][b][:, :, D:2 * D], k4(psB[b])).then_inc(S(f"h{s}row"), 1)

            def body(gb, ahead, after):
                hidden_rows(gb, 0)
                front(ahead)
                ln0_moments(after)
                hidden_rows(gb, 1)
                ln0_scales(after)
                for g, b in gb:
                    v.wait_ge(S("last"), g + 1)
                    v.tensor_tensor(fin[b][:], k4(psA[b]), row(c.b3row), ALU.add).then_inc(S("fa"), 1)
                for g, b in gb:
                    v.wait_ge(S("fa"), g + 1 + FLY)
                    v.wait_ge(S("x3_kept"), g + 1 + FLY)
                    v.scalar_tensor_tensor(out=fin[b][:], in0=fin[b][:], scalar=0.0, in1=x3k[b][:],
                                           op0=ALU.max, op1=ALU.add).then_inc(S("fin"), 1)
            ln0_moments(first)
            ln0_scales(first)
            front(first)
            ln0_moments(second)
            ln0_scales(second)
            node_groups_two_ahead(v, NM, body)

        @block.scalar
        def _(act):
            act.sem_inc(S("rows_free"), FLY)
            act.sem_inc(S("front_free"), FLY)

            def copies(gb, out_, src, ready, done):
                for g, b in gb:
                    act.wait_ge(S(ready), g + 1)
                    act.activation(out_[b][:], src[b][:], ACT.Copy).then_inc(S(done), 1)

            def roots(gb, ln):
                for g, b in gb:
                    ln.root(act, b, g)

            def norm0(g, b):
                act.wait_ge(S("front_free"), g + 1)
                ln0.apply(act, b, g, r[b], xin[b], S("r"))

            def turned(gb):
                copies(gb, nsT, psA, "ns_turned", "nsT")
                copies(gb, rT, psB, "rTp", "rT")
                for g, b in gb:
                    act.wait_ge(S("nb"), g + 1)
                    act.activation(nb[b][:], nb[b][:], ACT.Tanh).then_inc(S("th"), 1)

            def norm1(gb):
                for g, b in gb:
                    ln1.apply(act, b, g, r3[b], x3[b], S("r3"))
                copies(gb, r3T, psB, "r3Tp", "r3T")

            def hidden(g, b, s):
                act.wait_ge(S(f"hid{s}"), g + 1)
                for o in range(2):
                    last = act.activation(hT[o][b][:], ps[o][b][:], ACT.Relu, bias=c.bcol[s][:, o:o + 1])
                last.then_inc(S(f"relu{s}"), 1)

            def body(gb, ahead, after):
                for g, b in gb:
                    hidden(g, b, 0)
                    if b < len(ahead):
                        norm0(ahead[b][0], b)
                turned(ahead)
                for g, b in gb[:2]:
                    hidden(g, b, 1)
                roots(ahead, ln1)
                for g, b in gb[2:]:
                    hidden(g, b, 1)
                roots(after, ln0)
                norm1(ahead)
            roots(first, ln0)
            for g, b in first:
                norm0(g, b)
            turned(first)
            roots(first, ln1)
            roots(second, ln0)
            norm1(first)
            node_groups_two_ahead(act, NM, body)

        @block.tensor
        def _(pe):
            def front(gb, follows):
                for g, b in gb:
                    pe.wait_ge(S(f"ns_load{b}"), (g - b) * (16 // FLY) + 16)
                    pe.wait_ge(S("r"), g + 1)
                    if follows:
                        pe.wait_ge(S("h0row"), g + 1 - FLY)
                    turn(pe, psA[b], ns[b], c.ident[:], S("ns_turned"))
                    turn(pe, psB[b], r[b], c.ident[:], S("rTp"))
                for g, b in gb:
                    pe.wait_ge(S("nsT"), g + 1)
                    rows_of(pe, k4(psA[b]), nsT[b], c.W2n[:], S("nbr"))
                    pe.wait_ge(S("rT"), g + 1)
                    rows_of(pe, k4(psB[b]), rT[b], c.W2s[:], S("self"))

            def norm_turn(gb, follows):
                for g, b in gb:
                    pe.wait_ge(S("r3"), g + 1)
                    if follows:
                        pe.wait_ge(S("h1row"), g + 1 - FLY)
                    turn(pe, psB[b], r3[b], c.ident[:], S("r3Tp"))

            def turned_back(gb, s):
                for g, b in gb:
                    pe.wait_ge(S(f"relu{s}"), g + 1)
                    for o in range(2):
                        for k in range(K4):
                            last = pe.transpose(k4(ps[o][b])[:, k, :], hT[o][b][:, k * P:(k + 1) * P], c.ident[:])
                    last.then_inc(S(f"back{s}"), 1)

            def body(gb, ahead, after):
                for g, b in gb:
                    pe.wait_ge(S("r3T"), g + 1)
                    pe.wait_ge(S("fa"), g + 1)
                    for o in range(2):
                        last = pe.matmul(ps[o][b][:], c.Ws[0][:, 0, o * P:(o + 1) * P], r3T[b][:], start=True, stop=True)
                    last.then_inc(S("hid0"), 1)
                turned_back(gb, 0)
                front(ahead, True)
                for g, b in gb:
                    pe.wait_ge(S("h0row"), g + 1)
                    if b < len(ahead):
                        pe.wait_ge(S("xa"), ahead[b][0] + 1)
                    for o in range(2):
                        for f in range(2):
                            last = pe.matmul(ps[o][b][:], c.Ws[1][:, f, o * P:(o + 1) * P], hT[f][b][:], start=(f == 0), stop=(f == 1))
                    last.then_inc(S("hid1"), 1)
                turned_back(gb, 1)
                for g, b in gb:
                    pe.wait_ge(S("h1row"), g + 1)
                    for k in range(K4):
                        for f in range(2):
                            last = pe.matmul(k4(psA[b])[:, k, :], hT[f][b][:, k * P:(k + 1) * P], c.Ws[2][:, f, :],
                                             start=(f == 0), stop=(f == 1))
                    last.then_inc(S("last"), 1)
                norm_turn(ahead, True)
            front(first, False)
            norm_turn(first, False)
            node_groups_two_ahead(pe, NM, body)
    S.end()


def sage_edges(nc, c, s, out):
    d, S = c.d, Signals(nc, f"sage{s}")
    FI, FO = (1, 2, 2)[s], (2, 2, 1)[s]
    table = (c.R3, c.H[0], c.H[1])[s]
    with ExitStack() as st:
        def two(name, shape, dt=F32):
            return [st.enter_context(nc.sbuf_tensor(f"{S.tag}_{name}{i}", shape, dt)) for i in range(2)]

        def bank(name):
            return [st.enter_context(nc.psum_tensor(f"{S.tag}_{name}{i}", [P, MAC], F32)) for i in range(2)]
        ring, gw = two("ring", [P, K4, FI * D]), two("gw", [P, K4, FI * D])
        gix, six = two("gix", [P, K4], I32), two("six", [P, K4], I32)
        dix = two("dix", [P, K4], I32)
        srcI = st.enter_context(nc.sbuf_tensor(f"{S.tag}_srcI", [P, d.ET], I32))
        same, carried, s32 = two("same", [P, MAC], U8), two("carried", [P, MAC], U8), two("s32", [P, MAC])
        agg = [two(f"agg{f}_", [P, MAC]) for f in range(FI)]
        own = [two(f"own{f}_", [P, MAC]) for f in range(FI)]
        hd, xd = two("hd", [P, K4, D]), two("xd", [P, K4, D])
        new = [two(f"new{o}_", [P, MAC]) for o in range(FO)]
        rows = two("rows", [P, K4, FO * D])
        scrap = two("scrap", [P, 1])
        psA, psO = [bank("psA0"), bank("psA1")], [bank("psO0"), bank("psO1")]
        block = st.enter_context(nc.Block())
        made = "rows" if s < 2 else "result"
        lead = tuple(range(min(2, d.EM)))
        second = {0: (hd, c.R3, "own_turned"), 1: (xd, c.X3, "xd_free")}.get(s)
        stores = [f"new_out{o}_" for o in range(FO)] + ["rows_out"] if s < 2 else []

        def k4(t):
            return t[:].rearrange("p (k f) -> p k f", k=K4)

        @block.gpsimd
        def _(pool):
            def gathers(m, pars):
                for b in pars:
                    g = m + b
                    pool.wait_ge(S("gw"), g + 1)
                    pool.sem_inc(S("pool_pass"), 1)
                    pool.tensor_copy(gix[b][:], chunk(srcI if s == 0 else c.idxS, g, K4)).then_inc(S("gix"), 1)
                    pool.wait_ge(S("gix"), g + 1)
                    pool.sem_inc(S("pool_pass"), 1)
                    for k in range(K4):
                        pool.indirect_dma_start(out=ring[b][:, k, :], out_offset=None, in_=table,
                                                in_offset=bass.IndirectOffsetOnAxis(ap=gix[b][:, k:k + 1], axis=0)
                                                ).then_inc(S(f"slot{b}"), 16)
                    if second:
                        rows_d, table_d, free = second
                        pool.wait_ge(S(free), g + 1)
                        pool.sem_inc(S("pool_pass"), 1)
                        pool.tensor_copy(dix[b][:], chunk(c.idxD, g, K4)).then_inc(S("dix"), 1)
                        pool.wait_ge(S("dix"), g + 1)
                        pool.sem_inc(S("pool_pass"), 1)
                        for k in range(K4):
                            pool.indirect_dma_start(out=rows_d[b][:, k, :], out_offset=None, in_=table_d,
                                                    in_offset=bass.IndirectOffsetOnAxis(ap=dix[b][:, k:k + 1], axis=0)
                                                    ).then_inc(S(f"slot_dst{b}"), 16)

            def scatters(m, pars):
                for b in pars if s == 2 else ():
                    g = m + b
                    pool.wait_ge(S("result"), g + 3)
                    pool.wait_ge(S(f"put{b}"), (g - b) * 32 + 16)
                    pool.sem_inc(S("pool_pass"), 1)
                    pool.tensor_copy(six[b][:], chunk(c.canonI, g, K4)).then_inc(S("six"), 1)
                    pool.wait_ge(S("six"), g + 1)
                    pool.sem_inc(S("pool_pass"), 1)
                    for k in range(K4):
                        pool.indirect_dma_start(out=out, out_offset=bass.IndirectOffsetOnAxis(ap=six[b][:, k:k + 1], axis=0),
                                                in_=rows[b][:, k, :], in_offset=None, bounds_check=d.N - 1,
                                                oob_is_err=False).then_inc(S(f"put{b}"), 16)
            if s == 2:
                for b in range(2):
                    pool.dma_start(scrap[b][:], c.ident[:, 0:1]).then_inc(S(f"put{b}"), 16)
            if s == 0:
                pool.wait_ge(S("src_idx"), 1)
            def body(m, pars, ahead):
                scatters(m, pars)
                gathers(m + 4, ahead)
            even = d.EM // 2 * 2
            gathers(0, lead)
            gathers(2, tuple(range(min(2, d.EM - 2))))
            if even > 4:
                with pool.Fori(0, even // 2 - 2) as i:
                    body(i * 2, (0, 1), (0, 1))
            for m in range(max(even - 4, 0), d.EM, 2):
                body(m, tuple(range(min(2, d.EM - m))), tuple(range(max(min(2, d.EM - m - 4), 0))))
            if s == 2:
                for b in range(2):
                    pool.wait_ge(S(f"put{b}"), 16 + 64 * ((d.EM + 1 - b) // 2))

        @block.sync
        def _(sp):
            def fetch(what, buf, src, free, g, b):
                sp.wait_ge(S(free), g + 1)
                sp.sem_inc(S("sp_pass"), 1)
                sp.dma_start(buf, src).then_inc(S(f"{what}_in{b}"), 16)

            def early(m, pars):
                for b in pars:
                    fetch("same", same[b][:], chunk(c.SF, (m + b) * 2, MAC), "s32", m + b, b)

            def late(m, pars):
                for b in pars:
                    fetch("carried", carried[b][:], chunk(c.SF, (m + b) * 2 + 1, MAC), "agg3", m + b, b)

            def body(m, pars, ahead):
                early(m + 2, ahead)
                for b in pars:
                    g = m + b
                    if s:
                        for f in range(2):
                            fetch(f"own{f}_", own[f][b][:], chunk(c.HT[s - 1][f * P:(f + 1) * P, :], g, MAC), "dense", g, b)
                    if s == 2:
                        fetch("xd", xd[b][:], edge_rows(c.XD, g), "result", g, b)
                late(m + 2, ahead)
                if s == 1:
                    for b in pars:
                        g = m + b
                        sp.wait_ge(S(f"slot_dst{b}"), (g - b) * 32 + 64)
                        sp.sem_inc(S("sp_pass"), 1)
                        sp.dma_start(edge_rows(c.XD, g), xd[b][:]).then_inc(S(f"xd_out{b}"), 16)
                    for b in pars:
                        sp.wait_ge(S(f"xd_out{b}"), m * 8 + 16)
                        sp.sem_inc(S("xd_free"), 1)
            if s == 1:
                sp.sem_inc(S("xd_free"), 2)
            early(0, lead)
            late(0, lead)
            pairs_ahead(sp, d.EM, body)

        def loaded(eng, what, g, b):
            eng.wait_ge(S(f"{what}_in{b}"), (g - b) * 8 + 16)

        @block.vector
        def _(v):
            v.sem_inc(S("gw"), 2)
            v.sem_inc(S("agg3"), 1)
            if s == 0:
                v.tensor_scalar(srcI[:], c.srcF[:], 0.0, None, ALU.max).then_inc(S("src_idx"), 1)
            for f in range(FI):
                last = v.memset(agg[f][1][:, MAC - 1:MAC], 0.0)
            last.then_inc(S("agg3"), 1)
            v.sem_inc(S(made), 2)

            def weigh(m, pars):
                for b in pars:
                    g = m + b
                    v.wait_ge(S(f"slot{b}"), (g - b) * 32 + 64)
                    v.wait_ge(S("sums"), g + 1)
                    v.tensor_tensor(gw[b][:], ring[b][:], chunk(c.invdeg, g, K4).unsqueeze(2).broadcast_to([P, K4, FI * D]),
                                    ALU.mult).then_inc(S("gw"), 1)

            def carry(m, pars):
                for b in pars:
                    g = m + b
                    loaded(v, "carried", g, b)
                    v.wait_ge(S("sums"), g + 3)
                    for k in range(K4):
                        v.wait_ge(S(f"agg{(k - 1) % 4}"), g + (1 if k else 2))
                        for f in range(FI):
                            before = agg[f][b][:, k * P - 1:k * P] if k else agg[f][1 - b][:, MAC - 1:MAC]
                            last = v.scalar_tensor_tensor(out=agg[f][b][:, k * P:(k + 1) * P], in0=carried[b][:, k * P:(k + 1) * P],
                                                          scalar=before, in1=psA[f][b][:, k * P:(k + 1) * P], op0=ALU.mult, op1=ALU.add)
                        last.then_inc(S(f"agg{k}"), 1)

            def result(m, pars):
                for b in pars:
                    g = m + b
                    v.wait_ge(S("back"), g + 1)
                    if s < 2:
                        v.wait_ge(S(f"rows_out{b}"), (g - b) * 8 + 16)
                        for o in range(2):
                            last = v.tensor_copy(rows[b][:, :, o * D:(o + 1) * D], k4(psO[o][b]))
                        last.then_inc(S("rows"), 1)
                    else:
                        loaded(v, "xd", g, b)
                        v.wait_ge(S(f"put{b}"), (g - b) * 32 + 16)
                        v.tensor_tensor(rows[b][:], k4(psO[0][b]), xd[b][:], ALU.add).then_inc(S("result"), 1)

            def body(m, pars, ahead):
                if s == 2:
                    result(m, pars)
                weigh(m + 2, ahead)
                carry(m + 2, ahead)
                if s < 2:
                    result(m, pars)
            weigh(0, lead)
            carry(0, lead)
            pairs_ahead(v, d.EM, body)

        @block.scalar
        def _(act):
            act.sem_inc(S("s32"), 2)
            for b in range(2):
                for name in stores:
                    act.dma_start(scrap[b][:], c.ident[:, 0:1]).then_inc(S(f"{name}{b}"), 16)
                    act.wait_ge(S(f"{name}{b}"), 16)

            def widen(m, pars):
                for b in pars:
                    g = m + b
                    loaded(act, "same", g, b)
                    act.wait_ge(S("sums"), g + 1)
                    act.activation(s32[b][:], same[b][:], ACT.Copy).then_inc(S("s32"), 1)

            def own_rows(m, pars):
                for b in pars if s == 0 else ():
                    act.wait_ge(S("own_turned"), m + b + 3)
                    act.activation(own[0][b][:], psA[1][b][:], ACT.Copy).then_inc(S("own"), 1)

            def body(m, pars, ahead):
                widen(m + 2, ahead)
                for b in pars:
                    g = m + b
                    act.wait_ge(S("dense"), g + 3)
                    for o in range(FO):
                        if s < 2:
                            act.wait_ge(S(f"new_out{o}_{b}"), (g - b) * 8 + 16)
                        act.activation(new[o][b][:], psO[o][b][:], ACT.Relu, bias=c.bcol[s][:, o:o + 1]).then_inc(S("new"), 1)
                own_rows(m + 2, ahead)
                if s < 2:
                    for b in pars:
                        g = m + b
                        act.wait_ge(S("new"), (g + 1) * FO)
                        for o in range(2):
                            act.dma_start(chunk(c.HT[s][o * P:(o + 1) * P, :], g, MAC), new[o][b][:]).then_inc(S(f"new_out{o}_{b}"), 16)
                    for b in pars:
                        g = m + b
                        act.wait_ge(S("rows"), g + 3)
                        act.dma_start(edge_rows(c.H[s][d.N:, :], g), rows[b][:]).then_inc(S(f"rows_out{b}"), 16)
            widen(0, lead)
            own_rows(0, lead)
            pairs_ahead(act, d.EM, body)
            for b in range(2):
                for name in stores:
                    act.wait_ge(S(f"{name}{b}"), 16 + 16 * ((d.EM + 1 - b) // 2))

        @block.tensor
        def _(pe):
            pe.sem_inc(S("sums"), 2)
            pe.sem_inc(S("dense"), 2)
            if s == 0:
                pe.sem_inc(S("own_turned"), 2)

            def sums(m, pars):
                for b in pars:
                    g = m + b
                    pe.wait_ge(S("gw"), g + 3)
                    pe.wait_ge(S("s32"), g + 3)
                    pe.wait_ge(S("agg3"), g + 1)
                    for f in range(FI):
                        for k in range(K4):
                            col = slice(k * P, (k + 1) * P)
                            last = pe.matmul(psA[f][b][:, col], gw[b][:, k, f * D:(f + 1) * D], s32[b][:, col], start=True, stop=True)
                    last.then_inc(S("sums"), 1)
                    if s == 0:
                        pe.wait_ge(S(f"slot_dst{b}"), (g - b) * 32 + 64)
                        turn(pe, psA[1][b], hd[b], c.ident[:], S("own_turned"))

            def turned_back(m, pars):
                for b in pars:
                    g = m + b
                    pe.wait_ge(S("new"), (g + 1) * FO)
                    for o in range(FO):
                        for k in range(K4):
                            last = pe.transpose(k4(psO[o][b])[:, k, :], new[o][b][:, k * P:(k + 1) * P], c.ident[:])
                    last.then_inc(S("back"), 1)

            def body(m, pars, ahead):
                for b in pars:
                    g = m + b
                    if s == 0:
                        pe.wait_ge(S("own"), g + 1)
                    else:
                        loaded(pe, "own0_", g, b)
                        loaded(pe, "own1_", g, b)
                    pe.wait_ge(S(made), g + 1)
                    pe.wait_ge(S("agg3"), g + 3)
                    for o in range(FO):
                        for f in range(FI):
                            col = slice(o * P, (o + 1) * P)
                            pe.matmul(psO[o][b][:], c.Ws[s][:, f, col], own[f][b][:], start=(f == 0), stop=False)
                            last = pe.matmul(psO[o][b][:], c.Wn[s][:, f, col], agg[f][b][:], start=False, stop=(f == FI - 1))
                    last.then_inc(S("dense"), 1)
                if s == 2:
                    turned_back(m, pars)
                sums(m + 2, ahead)
                if s < 2:
                    turned_back(m, pars)
            sums(0, lead)
            pairs_ahead(pe, d.EM, body)
    S.end()


class Context:
    pass


def graph_kernel(nc, w, out):
    c = Context()
    c.d = d = Dims(w["x"].shape[0], w["src"].shape[0])
    rows = d.N + d.EP
    c.TW = [D + 2] * 5 + [D + 8]
    with ExitStack() as st:
        def sb(name, shape, dt=F32):
            return st.enter_context(nc.sbuf_tensor(name, shape, dt))

        def dram(name, shape, dt=F32):
            return nc.dram_tensor(name, shape, dt).ap()
        c.HP = [dram(f"hp_table{l}", (rows, c.TW[l])) for l in range(6)]
        c.X2 = dram("x2_table", (d.N, D))
        c.X3, c.R3 = dram("x3_table", (d.N, D)), dram("r3_table", (d.N, D))
        c.H = [dram(f"hidden_table{i}", (rows, 2 * D)) for i in range(2)]
        c.NS = dram("sum_by_src", (d.NP + MAC, D))
        c.POS = dram("slot_table", (d.NP, 1), I32)
        c.dstRow, c.srcRow = dram("dst_row", (d.EP,)), dram("src_row", (d.EP,))
        c.SF = dram("same_dst_tiles", (P, d.EM * 2 * MAC), U8)
        c.XD = dram("x_of_dst", (d.EP, D))
        c.X0T = dram("x0_of_dst_T", (P, d.EP))
        c.HT = [dram("h1_of_dst_T", (2 * P, d.EP)), dram("h2_of_dst_T", (2 * P, d.EP))]

        c.ident, c.zero = sb("ident", [P, P]), sb("zero", [P, D])
        c.contF, c.contB, c.negF = sb("contF", [P, 4, 256]), sb("contB", [P, 4, 256]), sb("negF", [P, 4, 256])
        c.runF, c.runB, c.negRunF = sb("runF", [P, 256]), sb("runB", [P, 256]), sb("negRunF", [P, 256])
        c.last, c.negLast = sb("last", [P, 256]), sb("negLast", [P, 256])
        c.wholeF, c.wholeB, c.negWholeF = sb("wholeF", [4, d.QP]), sb("wholeB", [4, d.QP]), sb("negWholeF", [4, d.QP])
        c.EL, c.loopEL = sb("EL", [P, 5, 256]), sb("loopEL", [P, 5, 256])
        c.dstF, c.srcF, c.invdeg = sb("dstF", [P, d.ET]), sb("srcF", [P, d.ET]), sb("invdeg", [P, d.ET])
        c.canonI, c.idxD, c.idxS, c.accI, c.slotI = (sb(n, [P, d.ET], I32) for n in ("canonI", "idxD", "idxS", "accI", "slotI"))
        c.SS, c.SD, c.SL, c.AL, c.AF = (sb(n, [P, d.ET * 4]) for n in ("score_src", "score_dst", "score_self", "alpha", "alpha_self"))
        c.W0, c.W5 = sb("W0", [P, 5, D + 2]), sb("W5", [P, D + 8])
        c.M = sb("M", [P, 3, D])
        c.b0row, c.b4row, c.b5row, c.blin = sb("b0row", [P, D]), sb("b4row", [P, D]), sb("b5row", [P, D]), sb("blin", [P, D + 8])
        c.b0col, c.bm = sb("b0col", [P, 1]), sb("bm", [P, 3])
        c.W2n, c.W2s, c.b2nrow = sb("W2n", [P, D]), sb("W2s", [P, D]), sb("b2nrow", [P, D])
        c.Ws = [sb("Ws0", [P, 1, 256]), sb("Ws1", [P, 2, 256]), sb("Ws2", [P, 2, D])]
        c.Wn = [sb("Wn0", [P, 1, 256]), sb("Wn1", [P, 2, 256]), sb("Wn2", [P, 2, D])]
        c.bcol = [sb("bcol0", [P, 2]), sb("bcol1", [P, 2]), sb("bcol2", [P, 1])]
        c.b3row = sb("b3row", [P, D])

        Signals.kept = [st.enter_context(nc.semaphore(f"soft_dma{i}")) for i in range(12)]
        with nc.sbuf_tensor("upper", [P, MAC], F32) as c.upper:
            prepare_edges(nc, c, w["src"], w["dst"], w["edge_attr_16"])
            prepare_tiles(nc, c)
        with nc.sbuf_tensor("alpha_M", [P, 3, D], F32) as c.AM, nc.sbuf_tensor("W_M", [P, 3, D], F32) as c.WM:
            prepare_weights(nc, c, w)
            nodes_gat(nc, c, w["x"])
        edge_degrees(nc, c)
        rows_of_dst(nc, c, "hp0d", c.HP[0][0:d.N, :], c.HP[0][d.N:, :], scores=True)
        with nc.sbuf_tensor("source_rows", [P, d.ET * D], F32) as c.G:
            for l in range(6):
                gather_sources(nc, c, l)
                attention(nc, c, l)
                gat_messages(nc, c, l)
        sum_by_source(nc, c)
        nodes_sage(nc, c, out)
        for s in range(3):
            sage_edges(nc, c, s, out)


def kernel(**inputs):
    import numpy as _np
    import concourse.bacc as _bacc
    from concourse import mybir as _mybir
    from concourse.bass_utils import run_bass_kernel_spmd as _run

    nc = _bacc.Bacc("TRN2", target_bir_lowering=False, num_devices=1)
    arrays, w = {}, {}
    for name in inputs:
        a = _np.ascontiguousarray(inputs[name])
        arrays[f"in_{name}_dram"] = a
        w[name] = nc.dram_tensor(f"in_{name}_dram", a.shape, _mybir.dt.from_np(a.dtype), kind="ExternalInput").ap()
    out = nc.dram_tensor("out_dram", w["x"].shape, F32, kind="ExternalOutput").ap()
    graph_kernel(nc, w, out)
    r = _run(nc, [arrays], core_ids=[0])
    return r.results[0]["out_dram"]
```
